# Optimizing a Trainium2 kernel written in Bass

```python
import numpy as np
import jax
import jax.numpy as jnp

def _softmax(x, axis=-1):
    return jax.nn.softmax(x, axis=axis)

def _gelu(x):
    return jax.nn.gelu(x, approximate=True)

def _silu(x):
    return jax.nn.silu(x)

def _sigmoid(x):
    return jax.nn.sigmoid(x)

def _layernorm(x, axis=-1, eps=1e-05):
    m = jnp.mean(x, axis=axis, keepdims=True)
    v = jnp.var(x, axis=axis, keepdims=True)
    return (x - m) / jnp.sqrt(v + eps)

def _scatter_add(tgt, idx, src, axis=0):
    return tgt.at[idx].add(src)

def _segment_sum(src, seg, n):
    return jax.ops.segment_sum(src, seg, n)
kernel_name = 'mk_early_fusion_d1_tok_img1024_r4_b3f18a'

def setup_inputs(seed: int=0):
    np.random.seed(seed)
    _w = jnp.asarray

    def _rec_inputs():
        import jax
        import jax.numpy as jnp
        _rk = jax.random.key(seed)
        x = -0.000356955 + 1 * jax.random.normal(jax.random.fold_in(_rk, 1), (32, 3, 224, 224), jnp.float32)
        txt = 4.19695e-11 + 0.999995 * jax.random.normal(jax.random.fold_in(_rk, 2), (32, 77, 256), jnp.float32)
        return (x, txt)
    x, txt = _rec_inputs()

    def _L0_tok_setup():
        import jax, jax.numpy as jnp
        import numpy as np
        PATCH = 16
        EMBED = 256
        IN_FEATS = PATCH * PATCH * 3
        EPS = 1e-05

        def _layernorm(x, g, b):
            mu = jnp.mean(x, axis=-1, keepdims=True)
            var = jnp.mean(jnp.square(x - mu), axis=-1, keepdims=True)
            return (x - mu) * jax.lax.rsqrt(var + EPS) * g + b
        key = jax.random.key(seed)
        ks = jax.random.split(key, 4)
        x = jax.random.normal(ks[0], (128, 3, 224, 224), dtype=jnp.float32)
        W = jax.random.normal(ks[1], (IN_FEATS, EMBED), dtype=jnp.float32) / np.sqrt(IN_FEATS)
        bias = jax.random.normal(ks[2], (EMBED,), dtype=jnp.float32) * 0.01
        ln1_g = jnp.ones((IN_FEATS,), dtype=jnp.float32)
        ln1_b = jnp.zeros((IN_FEATS,), dtype=jnp.float32)
        ln2_g = jnp.ones((EMBED,), dtype=jnp.float32)
        ln2_b = jnp.zeros((EMBED,), dtype=jnp.float32)
        return {'x': x, 'W': W, 'bias': bias, 'ln1_g': ln1_g, 'ln1_b': ln1_b, 'ln2_g': ln2_g, 'ln2_b': ln2_b}
    _L0_tok_all = _L0_tok_setup()
    _L0_tok_in = {k: v for k, v in _L0_tok_all.items() if k in ('W', 'bias', 'ln1_g', 'ln1_b', 'ln2_g', 'ln2_b')}
    del _L0_tok_all

    def _L0_attn_setup():
        import jax, jax.numpy as jnp
        import numpy as np
        BATCH, SEQ, D_MODEL, D_STATE, TIMESCALE = (4, 512, 256, 64, 2)
        EPS = 1e-06

        def _reference_tuple_inner(x, w_in, b_in, A, Bm, Cm, Dv, w_out, b_out, g_norm):
            B, L, D = x.shape
            S = A.shape[1]
            ts = TIMESCALE
            x_sub = x[:, ::ts] if ts > 1 else x
            x_sub = x_sub * jax.lax.rsqrt(jnp.mean(jnp.square(x_sub), axis=-1, keepdims=True) + EPS) * g_norm
            xz = jnp.einsum('bld,ed->ble', x_sub, w_in) + b_in
            x_proj, gate = jnp.split(xz, 2, axis=-1)
            c_sum = Cm.sum(axis=0)
            h0 = jnp.zeros((B, D, S), dtype=x.dtype)

            def step(h, xt):
                h = jnp.tanh(h * A + xt[:, :, None] * Bm)
                y = h @ c_sum + Dv * xt
                return (h, y)
            h_last, ys = jax.lax.scan(step, h0, jnp.swapaxes(x_proj, 0, 1))
            out = jnp.swapaxes(ys, 0, 1)
            out = out * jax.nn.silu(gate)
            out = jnp.einsum('bld,ed->ble', out, w_out) + b_out
            if ts > 1:
                out = jnp.repeat(out, ts, axis=1)[:, :L]
            return (out, h_last)
        key = jax.random.key(seed)
        ks = jax.random.split(key, 6)
        D, S = (D_MODEL, D_STATE)
        return {'x': jax.random.normal(ks[0], (BATCH, SEQ, D), dtype=jnp.float32), 'w_in': jax.random.normal(ks[1], (2 * D, D), dtype=jnp.float32) * 0.02, 'b_in': jnp.zeros((2 * D,), dtype=jnp.float32), 'A': jax.random.normal(ks[2], (D, S), dtype=jnp.float32) * 0.01, 'Bm': jax.random.normal(ks[3], (D, S), dtype=jnp.float32) * 0.01, 'Cm': jax.random.normal(ks[4], (D, S), dtype=jnp.float32) * 0.01, 'Dv': jnp.ones((D,), dtype=jnp.float32), 'w_out': jax.random.normal(ks[5], (D, D), dtype=jnp.float32) * 0.02, 'b_out': jnp.zeros((D,), dtype=jnp.float32), 'g_norm': jnp.ones((D,), dtype=jnp.float32)}
    _L0_attn_all = _L0_attn_setup()
    _L0_attn_in = {k: v for k, v in _L0_attn_all.items() if k in ('w_in', 'b_in', 'A', 'Bm', 'Cm', 'Dv', 'w_out', 'b_out', 'g_norm')}
    del _L0_attn_all

    def _L0_ffn_setup():
        import jax, jax.numpy as jnp
        import numpy as np
        DIM = 256
        HIDDEN = 768
        SCALE = 1.0 / 127.0

        def _dequant(w_int, dtype):
            return w_int.astype(dtype) * jnp.asarray(SCALE, dtype)
        key = jax.random.key(seed)
        k_x, k_g, k_u, k_d = jax.random.split(key, 4)
        x = jax.random.normal(k_x, (4, 512, DIM), dtype=jnp.float32)
        w_gate = jax.random.randint(k_g, (HIDDEN, DIM), -127, 128, dtype=jnp.int32)
        w_up = jax.random.randint(k_u, (HIDDEN, DIM), -127, 128, dtype=jnp.int32)
        w_down = jax.random.randint(k_d, (DIM, HIDDEN), -127, 128, dtype=jnp.int32)
        return {'x': x, 'w_gate': w_gate, 'w_up': w_up, 'w_down': w_down}
    _L0_ffn_all = _L0_ffn_setup()
    _L0_ffn_in = {k: v for k, v in _L0_ffn_all.items() if k in ('w_gate', 'w_up', 'w_down')}
    del _L0_ffn_all
    return {'x': x, 'txt': txt, 'L0_tok_W': _L0_tok_in['W'], 'L0_tok_bias': _L0_tok_in['bias'], 'L0_tok_ln1_g': _L0_tok_in['ln1_g'], 'L0_tok_ln1_b': _L0_tok_in['ln1_b'], 'L0_tok_ln2_g': _L0_tok_in['ln2_g'], 'L0_tok_ln2_b': _L0_tok_in['ln2_b'], 'L0_attn_w_in': _L0_attn_in['w_in'], 'L0_attn_b_in': _L0_attn_in['b_in'], 'L0_attn_A': _L0_attn_in['A'], 'L0_attn_Bm': _L0_attn_in['Bm'], 'L0_attn_Cm': _L0_attn_in['Cm'], 'L0_attn_Dv': _L0_attn_in['Dv'], 'L0_attn_w_out': _L0_attn_in['w_out'], 'L0_attn_b_out': _L0_attn_in['b_out'], 'L0_attn_g_norm': _L0_attn_in['g_norm'], 'L0_ffn_w_gate': _L0_ffn_in['w_gate'], 'L0_ffn_w_up': _L0_ffn_in['w_up'], 'L0_ffn_w_down': _L0_ffn_in['w_down']}

def reference(x, txt, L0_tok_W, L0_tok_bias, L0_tok_ln1_g, L0_tok_ln1_b, L0_tok_ln2_g, L0_tok_ln2_b, L0_attn_w_in, L0_attn_b_in, L0_attn_A, L0_attn_Bm, L0_attn_Cm, L0_attn_Dv, L0_attn_w_out, L0_attn_b_out, L0_attn_g_norm, L0_ffn_w_gate, L0_ffn_w_up, L0_ffn_w_down):
    import jax
    import jax.numpy as jnp

    def _L0_tok_ref(x, W, bias, ln1_g, ln1_b, ln2_g, ln2_b):
        import jax, jax.numpy as jnp
        import numpy as np
        PATCH = 16
        EMBED = 256
        IN_FEATS = PATCH * PATCH * 3
        EPS = 1e-05

        def _layernorm(x, g, b):
            mu = jnp.mean(x, axis=-1, keepdims=True)
            var = jnp.mean(jnp.square(x - mu), axis=-1, keepdims=True)
            return (x - mu) * jax.lax.rsqrt(var + EPS) * g + b
        B, C, H, Wd = x.shape
        h, w = (H // PATCH, Wd // PATCH)
        p = x.reshape(B, C, h, PATCH, w, PATCH)
        p = jnp.transpose(p, (0, 2, 4, 3, 5, 1))
        p = p.reshape(B, h * w, PATCH * PATCH * C)
        y = _layernorm(p, ln1_g, ln1_b)
        y = jnp.einsum('bnf,fe->bne', y, W) + bias
        y = _layernorm(y, ln2_g, ln2_b)
        return y

    def _L0_attn_ref(x, w_in, b_in, A, Bm, Cm, Dv, w_out, b_out, g_norm):
        import jax, jax.numpy as jnp
        import numpy as np
        BATCH, SEQ, D_MODEL, D_STATE, TIMESCALE = (4, 512, 256, 64, 2)
        EPS = 1e-06

        def _reference_tuple_inner(x, w_in, b_in, A, Bm, Cm, Dv, w_out, b_out, g_norm):
            B, L, D = x.shape
            S = A.shape[1]
            ts = TIMESCALE
            x_sub = x[:, ::ts] if ts > 1 else x
            x_sub = x_sub * jax.lax.rsqrt(jnp.mean(jnp.square(x_sub), axis=-1, keepdims=True) + EPS) * g_norm
            xz = jnp.einsum('bld,ed->ble', x_sub, w_in) + b_in
            x_proj, gate = jnp.split(xz, 2, axis=-1)
            c_sum = Cm.sum(axis=0)
            h0 = jnp.zeros((B, D, S), dtype=x.dtype)

            def step(h, xt):
                h = jnp.tanh(h * A + xt[:, :, None] * Bm)
                y = h @ c_sum + Dv * xt
                return (h, y)
            h_last, ys = jax.lax.scan(step, h0, jnp.swapaxes(x_proj, 0, 1))
            out = jnp.swapaxes(ys, 0, 1)
            out = out * jax.nn.silu(gate)
            out = jnp.einsum('bld,ed->ble', out, w_out) + b_out
            if ts > 1:
                out = jnp.repeat(out, ts, axis=1)[:, :L]
            return (out, h_last)
        return _reference_tuple_inner(x, w_in, b_in, A, Bm, Cm, Dv, w_out, b_out, g_norm)[0]

    def _L0_ffn_ref(x, w_gate, w_up, w_down):
        import jax, jax.numpy as jnp
        import numpy as np
        DIM = 256
        HIDDEN = 768
        SCALE = 1.0 / 127.0

        def _dequant(w_int, dtype):
            return w_int.astype(dtype) * jnp.asarray(SCALE, dtype)
        wg = _dequant(w_gate, x.dtype)
        wu = _dequant(w_up, x.dtype)
        wd = _dequant(w_down, x.dtype)
        gate = jnp.einsum('bsd,hd->bsh', x, wg)
        up = jnp.einsum('bsd,hd->bsh', x, wu)
        h = jax.nn.silu(gate) * up
        return jnp.einsum('bsh,dh->bsd', h, wd)
    h = _L0_tok_ref(x, L0_tok_W, L0_tok_bias, L0_tok_ln1_g, L0_tok_ln1_b, L0_tok_ln2_g, L0_tok_ln2_b)
    h = jnp.concatenate([h, txt], axis=1)
    h = h + _L0_attn_ref(_layernorm(h, axis=-1), L0_attn_w_in, L0_attn_b_in, L0_attn_A, L0_attn_Bm, L0_attn_Cm, L0_attn_Dv, L0_attn_w_out, L0_attn_b_out, L0_attn_g_norm)
    h = h + _L0_ffn_ref(_layernorm(h, axis=-1), L0_ffn_w_gate, L0_ffn_w_up, L0_ffn_w_down)
    return h

_drawn_inputs = setup_inputs


def setup_inputs(seed=0):
    import zlib

    import numpy as np

    out = dict(_drawn_inputs(seed))
    spreads = {'L0_tok_ln1_g': (1.0, 0.2),
     'L0_tok_ln1_b': (0.0, 0.1),
     'L0_tok_ln2_g': (1.0, 0.2),
     'L0_tok_ln2_b': (0.0, 0.1),
     'L0_attn_b_in': (0.0, 0.611),
     'L0_attn_Dv': (1.0, 0.6),
     'L0_attn_b_out': (0.0, 0.1),
     'L0_attn_g_norm': (1.0, 0.6)}
    factors = {'L0_tok_bias': 4.865, 'L0_attn_A': 53.053, 'L0_attn_Bm': 8.0, 'L0_attn_Cm': 8.0}
    for name, (base, spread) in spreads.items():
        noise = np.random.default_rng([zlib.crc32(name.encode()), seed]).standard_normal(out[name].shape)
        drawn = base * np.exp(spread * noise) if base else spread * noise
        out[name] = jnp.asarray(drawn.astype(out[name].dtype))
    for name, factor in factors.items():
        out[name] = (out[name] * factor).astype(out[name].dtype)
    return out
```

```python
import numpy as np
import concourse.bass as bass
from concourse import mybir
from contextlib import ExitStack

FP32 = mybir.dt.float32
FP16 = mybir.dt.float16
INT32 = mybir.dt.int32
ACT = mybir.ActivationFunctionType
ALU = mybir.AluOpType

B = 32
CH, IMG, PATCH = 3, 224, 16
ROW = IMG // PATCH
NTXT = 77
L = ROW * ROW + NTXT
D, S, HID = 256, 64, 768
DB = D // 128
HB = HID // 128
STEPS = ROW // 2
TOK = B * STEPS
PT = TOK // 2
IMG_GROUPS = ROW
GROUPS = -(-L // ROW)
LAST = L - (GROUPS - 1) * ROW
LAST_STEPS = (LAST + 1) // 2
EARLY = 4
CHUNKS = 8
DL = 16
CW = DL * B
SLOTS = STEPS * CHUNKS
LAG = 3
NU = 3
KF = CH * PATCH * PATCH // 128
RAWP = CH * B
X_SCALE, B_SCALE = 16.0, 64.0
U_SCALE = X_SCALE * B_SCALE
EPS = 1e-5
RMS_EPS = 1e-6
DEQUANT = 1.0 / 127.0

C_ID, C_AVG, C_HI, C_LO, C_D0, C_D1, C_READ = 0, 128, 224, 225, 226, 227, 228
C_COLS = C_READ + STEPS * 32


def constant_table():
    t = np.zeros((128, C_COLS), np.float32)
    p = np.arange(128)
    t[:, C_ID:C_ID + 128] = np.eye(128)
    for a in range(RAWP):
        for c in range(CH):
            t[a, C_AVG + c * B + a % B] = 1.0 / CH
    t[:, C_HI] = (p // 2) % 2 == 0
    t[:, C_LO] = (p // 2) % 2 == 1
    t[:, C_D0] = (p // 4) % 2 == 0
    t[:, C_D1] = (p // 4) % 2 == 1
    for tau in range(STEPS):
        t[p, C_READ + tau * 32 + 2 * tau + p // S] = 1.0
    return t


def build(nc, x, txt, W, tok_bias, ln1_g, ln1_b, ln2_g, ln2_b, w_in, b_in, A, Bm, Cm, Dv, w_out, b_out,
          g_norm, w_gate, w_up, w_down, consts, out):
    scan_scr = nc.dram_tensor("scan_scr", [D, 4, TOK], FP16).ap()
    gate_scr = nc.dram_tensor("gate_scr", [GROUPS, 128, 2, DB * TOK], FP32).ap()
    tok_scr = nc.dram_tensor("tok_scr", [GROUPS, PT, 4, D], FP32).ap()
    y_scr = nc.dram_tensor("y_scr", [CHUNKS, 2 * STEPS, CW], FP32).ap()

    ctx = ExitStack()
    with ctx:
        def sb(name, shape, dt=FP32):
            return ctx.enter_context(nc.sbuf_tensor(name, shape, dt))

        def sem(name):
            return ctx.enter_context(nc.semaphore(name))

        cst = sb("cst", [128, C_COLS])
        ident = cst[:, C_ID:C_ID + 128]
        tok_w = sb("tok_w", [128, KF, D])
        in_w = sb("in_w", [128, DB, 2 * D])
        out_w = sb("out_w", [128, DB, D])
        gate_w = sb("gate_w", [128, DB, HID])
        up_w = sb("up_w", [128, DB, HID])
        down_w = sb("down_w", [128, HB, D])
        rows = sb("rows", [PT, 4, D])
        cols = sb("cols", [128, 4 * DB])
        a_col = sb("a_col", [128, CHUNKS * DL])
        b_st = sb("b_st", [128, CHUNKS, 2 * S], FP16)
        read_st = sb("read_st", [128, STEPS, 32])
        half_th = sb("half_th", [128, 1])

        h = sb("h", [128, CHUNKS, CW])
        x_diag = sb("x_diag", [128, CHUNKS, DL, TOK], FP16)
        y_sb = sb("y_sb", [128, 2, CW])

        raw = sb("raw", [RAWP, PATCH, ROW, PATCH])
        rawn = sb("rawn", [RAWP, ROW, PATCH * PATCH])
        raw_st = sb("raw_st", [RAWP, ROW, 6])
        raw_mv = sb("raw_mv", [RAWP, ROW, 2])
        raw_s = sb("raw_s", [RAWP, 7, ROW])
        xT = sb("xT", [128, KF, 2, TOK])
        tok = sb("tok", [PT, 4, D])
        tok_st = sb("tok_st", [PT, 4, 6])
        tok_mv = sb("tok_mv", [PT, 4, 2])
        tok_s = sb("tok_s", [PT, 3, 4])
        ln_st = sb("ln_st", [PT, 2, 6])
        ln_mv = sb("ln_mv", [PT, 2, 2])
        ln_s = sb("ln_s", [PT, 3, 2])
        xa = sb("xa", [PT, 2, D])
        xaT = sb("xaT", [128, DB, TOK])
        xf = sb("xf", [128, DB, TOK])
        x_hi = sb("x_hi", [128, DB, TOK], FP16)
        x_lo = sb("x_lo", [128, DB, TOK], FP16)
        gf = sb("gf", [128, DB, TOK])
        gth = sb("gth", [128, DB, TOK])
        gate_o = sb("gate_o", [128, 2, DB, TOK])

        yT = sb("yT", [128, DB, TOK])
        gate_i = sb("gate_i", [128, 2, DB, TOK])
        zT = sb("zT", [128, DB, TOK])
        attn = sb("attn", [PT, 2, D])
        res = sb("res", [PT, 4, D])
        res_st = sb("res_st", [PT, 4, 6])
        res_mv = sb("res_mv", [PT, 4, 2])
        res_s = sb("res_s", [PT, 3, 4])
        fx = sb("fx", [PT, 4, D])
        fxT = sb("fxT", [128, DB, 4 * PT])
        fth = sb("fth", [128, 4 * PT])
        fsg = sb("fsg", [128, 4 * PT])
        act = sb("act", [128, HB, 4 * PT])

        U = [ctx.enter_context(nc.psum_tensor(f"U{n}", [128, CW], FP32)) for n in range(NU)]
        Y = [ctx.enter_context(nc.psum_tensor(f"Y{n}", [128, CW], FP32)) for n in range(2)]
        P = [ctx.enter_context(nc.psum_tensor(f"P{n}", [128, 512], FP32)) for n in range(3)]

        stage = x_diag[:, :, :, :].rearrange("p c l t -> p (c l t)").bitcast(FP32)

        def staged(at, n, parts=128):
            return stage[0:parts, at:at + n]

        w_in_r = staged(0, 4 * D).rearrange("p (k d) -> p k d", k=4)
        w_out_r = staged(1024, 2 * D).rearrange("p (k d) -> p k d", k=2)
        a_r = staged(1536, 2 * S)
        c_r = staged(1664, 2 * S)
        b_r = staged(1792, CHUNKS * S).rearrange("p (c s) -> p c s", c=CHUNKS)
        b_d = staged(2304, CHUNKS * S).rearrange("p (c s) -> p c s", c=CHUNKS)
        b_t = staged(2816, CHUNKS * S).rearrange("p (c s) -> p c s", c=CHUNKS)
        b_h = staged(3328, CHUNKS * S // 2).bitcast(FP16).rearrange("p (c s) -> p c s", c=CHUNKS)
        g1 = staged(3584, KF)
        b1 = staged(3592, KF)
        ones = staged(3600, 128)
        b1_rep = staged(3728, KF * PT).rearrange("p (k t) -> p k t", k=KF)
        c_dup = staged(4400, 2 * S)
        c_sum = staged(4528, 1)
        w_int = [staged(4608 + 1536 * n, 1536).bitcast(INT32) for n in range(3)]
        w_f = [staged(9216 + 1536 * n, 1536) for n in range(3)]

        s_ld = sem("s_ld")
        s_ldc = sem("s_ldc")
        s_prep = sem("s_prep")
        s_tr = sem("s_tr")
        s_ev = sem("s_ev")
        raw_in = sem("raw_in")

        turns = []
        for k in range(4):
            for j in range(DB):
                turns.append((w_in_r[:, k, j * 128:j * 128 + 128], in_w[:, j, k * 128:k * 128 + 128],
                              cols[:, 6 + j:7 + j]))
        for k in range(2):
            for j in range(DB):
                turns.append((w_out_r[:, k, j * 128:j * 128 + 128], out_w[:, j, k * 128:k * 128 + 128], 0.5))
        turns.append((a_r, a_col[:, :], U_SCALE))
        for n, dst in ((0, gate_w), (1, up_w)):
            for k in range(HB):
                for j in range(DB):
                    turns.append((w_f[n][:, k * D + j * 128:k * D + j * 128 + 128],
                                  dst[:, j, k * 128:k * 128 + 128], 1.0))
        for k in range(DB):
            for j in range(HB):
                turns.append((w_f[2][:, k * HID + j * 128:k * HID + j * 128 + 128],
                              down_w[:, j, k * 128:k * 128 + 128], 0.5))

        with nc.Block() as block:
            @block.sync
            def _(sp):
                def load(dst, src, **slow):
                    sp.dma_start(dst, src, **slow).then_inc(s_ld, 16)

                load(cst[:, :], consts)
                load(tok_w[:, :, :], W.rearrange("(h k c) e -> k h c e", h=2, c=CH))
                load(g1, ln1_g.rearrange("(h k c) -> k h c", h=2, c=CH))
                load(b1, ln1_b.rearrange("(h k c) -> k h c", h=2, c=CH))
                load(w_in_r, w_in.rearrange("(k p) d -> p k d", p=128))
                load(w_out_r, w_out.rearrange("(k p) d -> p k d", p=128))
                load(a_r, A.rearrange("(p two) s -> p (two s)", two=2))
                load(c_r, Cm.rearrange("(p two) s -> p (two s)", two=2))
                for q in range(4):
                    load(b_r[q:128:4, :, :], Bm.rearrange("(c r) s -> r c s", c=CHUNKS))
                for n, v in enumerate((tok_bias, ln2_g, ln2_b, b_out)):
                    load(rows[:, n, :], v.rearrange("(a d) -> a d", a=1).to_broadcast([PT, D]))
                load(cols[:, 0:4], b_in.rearrange("(k p) -> p k", p=128), allow_slow_non_contiguous=True)
                load(cols[:, 4:6], Dv.rearrange("(k p) -> p k", p=128), allow_slow_non_contiguous=True)
                load(cols[:, 6:8], g_norm.rearrange("(k p) -> p k", p=128), allow_slow_non_contiguous=True)
                load(w_int[0].rearrange("p (k d) -> p k d", k=HB), w_gate.rearrange("(k p) d -> p k d", p=128))
                load(w_int[1].rearrange("p (k d) -> p k d", k=HB), w_up.rearrange("(k p) d -> p k d", p=128))
                load(w_int[2].rearrange("p (k d) -> p k d", k=DB), w_down.rearrange("(k p) d -> p k d", p=128))
                sp.dma_start(raw[:, :, :, :], raw_rows(x, 0)).then_inc(raw_in, 16)

            loads = 8 + 4 + 4 + 3 + 3

            @block.vector
            def _(dve):
                count = [0]

                def step(ins):
                    count[0] += 1
                    ins.then_inc(s_prep, 1)

                def settled():
                    dve.wait_ge(s_prep, count[0])

                dve.wait_ge(s_ld, 16 * loads)
                for n in range(3):
                    step(dve.tensor_scalar(w_f[n], w_int[n], DEQUANT, None, ALU.mult))
                step(dve.memset(ones, 1.0))
                step(dve.memset(half_th[:, :], -0.5))
                step(dve.memset(h[:, :, :], 0.0))
                step(dve.tensor_tensor(c_dup[:, 0:S], c_r[:, 0:S], c_r[:, S:2 * S], ALU.add))
                step(dve.tensor_tensor(c_dup[:, S:2 * S], c_r[:, 0:S], c_r[:, S:2 * S], ALU.add))
                step(dve.tensor_scalar(b_h, b_r, B_SCALE, None, ALU.mult))
                settled()
                for f in range(KF):
                    step(dve.tensor_scalar(b1_rep[:, f, :], ones[:, 0:PT], b1[:, f:f + 1], None, ALU.mult))
                step(dve.scalar_tensor_tensor(b_d, b_r, B_SCALE, b_h, ALU.mult, ALU.subtract))
                step(dve.tensor_scalar(b_t, b_h, cst[:, C_HI:C_HI + 1], None, ALU.mult))
                settled()
                step(dve.scalar_tensor_tensor(b_d, b_d, cst[:, C_LO:C_LO + 1], b_t, ALU.mult, ALU.add))
                settled()
                for d2, c in ((0, C_D0), (1, C_D1)):
                    step(dve.tensor_scalar(b_st[:, :, d2 * S:d2 * S + S], b_d, cst[:, c:c + 1], None, ALU.mult))
                vector_ready[0] = count[0]
                dve.wait_ge(s_tr, 1)
                step(dve.tensor_tensor(rows[:, 0, :], P[2][0:PT, 0:D], rows[:, 0, :], ALU.add))
                for f in range(KF):
                    step(dve.tensor_scalar(tok_w[:, f, :], tok_w[:, f, :], g1[:, f:f + 1], None, ALU.mult))
                dve.wait_ge(s_tr, 2)
                settled()
                step(dve.tensor_copy(c_sum, P[2][:, 0:1]))
                settled()
                step(dve.tensor_scalar(read_st[:, :, :],
                                       cst[:, C_READ:C_COLS].rearrange("p (t m) -> p t m", m=32),
                                       c_sum, None, ALU.mult))
                settled()
                dve.wait_ge(s_ev, len(turns))
                step(dve.memset(stage.bitcast(INT32), 0))
                settled()

            @block.tensor
            def _(pe):
                pe.wait_ge(s_prep, vector_ready[0])
                for f in range(KF):
                    mm = pe.matmul(P[2][0:PT, 0:D], b1_rep[:, f, :], tok_w[:, f, :], start=(f == 0), stop=(f == KF - 1))
                mm.then_inc(s_tr, 1)
                pe.wait_ge(s_prep, vector_ready[0] + 1)
                pe.matmul(P[2][:, 0:1], c_dup, ones[:, 0:1], start=True, stop=True).then_inc(s_tr, 1)
                for n, (src, _, _) in enumerate(turns):
                    if n >= 2:
                        pe.wait_ge(s_ev, n - 1)
                    pe.transpose(P[n % 2][:, 0:128], src, ident).then_inc(s_tr, 1)
                for n in range(NU):
                    pe.matmul(U[n][:, :], ident, h[:, 0, :], start=True, stop=True).then_inc(s_tr, 1)

            @block.scalar
            def _(sc):
                for n, (_, dst, scale) in enumerate(turns):
                    sc.wait_ge(s_tr, 3 + n)
                    sc.activation(dst, P[n % 2][:, 0:128], ACT.Copy, scale=scale).then_inc(s_ev, 1)

        raw_stats = sem("raw_stats")
        raw_aggr = sem("raw_aggr")
        avg_ps = sem("avg_ps")
        raw_small = sem("raw_small")
        raw_rstd = sem("raw_rstd")
        norm_even = sem("norm_even")
        norm_odd = sem("norm_odd")
        turned_ps = sem("turned_ps")
        xT_done = sem("xT_done")
        tok_ps = sem("tok_ps")
        tok_small = sem("tok_small")
        tok_rstd = sem("tok_rstd")
        tok_norm = sem("tok_norm")
        tok_g = sem("tok_g")
        tok_done = sem("tok_done")
        txt_in = sem("txt_in")
        ln_small = sem("ln_small")
        ln_rstd = sem("ln_rstd")
        xa_done = sem("xa_done")
        xa_ps = sem("xa_ps")
        xaT_done = sem("xaT_done")
        proj_ps = sem("proj_ps")
        xf_done = sem("xf_done")
        x_hi_done = sem("x_hi_done")
        x_lo_done = sem("x_lo_done")
        gf_done = sem("gf_done")
        gth_done = sem("gth_done")
        gate_done = sem("gate_done")
        scan_wr = sem("scan_wr")
        gate_wr = sem("gate_wr")
        tok_wr = sem("tok_wr")
        diag_early = sem("diag_early")
        diag_late = sem("diag_late")
        grown = sem("grown")
        driven = sem("driven")
        squashed = sem("squashed")
        y_ps = sem("y_ps")
        y_out = sem("y_out")
        y_wr = sem("y_wr")
        y_ld = sem("y_ld")
        gate_ld = sem("gate_ld")
        res_ld = sem("res_ld")
        z_sum = sem("z_sum")
        z_done = sem("z_done")
        attn_ps = sem("attn_ps")
        attn_done = sem("attn_done")
        res_done = sem("res_done")
        res_small = sem("res_small")
        res_rstd = sem("res_rstd")
        fx_done = sem("fx_done")
        fx_ps = sem("fx_ps")
        fxT_done = sem("fxT_done")
        ffn_g_ps = sem("ffn_g_ps")
        ffn_u_ps = sem("ffn_u_ps")
        fth_done = sem("fth_done")
        fsg_done = sem("fsg_done")
        act_done = sem("act_done")
        down_ps = sem("down_ps")
        out_done = sem("out_done")
        stored = sem("stored")
        passed = sem("passed")

        def due(count):
            return not (isinstance(count, int) and count <= 0)

        def bank_of(slot):
            return slot % NU

        def bank_user(slot):
            if slot >= NU:
                return slot - NU
            return max(n for n in range(SLOTS) if bank_of(n) == bank_of(slot)) - SLOTS

        def halves(t):
            return t.rearrange("b (t two) d -> two b t d", two=2)

        def sync_body(sp, i, image, pre, scan, post, down, steps, prefetch, last_pre, last_down):
            g, s, q, d = i, i - 1, i - 2, i - 3
            if pre and not image:
                if due(g * 16):
                    sp.wait_ge(tok_wr, g * 16)
                    sp.sem_inc(passed, 1)
                if due(g * 2):
                    sp.wait_ge(xa_done, g * 2)
                    sp.sem_inc(passed, 1)
                t0 = (g - IMG_GROUPS) * ROW
                if last_pre:
                    for par in range(2):
                        for b in range(B):
                            n = (LAST + 1 - par) // 2
                            sp.dma_start(tok[(b % 16) * STEPS:(b % 16) * STEPS + n, par * 2 + b // 16, :],
                                         txt[b, t0 + par:t0 + par + 2 * n - 1:2, :]).then_inc(txt_in, 16)
                else:
                    src = halves(txt[:, bass.ds(t0, ROW), :])
                    for par in range(2):
                        for hf in range(2):
                            sp.dma_start(tok[:, par * 2 + hf, :], src[par][hf * 16:hf * 16 + 16]).then_inc(txt_in, 16)
            if scan and steps > EARLY:
                sp.wait_ge(scan_wr, (s + 1) * 64)
                sp.sem_inc(passed, 1)
                if due(s * SLOTS):
                    sp.wait_ge(driven, s * SLOTS)
                    sp.sem_inc(passed, 1)
                load_diag(sp, EARLY, STEPS, diag_late)
            if post:
                sp.wait_ge(y_out, (q + 1) * 2)
                sp.sem_inc(passed, 1)
                if due(q * 256):
                    sp.wait_ge(y_ld, q * 256)
                    sp.sem_inc(passed, 1)
                for c4 in range(4):
                    sp.dma_start(y_scr.rearrange("(k c) m n -> c m k n", k=2)[c4],
                                 y_sb[c4 * 32:c4 * 32 + 2 * STEPS, :, :]).then_inc(y_wr, 16)
                sp.wait_ge(gate_wr, (q + 1) * 16)
                sp.sem_inc(passed, 1)
                if due(q):
                    sp.wait_ge(z_done, q)
                    sp.sem_inc(passed, 1)
                sp.dma_start(gate_i[:, :, :, :].rearrange("p a k t -> p a (k t)"), group_of(gate_scr, q)).then_inc(gate_ld, 16)
                sp.wait_ge(y_wr, (q + 1) * 64)
                sp.sem_inc(passed, 1)
                for c in range(CHUNKS):
                    for d2 in range(2):
                        p0 = (c % 4) * 32 + d2
                        sp.dma_start(
                            yT[p0:p0 + 31:2, c // 4, :].rearrange("p (t b) -> p t b", b=B),
                            y_scr[c].rearrange("(t two) (l b) -> two l t b", two=2, b=B)[d2]).then_inc(y_ld, 16)
            if down:
                for pair in range(2):
                    sp.wait_ge(out_done, d * 2 + pair + 1)
                    sp.sem_inc(passed, 1)
                    for hf in range(2):
                        k = pair * 2 + hf
                        if last_down:
                            n = (LAST + 1 - pair) // 2
                            t0 = d * ROW + pair
                            for b in range(16):
                                sp.dma_start(out[hf * 16 + b, t0:t0 + 2 * n - 1:2, :],
                                             res[b * STEPS:b * STEPS + n, k, :]).then_inc(stored, 16)
                        else:
                            dst = halves(out[:, bass.ds(d * ROW, ROW), :])
                            sp.dma_start(dst[pair][hf * 16:hf * 16 + 16], res[:, k, :]).then_inc(stored, 16)
            if post:
                sp.wait_ge(stored, d * 64 + 64)
                sp.sem_inc(passed, 1)
                sp.wait_ge(tok_wr, (q + 1) * 16)
                sp.sem_inc(passed, 1)
                sp.dma_start(res[:, :, :], group_of(tok_scr, q)).then_inc(res_ld, 16)
            if prefetch:
                sp.wait_ge(norm_even, (g + 1) * STEPS)
                sp.sem_inc(passed, 1)
                sp.wait_ge(norm_odd, (g + 1) * STEPS)
                sp.sem_inc(passed, 1)
                sp.dma_start(raw[:, :, :, :], raw_rows(x, g + 1)).then_inc(raw_in, 16)
            if pre:
                if image:
                    sp.wait_ge(tok_done, (g + 1) * 2)
                    sp.sem_inc(passed, 1)
                elif last_pre:
                    if due((g - IMG_GROUPS) * 64 + 2 * B * 16):
                        sp.wait_ge(txt_in, (g - IMG_GROUPS) * 64 + 2 * B * 16)
                        sp.sem_inc(passed, 1)
                else:
                    if due((g - IMG_GROUPS + 1) * 64):
                        sp.wait_ge(txt_in, (g - IMG_GROUPS + 1) * 64)
                        sp.sem_inc(passed, 1)
                sp.dma_start(group_of(tok_scr, g), tok[:, :, :]).then_inc(tok_wr, 16)
                sp.wait_ge(x_hi_done, g + 1)
                sp.sem_inc(passed, 1)
                sp.wait_ge(x_lo_done, g + 1)
                sp.sem_inc(passed, 1)
                if due(g * 256):
                    sp.wait_ge(diag_early, g * 256)
                    sp.sem_inc(passed, 1)
                if due(g * 256):
                    sp.wait_ge(diag_late, g * 256)
                    sp.sem_inc(passed, 1)
                for bpart in range(2):
                    for xpart, part in enumerate((x_hi, x_lo)):
                        sp.dma_start(scan_scr.rearrange("(k p) r t -> r p k t", k=DB)[bpart * 2 + xpart],
                                     part[:, :, :]).then_inc(scan_wr, 16)
                sp.wait_ge(gate_done, (g + 1) * 3)
                sp.sem_inc(passed, 1)
                sp.dma_start(group_of(gate_scr, g), gate_o[:, :, :, :].rearrange("p a k t -> p a (k t)")).then_inc(gate_wr, 16)
                sp.wait_ge(scan_wr, (g + 1) * 64)
                sp.sem_inc(passed, 1)
                if scan:
                    sp.wait_ge(driven, s * SLOTS + EARLY * CHUNKS)
                    sp.sem_inc(passed, 1)
                load_diag(sp, 0, EARLY, diag_early)

        def load_diag(sp, t0, t1, done):
            for l in range(DL):
                sp.dma_start(x_diag[l * 8:l * 8 + 8, :, l, t0 * B:t1 * B],
                             scan_scr.rearrange("(c l two) r t -> l (two r) c t", c=CHUNKS, two=2)[l][:, :, t0 * B:t1 * B])\
                    .then_inc(done, 16)

        def vector_body(dve, i, image, pre, scan, post, down, steps):
            g, s, q, d = i, i - 1, i - 2, i - 3

            def grow(slot):
                t, c = divmod(slot, CHUNKS)
                if due(s * SLOTS + bank_user(slot) + 1):
                    dve.wait_ge(squashed, s * SLOTS + bank_user(slot) + 1)
                dve.tensor_tensor(U[bank_of(slot)][:, :].rearrange("p (l b) -> p l b", b=B),
                                  h[:, c, :].rearrange("p (l b) -> p l b", b=B),
                                  a_col[:, c * DL:c * DL + DL].unsqueeze(2).to_broadcast([128, DL, B]),
                                  ALU.mult).then_inc(grown, 1)

            def raw_patch(w):
                dve.wait_ge(raw_in, (g + 1) * 16)
                dve.bn_stats(raw_st[:, w, :], raw[:, :, w, :]).then_inc(raw_stats, 1)

            def raw_means():
                dve.wait_ge(raw_stats, (g + 1) * ROW)
                dve.sem_inc(passed, 1)
                for w in range(ROW):
                    dve.bn_aggr(raw_mv[:, w, :], raw_st[:, w, :]).then_inc(raw_aggr, 1)

            def raw_deviation():
                dve.wait_ge(avg_ps, g * 2 + 1)
                dve.tensor_copy(raw_s[:, 0, :], P[2][0:RAWP, 0:ROW]).then_inc(raw_small, 1)
                dve.wait_ge(raw_small, g * 6 + 1)
                dve.tensor_tensor(raw_s[:, 1, :], raw_mv[:, :, 0], raw_s[:, 0, :], ALU.subtract).then_inc(raw_small, 1)
                dve.wait_ge(raw_small, g * 6 + 2)
                dve.tensor_tensor(raw_s[:, 2, :], raw_s[:, 1, :], raw_s[:, 1, :], ALU.mult).then_inc(raw_small, 1)
                dve.wait_ge(raw_small, g * 6 + 3)
                dve.tensor_tensor(raw_s[:, 3, :], raw_mv[:, :, 1], raw_s[:, 2, :], ALU.add).then_inc(raw_small, 1)

            def raw_variance():
                dve.wait_ge(avg_ps, g * 2 + 2)
                dve.tensor_scalar(raw_s[:, 4, :], P[2][0:RAWP, 0:ROW], EPS, None, ALU.add).then_inc(raw_small, 1)

            def raw_shift():
                dve.wait_ge(raw_rstd, g + 1)
                dve.scalar_tensor_tensor(raw_s[:, 6, :], raw_s[:, 0, :], -1.0, raw_s[:, 5, :], ALU.mult, ALU.mult)\
                    .then_inc(raw_small, 1)

            def tok_stats(pair):
                n = g * 16 + pair * 8
                dve.wait_ge(tok_ps, g * 2 + pair + 1)
                if pair == 0:
                    if due(g * 16):
                        dve.wait_ge(tok_wr, g * 16)
                for k in range(2):
                    dve.tensor_tensor(tok[:, pair * 2 + k, :], P[2][0:PT, k * D:k * D + D], rows[:, 0, :], ALU.add)\
                        .then_inc(tok_small, 1)
                for k in range(2):
                    dve.wait_ge(tok_small, n + 1 + k)
                    dve.bn_stats(tok_st[:, pair * 2 + k, :], tok[:, pair * 2 + k, :]).then_inc(tok_small, 1)
                dve.wait_ge(tok_small, n + 4)
                dve.sem_inc(passed, 1)
                for k in range(2):
                    dve.bn_aggr(tok_mv[:, pair * 2 + k, :], tok_st[:, pair * 2 + k, :]).then_inc(tok_small, 1)
                dve.wait_ge(tok_small, n + 6)
                dve.tensor_scalar(tok_s[:, 0, pair * 2:pair * 2 + 2], tok_mv[:, pair * 2:pair * 2 + 2, 1], EPS, None,
                                  ALU.add).then_inc(tok_small, 1)

            def tok_shift(pair):
                dve.wait_ge(tok_rstd, g * 2 + pair + 1)
                dve.scalar_tensor_tensor(tok_s[:, 2, pair * 2:pair * 2 + 2], tok_mv[:, pair * 2:pair * 2 + 2, 0], -1.0,
                                         tok_s[:, 1, pair * 2:pair * 2 + 2], ALU.mult, ALU.mult).then_inc(tok_small, 1)

            def ln_stats():
                if image:
                    dve.wait_ge(tok_done, g * 2 + 1)
                else:
                    dve.wait_ge(txt_in, txt_count)
                for k in range(2):
                    dve.bn_stats(ln_st[:, k, :], tok[:, k, :]).then_inc(ln_small, 1)
                dve.wait_ge(ln_small, g * 6 + 2)
                dve.sem_inc(passed, 1)
                for k in range(2):
                    dve.bn_aggr(ln_mv[:, k, :], ln_st[:, k, :]).then_inc(ln_small, 1)
                dve.wait_ge(ln_small, g * 6 + 4)
                dve.tensor_scalar(ln_s[:, 0, :], ln_mv[:, :, 1], 1.0 + RMS_EPS, EPS * RMS_EPS, ALU.mult, ALU.add)\
                    .then_inc(ln_small, 1)

            def ln_shift():
                dve.wait_ge(ln_rstd, g + 1)
                dve.scalar_tensor_tensor(ln_s[:, 2, :], ln_mv[:, :, 0], -1.0, ln_s[:, 1, :], ALU.mult, ALU.mult)\
                    .then_inc(ln_small, 1)

            def x_low_part():
                dve.wait_ge(x_hi_done, g + 1)
                if due(g * 64):
                    dve.wait_ge(scan_wr, g * 64)
                dve.scalar_tensor_tensor(x_lo[:, :, :], xf[:, :, :], X_SCALE, x_hi[:, :, :], ALU.mult, ALU.subtract)\
                    .then_inc(x_lo_done, 1)
                if due(g * 16):
                    dve.wait_ge(gate_wr, g * 16)
                for k in range(DB):
                    dve.tensor_scalar(gate_o[:, 0, k, :], xf[:, k, :], cols[:, 4 + k:5 + k], None, ALU.mult)\
                        .then_inc(gate_done, 1)

            def silu():
                dve.wait_ge(gth_done, g + 1)
                dve.scalar_tensor_tensor(gate_o[:, 1, :, :], gth[:, :, :], 1.0, gf[:, :, :], ALU.add, ALU.mult)\
                    .then_inc(gate_done, 1)

            def attn_bias():
                dve.wait_ge(attn_ps, q + 1)
                if due(q):
                    dve.wait_ge(res_done, q)
                dve.tensor_tensor(attn[:, :, :], P[0][0:PT, :].rearrange("p (k d) -> p k d", k=2),
                                  rows[:, 3, :].unsqueeze(1).to_broadcast([PT, 2, D]), ALU.add).then_inc(attn_done, 1)

            def res_stats():
                dve.wait_ge(res_done, q + 1)
                for k in range(4):
                    dve.bn_stats(res_st[:, k, :], res[:, k, :]).then_inc(res_small, 1)
                dve.wait_ge(res_small, q * 10 + 4)
                dve.sem_inc(passed, 1)
                for k in range(4):
                    dve.bn_aggr(res_mv[:, k, :], res_st[:, k, :]).then_inc(res_small, 1)
                dve.wait_ge(res_small, q * 10 + 8)
                dve.tensor_scalar(res_s[:, 0, :], res_mv[:, :, 1], EPS, None, ALU.add).then_inc(res_small, 1)

            def res_shift():
                dve.wait_ge(res_rstd, q + 1)
                dve.scalar_tensor_tensor(res_s[:, 2, :], res_mv[:, :, 0], -1.0, res_s[:, 1, :], ALU.mult, ALU.mult)\
                    .then_inc(res_small, 1)

            def ffn_silu(k):
                dve.wait_ge(fth_done, q * HB + k + 1)
                if due(q * HB + k):
                    dve.wait_ge(act_done, q * HB + k)
                dve.scalar_tensor_tensor(fsg[:, :], fth[:, :], 1.0, P[0][:, 0:4 * PT], ALU.add, ALU.mult)\
                    .then_inc(fsg_done, 1)

            def ffn_product(k):
                dve.wait_ge(ffn_u_ps, q * HB + k + 1)
                dve.wait_ge(fsg_done, q * HB + k + 1)
                dve.tensor_tensor(act[:, k, :], fsg[:, :], P[1][:, 0:4 * PT], ALU.mult).then_inc(act_done, 1)

            def finish(pair):
                dve.wait_ge(down_ps, d * 2 + pair + 1)
                dve.tensor_tensor(res[:, pair * 2:pair * 2 + 2, :], P[pair][0:PT, :].rearrange("p (k d) -> p k d", k=2),
                                  res[:, pair * 2:pair * 2 + 2, :], ALU.add).then_inc(out_done, 1)

            txt_count = ((g - IMG_GROUPS) * 64 + 2 * B * 16 if isinstance(g, int) and g == GROUPS - 1
                         else (g - IMG_GROUPS + 1) * 64)
            for slot in range(SLOTS):
                if scan and slot < steps * CHUNKS:
                    grow(slot)
                if pre and image:
                    if slot < 7:
                        raw_patch(2 * slot)
                        raw_patch(2 * slot + 1)
                    if slot == 7:
                        raw_means()
                    if slot == 10:
                        raw_deviation()
                    if slot == 12:
                        raw_variance()
                    if slot == 14:
                        raw_shift()
                    if slot == 28:
                        tok_stats(0)
                    if slot == 30:
                        tok_shift(0)
                if pre and slot == 34:
                    ln_stats()
                if pre and image and slot == 35:
                    tok_stats(1)
                if pre and slot == 36:
                    ln_shift()
                if pre and image and slot == 37:
                    tok_shift(1)
                if pre and slot == 42:
                    x_low_part()
                if pre and slot == 44:
                    silu()
                if down and slot in (4, 8):
                    finish(slot // 4 - 1)
                if post:
                    if slot == 13:
                        attn_bias()
                    if slot == 19:
                        res_stats()
                    if slot == 22:
                        res_shift()
                    if slot >= 30 and (slot - 30) % 4 == 0 and (slot - 30) // 4 < HB:
                        ffn_silu((slot - 30) // 4)
                    if slot >= 32 and (slot - 32) % 4 == 0 and (slot - 32) // 4 < HB:
                        ffn_product((slot - 32) // 4)

        def scalar_body(sc, i, image, pre, scan, post, down, steps):
            g, s, q, d = i, i - 1, i - 2, i - 3

            def squash(slot):
                t, c = divmod(slot, CHUNKS)
                sc.wait_ge(driven, s * SLOTS + slot + 1)
                sc.activation(h[:, c, :], U[bank_of(slot)][:, :], ACT.Tanh, scale=1.0 / U_SCALE).then_inc(squashed, 1)

            def y_copy(k):
                sc.wait_ge(y_ps, q + 1)
                if due(q * 64):
                    sc.wait_ge(y_wr, q * 64)
                sc.activation(y_sb[:, k, :], Y[k][:, :], ACT.Copy).then_inc(y_out, 1)

            def normalise(t):
                w = 2 * t
                sc.wait_ge(raw_small, (g + 1) * 6)
                sc.activation(rawn[:, w, :].rearrange("p (y x) -> p y x", x=PATCH), raw[:, :, w, :], ACT.Identity, scale=raw_s[:, 5, w:w + 1],
                              bias=raw_s[:, 6, w:w + 1]).then_inc(norm_even, 1)

            def xT_copy(n):
                hf, par, t0, nt = turn_part(n)
                sc.wait_ge(turned_ps, g * 8 + n + 1)
                sc.activation(
                    xT[:, hf * CH:hf * CH + CH, par, :].rearrange("p c (b t) -> p t c b", t=STEPS)[:, t0:t0 + nt],
                    P[turn_bank(n)][:, 0:nt * RAWP].rearrange("p (t c b) -> p t c b", c=CH, b=B),
                    ACT.Copy).then_inc(xT_done, 1)

            def tok_normalise(pair):
                sc.wait_ge(tok_small, g * 16 + pair * 8 + 8)
                for k in range(pair * 2, pair * 2 + 2):
                    sc.activation(tok[:, k, :], tok[:, k, :], ACT.Identity, scale=tok_s[:, 1, k:k + 1],
                                  bias=tok_s[:, 2, k:k + 1]).then_inc(tok_norm, 1)

            def ln_apply():
                sc.wait_ge(ln_small, (g + 1) * 6)
                for k in range(2):
                    sc.activation(xa[:, k, :], tok[:, k, :], ACT.Identity, scale=ln_s[:, 1, k:k + 1],
                                  bias=ln_s[:, 2, k:k + 1]).then_inc(xa_done, 1)

            def xaT_copy():
                sc.wait_ge(xa_ps, g + 1)
                sc.activation(xaT[:, :, :], P[2][:, 0:2 * TOK].rearrange("p (j t) -> p j t", j=DB),
                              ACT.Copy).then_inc(xaT_done, 1)

            def bank_in_step_order(k):
                return P[2][:, k * TOK:k * TOK + TOK].rearrange("p (b t) -> p t b", t=STEPS)

            def x_copy():
                sc.wait_ge(proj_ps, g * 2 + 1)
                if due(g):
                    sc.wait_ge(x_lo_done, g)
                if due(g * 3):
                    sc.wait_ge(gate_done, g * 3)
                for k in range(DB):
                    sc.activation(xf[:, k, :].rearrange("p (t b) -> p t b", b=B), bank_in_step_order(k),
                                  ACT.Identity, bias=cols[:, k:k + 1]).then_inc(xf_done, 1)
                sc.wait_ge(xf_done, (g + 1) * 2)
                if due(g * 64):
                    sc.wait_ge(scan_wr, g * 64)
                sc.activation(x_hi[:, :, :], xf[:, :, :], ACT.Copy, scale=X_SCALE).then_inc(x_hi_done, 1)

            def gate_copy():
                sc.wait_ge(proj_ps, g * 2 + 2)
                for k in range(DB):
                    sc.activation(gf[:, k, :].rearrange("p (t b) -> p t b", b=B), bank_in_step_order(k),
                                  ACT.Identity, bias=cols[:, 2 + k:3 + k]).then_inc(gf_done, 1)
                sc.wait_ge(gf_done, (g + 1) * 2)
                sc.activation(gth[:, :, :], gf[:, :, :], ACT.Tanh, scale=0.5).then_inc(gth_done, 1)

            def fx_apply(k):
                sc.wait_ge(res_small, (q + 1) * 10)
                sc.activation(fx[:, k, :], res[:, k, :], ACT.Identity, scale=res_s[:, 1, k:k + 1],
                              bias=res_s[:, 2, k:k + 1]).then_inc(fx_done, 1)

            def fxT_copy(j):
                sc.wait_ge(fx_ps, q * 2 + j + 1)
                sc.activation(fxT[:, j, :], P[j][:, 0:4 * PT], ACT.Copy).then_inc(fxT_done, 1)

            def ffn_tanh(k):
                sc.wait_ge(ffn_g_ps, q * HB + k + 1)
                if due(q * HB + k):
                    sc.wait_ge(fsg_done, q * HB + k)
                sc.activation(fth[:, :], P[0][:, 0:4 * PT], ACT.Tanh, scale=0.5).then_inc(fth_done, 1)

            for slot in range(SLOTS):
                if scan and slot < steps * CHUNKS:
                    squash(slot)
                if post and slot in (1, 2):
                    y_copy(slot - 1)
                if pre and image:
                    if 15 <= slot < 19:
                        normalise(2 * (slot - 15))
                        if slot < 18:
                            normalise(2 * (slot - 15) + 1)
                    if 19 <= slot < 27:
                        xT_copy(slot - 19)
                    if slot == 31:
                        tok_normalise(0)
                    if slot == 38:
                        tok_normalise(1)
                if pre:
                    if slot == 37:
                        ln_apply()
                    if slot == 39:
                        xaT_copy()
                    if slot == 41:
                        x_copy()
                    if slot == 43:
                        gate_copy()
                if post:
                    if slot in (23, 24):
                        fx_apply(2 * (slot - 23))
                        fx_apply(2 * (slot - 23) + 1)
                    if slot in (27, 28):
                        fxT_copy(slot - 27)
                    if slot >= 29 and (slot - 29) % 4 == 0 and (slot - 29) // 4 < HB:
                        ffn_tanh((slot - 29) // 4)

        def gpsimd_body(gp, i, image, pre, scan, post, down, steps):
            g, s, q, d = i, i - 1, i - 2, i - 3

            def rsqrt(dst, src, parts, n):
                return gp.tensor_tensor(dst, src, half_th[0:parts, :].to_broadcast([parts, n]), ALU.pow)

            if post:
                gp.wait_ge(y_ld, (q + 1) * 256)
                gp.wait_ge(gate_ld, (q + 1) * 16)
                gp.tensor_tensor(yT[:, :, :], yT[:, :, :], gate_i[:, 0, :, :], ALU.add).then_inc(z_sum, 1)
                gp.wait_ge(z_sum, q + 1)
                if due(q):
                    gp.wait_ge(attn_ps, q)
                gp.tensor_tensor(zT[:, :, :].rearrange("p k (b t) -> p k t b", t=STEPS),
                                 yT[:, :, :].rearrange("p k (t b) -> p k t b", b=B),
                                 gate_i[:, 1, :, :].rearrange("p k (t b) -> p k t b", b=B), ALU.mult).then_inc(z_done, 1)
            if pre and image:
                gp.wait_ge(raw_small, g * 6 + 5)
                rsqrt(raw_s[:, 5, :], raw_s[:, 4, :], RAWP, ROW).then_inc(raw_rstd, 1)
                gp.wait_ge(raw_small, g * 6 + 6)
                gp.sem_inc(passed, 1)
                for t in range(STEPS):
                    w = 2 * t + 1
                    gp.tensor_scalar(rawn[:, w, :].rearrange("p (y x) -> p y x", x=PATCH), raw[:, :, w, :], raw_s[:, 5, w:w + 1], raw_s[:, 6, w:w + 1],
                                     ALU.mult, ALU.add).then_inc(norm_odd, 1)
            if post:
                gp.wait_ge(res_ld, (q + 1) * 16)
                gp.wait_ge(attn_done, q + 1)
                both = res[:, :, :].rearrange("p (a k) d -> p a (k d)", a=2)
                gp.tensor_tensor(both, both, attn[:, :, :].rearrange("p k d -> p (k d)").unsqueeze(1)
                                 .to_broadcast([PT, 2, 2 * D]), ALU.add).then_inc(res_done, 1)
                gp.wait_ge(res_small, q * 10 + 9)
                rsqrt(res_s[:, 1, :], res_s[:, 0, :], PT, 4).then_inc(res_rstd, 1)

            def token_tiles(pair):
                two = tok[:, pair * 2:pair * 2 + 2, :]
                gp.wait_ge(tok_norm, g * 4 + pair * 2 + 2)
                gp.tensor_tensor(two, two, rows[:, 1, :].unsqueeze(1).to_broadcast([PT, 2, D]), ALU.mult)\
                    .then_inc(tok_g, 1)
                gp.wait_ge(tok_g, g * 2 + pair + 1)
                gp.tensor_tensor(two, two, rows[:, 2, :].unsqueeze(1).to_broadcast([PT, 2, D]), ALU.add)\
                    .then_inc(tok_done, 1)

            def token_rstd(pair):
                gp.wait_ge(tok_small, g * 16 + pair * 8 + 7)
                rsqrt(tok_s[:, 1, pair * 2:pair * 2 + 2], tok_s[:, 0, pair * 2:pair * 2 + 2], PT, 2).then_inc(tok_rstd, 1)

            if pre and image:
                token_rstd(0)
                token_tiles(0)
            if pre:
                gp.wait_ge(ln_small, g * 6 + 5)
                rsqrt(ln_s[:, 1, :], ln_s[:, 0, :], PT, 2).then_inc(ln_rstd, 1)
            if pre and image:
                token_rstd(1)
                token_tiles(1)

        def turn_part(n):
            hf, par, late = n // 4, (n // 2) % 2, n % 2
            return hf, par, 4 * late, 3 if late else 4

        def turn_bank(n):
            return (1, 2, 0)[n % 3]

        def tensor_body(pe, i, image, pre, scan, post, down, steps):
            g, s, q, d = i, i - 1, i - 2, i - 3
            slots = steps * CHUNKS

            def drive(slot):
                t, c = divmod(slot, CHUNKS)
                if slot == 0:
                    pe.wait_ge(diag_early, (s + 1) * 256)
                if slot == EARLY * CHUNKS:
                    pe.wait_ge(diag_late, (s + 1) * 256)
                pe.wait_ge(grown, s * SLOTS + slot + 1)
                pe.matmul(U[bank_of(slot)][:, :], b_st[:, c, :], x_diag[:, c, :, t * B:t * B + B],
                          start=False, stop=True, skip_group_check=True).then_inc(driven, 1)

            def read(slot):
                t, c = divmod(slot, CHUNKS)
                pe.wait_ge(squashed, s * SLOTS + slot + 1)
                if t == 0 and c % 4 == 0:
                    if due((s - 1) * 2 + c // 4 + 1):
                        pe.wait_ge(y_out, (s - 1) * 2 + c // 4 + 1)
                q4 = (c % 4) * 32
                mm = pe.matmul(Y[c // 4][q4:q4 + 32, :], read_st[:, t, :], h[:, c, :],
                               start=(t == 0), stop=(t == steps - 1), skip_group_check=True)
                if slot == slots - 1:
                    mm.then_inc(y_ps, 1)

            def average(which):
                if which == 0:
                    pe.wait_ge(raw_aggr, (g + 1) * ROW)
                    if due(g * 2):
                        pe.wait_ge(gf_done, g * 2)
                    src = raw_mv[:, :, 0]
                else:
                    pe.wait_ge(raw_small, g * 6 + 4)
                    src = raw_s[:, 3, :]
                pe.matmul(P[2][0:RAWP, 0:ROW], cst[0:RAWP, C_AVG:C_AVG + RAWP], src, start=True, stop=True)\
                    .then_inc(avg_ps, 1)

            def turn(n):
                hf, par, t0, nt = turn_part(n)
                if par == 0:
                    pe.wait_ge(norm_even, g * STEPS + t0 + nt)
                else:
                    pe.wait_ge(norm_odd, g * STEPS + t0 + nt)
                if n == 0 and down:
                    pe.wait_ge(out_done, d * 2 + 2)
                if n == 1:
                    pe.wait_ge(raw_small, g * 6 + 5)
                if n == 2 and post:
                    pe.wait_ge(attn_done, q + 1)
                if n >= 3:
                    pe.wait_ge(xT_done, g * 8 + n - 2)
                for k in range(nt):
                    w = 2 * (t0 + k) + par
                    mm = pe.transpose(P[turn_bank(n)][:, k * RAWP:k * RAWP + RAWP], rawn[:, w, hf * 128:hf * 128 + 128],
                                      cst[0:RAWP, C_ID:C_ID + RAWP])
                mm.then_inc(turned_ps, 1)

            def embed(k, f0):
                if f0 == 0 and k == 0:
                    pe.wait_ge(xT_done, (g + 1) * 8)
                if f0 == 0 and k == 2:
                    pe.wait_ge(tok_small, g * 16 + 2)
                for f in range(f0, f0 + 3):
                    mm = pe.matmul(P[2][0:PT, (k % 2) * D:(k % 2) * D + D],
                                   xT[:, f, k // 2, (k % 2) * PT:(k % 2) * PT + PT], tok_w[:, f, :],
                                   start=(f == 0), stop=(f == KF - 1))
                if f0 and k % 2:
                    mm.then_inc(tok_ps, 1)

            def turn_xa():
                pe.wait_ge(xa_done, (g + 1) * 2)
                if image:
                    pe.wait_ge(tok_small, g * 16 + 10)
                else:
                    if due(g * 2):
                        pe.wait_ge(gf_done, g * 2)
                for j in range(DB):
                    for k in range(2):
                        mm = pe.transpose(P[2][:, (j * 2 + k) * PT:(j * 2 + k + 1) * PT], xa[:, k, j * 128:j * 128 + 128],
                                          cst[0:PT, C_ID:C_ID + PT])
                mm.then_inc(xa_ps, 1)

            def project(part):
                if part == 0:
                    pe.wait_ge(xaT_done, g + 1)
                else:
                    pe.wait_ge(xf_done, (g + 1) * 2)
                for k in range(DB):
                    e0 = (part * DB + k) * 128
                    for j in range(DB):
                        mm = pe.matmul(P[2][:, k * TOK:k * TOK + TOK], in_w[:, j, e0:e0 + 128], xaT[:, j, :],
                                       start=(j == 0), stop=(j == DB - 1))
                mm.then_inc(proj_ps, 1)

            def attend():
                pe.wait_ge(z_done, q + 1)
                if down:
                    pe.wait_ge(out_done, d * 2 + 1)
                elif image and pre:
                    if due(g * 8):
                        pe.wait_ge(xT_done, g * 8)
                for k in range(2):
                    for j in range(DB):
                        mm = pe.matmul(P[0][0:PT, k * D:k * D + D], zT[:, j, k * PT:k * PT + PT], out_w[:, j, :],
                                       start=(j == 0), stop=(j == DB - 1))
                mm.then_inc(attn_ps, 1)

            def turn_fx(j):
                pe.wait_ge(fx_done, (q + 1) * 4)
                if pre and image:
                    if due(g * 8 + 6 + j):
                        pe.wait_ge(xT_done, g * 8 + 6 + j)
                elif j == 0:
                    pe.wait_ge(attn_done, q + 1)
                else:
                    pe.wait_ge(out_done, d * 2 + 2)
                for k in range(4):
                    mm = pe.transpose(P[j][:, k * PT:k * PT + PT], fx[:, k, j * 128:j * 128 + 128],
                                      cst[0:PT, C_ID:C_ID + PT])
                mm.then_inc(fx_ps, 1)

            def ffn(k, which):
                if k == 0:
                    pe.wait_ge(fxT_done, (q + 1) * 2)
                elif which == 0:
                    if due(q * HB + k):
                        pe.wait_ge(fsg_done, q * HB + k)
                else:
                    if due(q * HB + k):
                        pe.wait_ge(act_done, q * HB + k)
                w = (gate_w, up_w)[which]
                for j in range(DB):
                    mm = pe.matmul(P[which][:, 0:4 * PT], w[:, j, k * 128:k * 128 + 128], fxT[:, j, :],
                                   start=(j == 0), stop=(j == DB - 1))
                mm.then_inc((ffn_g_ps, ffn_u_ps)[which], 1)

            def shrink(k, f0):
                if k == 0 and f0 == 0:
                    pe.wait_ge(act_done, (d + 1) * HB)
                for f in range(f0, f0 + 3):
                    mm = pe.matmul(P[k // 2][0:PT, (k % 2) * D:(k % 2) * D + D], act[:, f, k * PT:k * PT + PT],
                                   down_w[:, f, :], start=(f == 0), stop=(f == HB - 1))
                if f0 and k % 2:
                    mm.then_inc(down_ps, 1)

            for slot in range(SLOTS):
                if scan and slot < slots:
                    drive(slot)
                    if slot >= LAG:
                        read(slot - LAG)
                if down and slot < 8:
                    shrink(slot // 2, 3 * (slot % 2))
                if pre and image:
                    if slot == 9:
                        average(0)
                    if slot == 11:
                        average(1)
                    if 18 <= slot < 26:
                        turn(slot - 18)
                    if slot in (26, 27):
                        embed(slot - 26, 0)
                        embed(slot - 26, 3)
                    if slot in (32, 33):
                        embed(slot - 30, 0)
                        embed(slot - 30, 3)
                if post:
                    if slot == 12:
                        attend()
                    if slot in (26, 27):
                        turn_fx(slot - 26)
                    if slot >= 28 and slot % 2 == 0 and (slot - 28) // 2 < 2 * HB:
                        ffn((slot - 28) // 4, (slot - 28) // 2 % 2)
                if pre:
                    if slot == 38:
                        turn_xa()
                    if slot == 40:
                        project(0)
                    if slot == 42:
                        project(1)
                if scan and slot == slots - 1:
                    for late in range(slots - LAG, slots):
                        read(late)

        IMAGE = dict(image=True, pre=True, scan=True, post=True, down=True, steps=STEPS)
        TEXT = dict(image=False, pre=True, scan=True, post=True, down=True, steps=STEPS)
        HEAD = [dict(IMAGE, scan=False, post=False, down=False), dict(IMAGE, post=False, down=False),
                dict(IMAGE, down=False)]
        TAIL = [dict(TEXT, pre=False, steps=LAST_STEPS), dict(TEXT, pre=False, scan=False),
                dict(TEXT, pre=False, scan=False, post=False)]

        def bodies(eng, body):
            for i, parts in enumerate(HEAD):
                body(eng, i, **parts)
            with eng.Fori(len(HEAD), IMG_GROUPS - 1) as i:
                body(eng, i, **IMAGE)
            body(eng, IMG_GROUPS - 1, **IMAGE)
            with eng.Fori(IMG_GROUPS, GROUPS - 1) as i:
                body(eng, i, **TEXT)
            body(eng, GROUPS - 1, **TEXT)
            for n, parts in enumerate(TAIL):
                body(eng, GROUPS + n, **parts)

        def sync_bodies(sp):
            no = dict(prefetch=False, last_pre=False, last_down=False)
            for i, parts in enumerate(HEAD):
                sync_body(sp, i, **parts, **dict(no, prefetch=True))
            with sp.Fori(len(HEAD), IMG_GROUPS - 1) as i:
                sync_body(sp, i, **IMAGE, **dict(no, prefetch=True))
            sync_body(sp, IMG_GROUPS - 1, **IMAGE, **no)
            with sp.Fori(IMG_GROUPS, GROUPS - 1) as i:
                sync_body(sp, i, **TEXT, **no)
            sync_body(sp, GROUPS - 1, **TEXT, **dict(no, last_pre=True))
            for n, parts in enumerate(TAIL):
                sync_body(sp, GROUPS + n, **parts, **dict(no, last_down=n == len(TAIL) - 1))
            sp.wait_ge(stored, (GROUPS - 1) * 64 + 64 * 16)

        with nc.Block() as block:
            @block.sync
            def _(sp):
                sync_bodies(sp)

            @block.vector
            def _(dve):
                bodies(dve, vector_body)

            @block.scalar
            def _(sc):
                bodies(sc, scalar_body)

            @block.gpsimd
            def _(gp):
                bodies(gp, gpsimd_body)

            @block.tensor
            def _(pe):
                bodies(pe, tensor_body)


vector_ready = [0]


def raw_rows(x, g):
    v = x.rearrange("b c (g y) w -> g c b (y w)", y=PATCH)
    return group_of(v, g)


def group_of(v, g):
    return v[g]


_INS = ['x', 'txt', 'L0_tok_W', 'L0_tok_bias', 'L0_tok_ln1_g', 'L0_tok_ln1_b', 'L0_tok_ln2_g', 'L0_tok_ln2_b',
        'L0_attn_w_in', 'L0_attn_b_in', 'L0_attn_A', 'L0_attn_Bm', 'L0_attn_Cm', 'L0_attn_Dv', 'L0_attn_w_out',
        'L0_attn_b_out', 'L0_attn_g_norm', 'L0_ffn_w_gate', 'L0_ffn_w_up', 'L0_ffn_w_down']


def kernel(**inputs):
    import concourse.bacc as _bacc
    from concourse.bass_utils import run_bass_kernel_spmd as _run

    nc = _bacc.Bacc("TRN2", target_bir_lowering=False, num_devices=1)
    arrays, args = {}, []
    for name in _INS:
        a = np.ascontiguousarray(inputs[name])
        arrays[f"in_{name}"] = a
        args.append(nc.dram_tensor(f"in_{name}", a.shape, mybir.dt.from_np(a.dtype), kind="ExternalInput").ap())
    table = constant_table()
    arrays["constants"] = table
    args.append(nc.dram_tensor("constants", table.shape, FP32, kind="ExternalInput").ap())
    args.append(nc.dram_tensor("out", (B, L, D), FP32, kind="ExternalOutput").ap())
    build(nc, *args)
    r = _run(nc, [arrays], core_ids=[0])
    return r.results[0]["out"]
```

```python
import numpy as np
import concourse.bass as bass
from concourse import mybir
from contextlib import ExitStack

FP32 = mybir.dt.float32
FP16 = mybir.dt.float16
INT32 = mybir.dt.int32
BF16 = mybir.dt.bfloat16
ACT = mybir.ActivationFunctionType
ALU = mybir.AluOpType

B = 32
CH, IMG, PATCH = 3, 224, 16
ROW = IMG // PATCH
NTXT = 77
L = ROW * ROW + NTXT
D, S, HID = 256, 64, 768
DB = D // 128
HB = HID // 128
STEPS = ROW // 2
TOK = B * STEPS
PT = TOK // 2
IMG_GROUPS = ROW
GROUPS = -(-L // ROW)
LAST = L - (GROUPS - 1) * ROW
LAST_STEPS = (LAST + 1) // 2
EARLY = 4
CHUNKS = 8
DL = 16
CW = DL * B
SLOTS = STEPS * CHUNKS
LAG = 3
NU = 3
KF = CH * PATCH * PATCH // 128
RAWP = CH * B
X_SCALE, B_SCALE = 16.0, 64.0
U_SCALE = X_SCALE * B_SCALE
EPS = 1e-5
RMS_EPS = 1e-6
DEQUANT = 1.0 / 127.0
EXACT = 256.0
ACT_SCALE = 2.0 ** -6

C_ID, C_AVG, C_HI, C_LO, C_D0, C_D1, C_READ = 0, 128, 224, 225, 226, 227, 228
C_COLS = C_READ + STEPS * 32


def constant_table():
    t = np.zeros((128, C_COLS), np.float32)
    p = np.arange(128)
    t[:, C_ID:C_ID + 128] = np.eye(128)
    for a in range(RAWP):
        for c in range(CH):
            t[a, C_AVG + c * B + a % B] = 1.0 / CH
    t[:, C_HI] = (p // 2) % 2 == 0
    t[:, C_LO] = (p // 2) % 2 == 1
    t[:, C_D0] = (p // 4) % 2 == 0
    t[:, C_D1] = (p // 4) % 2 == 1
    for tau in range(STEPS):
        t[p, C_READ + tau * 32 + 2 * tau + p // S] = 1.0
    return t


def build(nc, x, txt, W, tok_bias, ln1_g, ln1_b, ln2_g, ln2_b, w_in, b_in, A, Bm, Cm, Dv, w_out, b_out,
          g_norm, w_gate, w_up, w_down, consts, out):
    scan_scr = nc.dram_tensor("scan_scr", [D, 4, TOK], FP16).ap()
    gate_scr = nc.dram_tensor("gate_scr", [GROUPS, 128, 2, DB * TOK], FP32).ap()
    tok_scr = nc.dram_tensor("tok_scr", [GROUPS, PT, 4, D], FP32).ap()
    y_scr = nc.dram_tensor("y_scr", [CHUNKS, 2 * STEPS, CW], FP32).ap()

    ctx = ExitStack()
    with ctx:
        def sb(name, shape, dt=FP32):
            return ctx.enter_context(nc.sbuf_tensor(name, shape, dt))

        def sem(name):
            return ctx.enter_context(nc.semaphore(name))

        cst = sb("cst", [128, C_COLS])
        ident = cst[:, C_ID:C_ID + 128]
        tok_w = sb("tok_w", [128, KF, D])
        in_w = sb("in_w", [128, DB, 2 * D])
        out_w = sb("out_w", [128, DB, D])
        gate_w = sb("gate_w", [128, DB, HID])
        up_w = sb("up_w", [128, DB, HID])
        down_w = sb("down_w", [128, HB, D])
        large = sb("large", [128, 4])
        large_flag = sb("large_flag", [1, 1], INT32)
        rows = sb("rows", [PT, 4, D])
        cols = sb("cols", [128, 4 * DB])
        a_col = sb("a_col", [128, CHUNKS * DL])
        b_st = sb("b_st", [128, CHUNKS, 2 * S], FP16)
        read_st = sb("read_st", [128, STEPS, 32])
        half_th = sb("half_th", [128, 1])

        h = sb("h", [128, CHUNKS, CW])
        x_diag = sb("x_diag", [128, CHUNKS, DL, TOK], FP16)
        y_fx = sb("y_fx", [128, 2 * CW])
        y_sb = y_fx[:, :].rearrange("p (k n) -> p k n", k=2)

        raw = sb("raw", [RAWP, PATCH, ROW, PATCH])
        rawn = sb("rawn", [RAWP, ROW, PATCH * PATCH])
        raw_st = sb("raw_st", [RAWP, ROW, 6])
        raw_mv = sb("raw_mv", [RAWP, ROW, 2])
        raw_s = sb("raw_s", [RAWP, 7, ROW])
        xT_act = sb("xT_act", [128, KF * 2 * TOK])
        xT = xT_act[:, :].rearrange("p (f a t) -> p f a t", f=KF, a=2)
        act_hi, act_lo = (xT_act[:, n * HB * 2 * PT:(n + 1) * HB * 2 * PT].bitcast(FP16)
                          .rearrange("p (k t) -> p k t", k=HB) for n in range(2))
        tok = sb("tok", [PT, 4, D])
        tok_st = sb("tok_st", [PT, 4, 6])
        tok_mv = sb("tok_mv", [PT, 4, 2])
        tok_s = sb("tok_s", [PT, 3, 4])
        ln_st = sb("ln_st", [PT, 2, 6])
        ln_mv = sb("ln_mv", [PT, 2, 2])
        ln_s = sb("ln_s", [PT, 3, 2])
        xa = sb("xa", [PT, 2, D])
        xaT = sb("xaT", [128, DB, TOK])
        xf = sb("xf", [128, DB, TOK])
        x_hi = sb("x_hi", [128, DB, TOK], FP16)
        x_lo = sb("x_lo", [128, DB, TOK], FP16)
        gf = sb("gf", [128, DB, TOK])
        gth = sb("gth", [128, DB, TOK])
        gate_o = sb("gate_o", [128, 2, DB, TOK])

        yT = sb("yT", [128, DB, TOK])
        gate_fx = sb("gate_fx", [128, 2 * DB * TOK])
        gate_i = gate_fx[:, :].rearrange("p (a k t) -> p a k t", a=2, k=DB)
        fx_hi, fx_lo = (gate_fx[:, n * DB * TOK:(n + 1) * DB * TOK].bitcast(FP16)
                        .rearrange("p (j t) -> p j t", j=DB) for n in range(2))
        zT = sb("zT", [128, DB, TOK])
        attn = sb("attn", [PT, 2, D])
        res = sb("res", [PT, 4, D])
        res_st = sb("res_st", [PT, 4, 6])
        res_mv = sb("res_mv", [PT, 4, 2])
        res_s = sb("res_s", [PT, 3, 4])
        fx = y_fx[0:PT, :].rearrange("p (k d) -> p k d", k=4)
        fxT = sb("fxT", [128, DB, 4 * PT])
        fth = sb("fth", [128, 4 * PT])
        fsg = sb("fsg", [128, 4 * PT])
        act = sb("act", [128, HB, 4 * PT])

        U = [ctx.enter_context(nc.psum_tensor(f"U{n}", [128, CW], FP32)) for n in range(NU)]
        Y = [ctx.enter_context(nc.psum_tensor(f"Y{n}", [128, CW], FP32)) for n in range(2)]
        P = [ctx.enter_context(nc.psum_tensor(f"P{n}", [128, 512], FP32)) for n in range(3)]

        stage = x_diag[:, :, :, :].rearrange("p c l t -> p (c l t)").bitcast(FP32)
        STAGED = 9216
        WORDS = CHUNKS * DL * TOK // 2

        def staged(at, n):
            return stage[:, at:at + n]

        w_in_r = staged(0, 4 * D).rearrange("p (k d) -> p k d", k=4)
        w_out_r = staged(1024, 2 * D).rearrange("p (k d) -> p k d", k=2)
        a_r = staged(1536, 2 * S)
        c_r = staged(1664, 2 * S)
        b_r = staged(1792, CHUNKS * S).rearrange("p (c s) -> p c s", c=CHUNKS)
        b_d = staged(2304, CHUNKS * S).rearrange("p (c s) -> p c s", c=CHUNKS)
        b_t = staged(2816, CHUNKS * S).rearrange("p (c s) -> p c s", c=CHUNKS)
        b_h = staged(3328, CHUNKS * S // 2).bitcast(FP16).rearrange("p (c s) -> p c s", c=CHUNKS)
        g1 = staged(3584, KF)
        b1 = staged(3592, KF)
        ones = staged(3600, 128)
        b1_rep = staged(3728, KF * PT).rearrange("p (k t) -> p k t", k=KF)
        c_dup = staged(4400, 2 * S)
        c_sum = staged(4528, 1)
        w_f = staged(4608, 3 * 1536)
        w_gu = w_f[:, 0:2 * 1536].rearrange("p (w k j n) -> p w k j n", w=2, k=HB, j=DB)
        w_dn = w_f[:, 2 * 1536:3 * 1536].rearrange("p (k j n) -> p k j n", k=DB, j=HB)

        s_cst = sem("s_cst")
        s_ld = sem("s_ld")
        s_int = sem("s_int")
        s_half = sem("s_half")
        s_rep = sem("s_rep")
        s_flt = sem("s_flt")
        s_row = sem("s_row")
        s_sum = sem("s_sum")
        s_own = sem("s_own")
        s_bias = sem("s_bias")
        s_csum = sem("s_csum")
        s_large = sem("s_large")
        s_tr = sem("s_tr")
        s_ev = sem("s_ev")
        s_zero = sem("s_zero")
        s_bits = sem("s_bits")
        raw_in = sem("raw_in")

        turns = []
        for j in range(DB):
            turns.append(([w_in_r[:, k, j * 128:j * 128 + 128] for k in range(4)], in_w[:, j, :], cols[:, 6 + j:7 + j]))
            turns.append(([w_out_r[:, k, j * 128:j * 128 + 128] for k in range(2)], out_w[:, j, :], 0.5))
        turns.append(([a_r], a_col[:, :], U_SCALE))
        for n, dst in ((0, gate_w), (1, up_w)):
            for j in range(DB):
                for k0, k1 in ((0, 4), (4, HB)):
                    turns.append(([w_gu[:, n, k, j, :] for k in range(k0, k1)], dst[:, j, k0 * 128:k1 * 128], 1.0))
        for j in range(0, HB, 2):
            turns.append(([w_dn[:, k, jj, :] for jj in (j, j + 1) for k in range(DB)],
                          down_w[:, j:j + 2, :].rearrange("p j d -> p (j d)"), 1.0))
        INTS = 2 * DB + 1

        def setup_sync(sp):
            def load(dst, src, **slow):
                sp.dma_start(dst, src, **slow).then_inc(s_ld, 16)

            sp.dma_start(raw[:, :, :, :], raw_rows(x, 0)).then_inc(raw_in, 16)
            sp.dma_start(cst[:, :], consts).then_inc(s_cst, 16)
            load(tok_w[:, :, :], W.rearrange("(h k c) e -> k h c e", h=2, c=CH))
            load(g1, ln1_g.rearrange("(h k c) -> k h c", h=2, c=CH))
            load(b1, ln1_b.rearrange("(h k c) -> k h c", h=2, c=CH))
            load(w_in_r, w_in.rearrange("(k p) d -> p k d", p=128))
            load(w_out_r, w_out.rearrange("(k p) d -> p k d", p=128))
            load(a_r, A.rearrange("(p two) s -> p (two s)", two=2))
            load(c_r, Cm.rearrange("(p two) s -> p (two s)", two=2))
            for q in range(4):
                load(b_r[q:128:4, :, :], Bm.rearrange("(c r) s -> r c s", c=CHUNKS))
            for n, v in enumerate((tok_bias, ln2_g, ln2_b, b_out)):
                load(rows[:, n, :], v.rearrange("(a d) -> a d", a=1).to_broadcast([PT, D]))
            load(cols[:, 0:4], b_in.rearrange("(k p) -> p k", p=128), allow_slow_non_contiguous=True)
            load(cols[:, 4:6], Dv.rearrange("(k p) -> p k", p=128), allow_slow_non_contiguous=True)
            load(cols[:, 6:8], g_norm.rearrange("(k p) -> p k", p=128), allow_slow_non_contiguous=True)
            for n, w in enumerate((w_gate, w_up, w_down)):
                sp.dma_start(w_f[:, n * 1536:n * 1536 + 1536].bitcast(INT32)
                             .rearrange("p (k d) -> p k d", k=w.shape[0] // 128),
                             w.rearrange("(k p) d -> p k d", p=128)).then_inc(s_int, 16)

        LOADS = 7 + 4 + 4 + 3

        def setup_vector(dve):
            count = [0]

            def own(ins):
                count[0] += 1
                ins.then_inc(s_own, 1)

            dve.memset(half_th[:, :], -0.5).then_inc(s_half, 1)
            vector_body(dve, -1, **AHEAD)
            dve.wait_ge(s_cst, 16)
            dve.wait_ge(s_ld, 16 * LOADS)
            own(dve.memset(ones, 1.0))
            own(dve.tensor_scalar(b_h, b_r, B_SCALE, None, ALU.mult))
            own(dve.tensor_tensor(c_dup[:, 0:S], c_r[:, 0:S], c_r[:, S:2 * S], ALU.add))
            own(dve.tensor_tensor(c_dup[:, S:2 * S], c_r[:, 0:S], c_r[:, S:2 * S], ALU.add))
            dve.wait_ge(s_own, count[0])
            for f in range(KF):
                last = dve.tensor_scalar(b1_rep[:, f, :], ones[:, 0:PT], b1[:, f:f + 1], None, ALU.mult)
            last.then_inc(s_rep, 1)
            dve.wait_ge(s_int, 16 * 3)
            dve.tensor_copy(w_f, w_f.bitcast(INT32)).then_inc(s_flt, 1)
            dve.wait_ge(s_flt, 1)
            own(dve.tensor_reduce(large[:, 0:1], w_f, mybir.AxisListType.X, ALU.max, apply_absolute_value=True))
            own(dve.scalar_tensor_tensor(b_d, b_r, B_SCALE, b_h, ALU.mult, ALU.subtract))
            own(dve.tensor_scalar(b_t, b_h, cst[:, C_HI:C_HI + 1], None, ALU.mult))
            dve.wait_ge(s_own, count[0])
            dve.tensor_scalar(large[:, 1:2], large[:, 0:1], EXACT, None, ALU.is_gt).then_inc(s_rep, 1)
            own(dve.scalar_tensor_tensor(b_d, b_d, cst[:, C_LO:C_LO + 1], b_t, ALU.mult, ALU.add))
            dve.wait_ge(s_own, count[0])
            for d2, c in ((0, C_D0), (1, C_D1)):
                own(dve.tensor_scalar(b_st[:, :, d2 * S:d2 * S + S], b_d, cst[:, c:c + 1], None, ALU.mult))
            dve.wait_ge(s_bias, 1)
            dve.tensor_tensor(rows[:, 0, :], P[2][0:PT, 0:D], rows[:, 0, :], ALU.add).then_inc(s_row, 1)
            for f in range(KF):
                own(dve.tensor_scalar(tok_w[:, f, :], tok_w[:, f, :], g1[:, f:f + 1], None, ALU.mult))
            dve.wait_ge(s_csum, 1)
            dve.tensor_copy(c_sum, P[2][:, 0:1]).then_inc(s_sum, 1)
            dve.wait_ge(s_sum, 1)
            own(dve.tensor_scalar(read_st[:, :, :], cst[:, C_READ:C_COLS].rearrange("p (t m) -> p t m", m=32),
                                  c_sum, None, ALU.mult))
            dve.wait_ge(s_large, 1)
            own(dve.tensor_scalar(large_flag[:, :], P[2][0:1, 0:1], 0.5, None, ALU.is_gt))
            dve.wait_ge(s_own, count[0])
            dve.wait_ge(s_ev, len(turns))
            dve.memset(stage[:, 0:STAGED // 2].bitcast(INT32), 0)

        def setup_gpsimd(gp):
            gp.memset(h[:, :, :].rearrange("p c n -> p (c n)").bitcast(INT32), 0).then_inc(s_zero, 1)
            gp.wait_ge(s_half, 1)
            gpsimd_body(gp, -1, **AHEAD)
            gp.memset(stage[:, STAGED:WORDS].bitcast(INT32), 0)
            gp.wait_ge(s_ev, len(turns))
            gp.memset(stage[:, STAGED // 2:STAGED].bitcast(INT32), 0)

        def setup_tensor(pe):
            pe.wait_ge(s_cst, 16)
            pe.wait_ge(s_zero, 1)
            for n in range(NU):
                pe.matmul(U[n][:, :], ident, h[:, 0, :], start=True, stop=True).then_inc(s_bits, 1)
            tensor_body(pe, -1, general=False, **AHEAD)
            pe.wait_ge(s_rep, 1)
            for f in range(KF):
                mm = pe.matmul(P[2][0:PT, 0:D], b1_rep[:, f, :], tok_w[:, f, :], start=(f == 0), stop=(f == KF - 1))
            mm.then_inc(s_bias, 1)
            pe.wait_ge(s_row, 1)
            pe.matmul(P[2][:, 0:1], c_dup, ones[:, 0:1], start=True, stop=True).then_inc(s_csum, 1)
            for n, (blocks, _, _) in enumerate(turns):
                if n == 1:
                    pe.wait_ge(raw_small, 5)
                if n >= 2:
                    pe.wait_ge(s_ev, n - 1)
                if n == INTS:
                    pe.wait_ge(s_flt, 1)
                for k, src in enumerate(blocks):
                    mm = pe.transpose(P[n % 2][:, k * 128:k * 128 + 128], src, ident)
                mm.then_inc(s_tr, 1)
                if n == INTS:
                    pe.wait_ge(s_rep, 2)
                    pe.wait_ge(s_sum, 1)
                    pe.matmul(P[2][0:1, 0:1], large[:, 1:2], ones[:, 0:1], start=True, stop=True).then_inc(s_large, 1)

        def setup_scalar(sc):
            scalar_body(sc, -1, **AHEAD)
            for n, (blocks, dst, scale) in enumerate(turns):
                sc.wait_ge(s_tr, n + 1)
                sc.activation(dst, P[n % 2][:, 0:128 * len(blocks)], ACT.Copy, scale=scale).then_inc(s_ev, 1)

        raw_stats = sem("raw_stats")
        raw_aggr = sem("raw_aggr")
        avg_ps = sem("avg_ps")
        raw_small = sem("raw_small")
        raw_rstd = sem("raw_rstd")
        norm_even = sem("norm_even")
        norm_odd = sem("norm_odd")
        turned_ps = sem("turned_ps")
        xT_done = sem("xT_done")
        tok_ps = sem("tok_ps")
        tok_small = sem("tok_small")
        tok_rstd = sem("tok_rstd")
        tok_norm = sem("tok_norm")
        tok_g = sem("tok_g")
        tok_done = sem("tok_done")
        txt_in = sem("txt_in")
        ln_small = sem("ln_small")
        ln_rstd = sem("ln_rstd")
        xa_done = sem("xa_done")
        xa_ps = sem("xa_ps")
        xaT_done = sem("xaT_done")
        proj_ps = sem("proj_ps")
        xf_done = sem("xf_done")
        x_hi_done = sem("x_hi_done")
        x_lo_done = sem("x_lo_done")
        gf_done = sem("gf_done")
        gth_done = sem("gth_done")
        gate_done = sem("gate_done")
        scan_wr = sem("scan_wr")
        gate_wr = sem("gate_wr")
        tok_wr = sem("tok_wr")
        diag_early = sem("diag_early")
        diag_late = sem("diag_late")
        grown = sem("grown")
        driven = sem("driven")
        squashed = sem("squashed")
        y_ps = sem("y_ps")
        y_out = sem("y_out")
        y_wr = sem("y_wr")
        y_ld = sem("y_ld")
        gate_ld = sem("gate_ld")
        res_ld = sem("res_ld")
        z_sum = sem("z_sum")
        z_done = sem("z_done")
        attn_ps = sem("attn_ps")
        attn_done = sem("attn_done")
        res_done = sem("res_done")
        res_small = sem("res_small")
        res_rstd = sem("res_rstd")
        fx_done = sem("fx_done")
        fx_ps = sem("fx_ps")
        fxT_done = sem("fxT_done")
        fx_lo_done = sem("fx_lo_done")
        ffn_g_ps = sem("ffn_g_ps")
        ffn_u_ps = sem("ffn_u_ps")
        fth_done = sem("fth_done")
        fsg_done = sem("fsg_done")
        act_done = sem("act_done")
        act_hi_done = sem("act_hi_done")
        act_lo_done = sem("act_lo_done")
        down_ps = sem("down_ps")
        out_done = sem("out_done")
        stored = sem("stored")
        passed = sem("passed")

        FFN_GATE, FFN_UP = (32, 34, 36, 39, 43, 48), (33, 35, 37, 42, 45, 50)
        FFN_TANH, FFN_HIGH = (33, 35, 37, 40, 44, 49), (37, 39, 41, 45, 50, 53)
        FFN_SILU, FFN_PRODUCT = (35, 37, 39, 42, 46, 51), (36, 38, 40, 43, 47, 52)
        EMBED = (18, 19, 20, 21, 22, 23, 24, 25, 26, 27, 30, 31)
        NORMALISE = (31, 32, 34, 43, 46, 51, 52)

        def due(count):
            return not (isinstance(count, int) and count <= 0)

        def bank_of(slot):
            return slot % NU

        def bank_user(slot):
            if slot >= NU:
                return slot - NU
            return max(n for n in range(SLOTS) if bank_of(n) == bank_of(slot)) - SLOTS

        def halves(t):
            return t.rearrange("b (t two) d -> two b t d", two=2)

        def sync_body(sp, i, image, ahead, pre, scan, post, down, steps, last_pre=False, last_down=False):
            r, g, s, q, d = i + 1, i, i - 1, i - 2, i - 3
            if ahead:
                sp.wait_ge(norm_even, r * STEPS)
                sp.sem_inc(passed, 1)
                sp.wait_ge(norm_odd, r * STEPS)
                sp.sem_inc(passed, 1)
                sp.dma_start(raw[:, :, :, :], raw_rows(x, r)).then_inc(raw_in, 16)
            if post:
                sp.wait_ge(y_out, (q + 1) * 2)
                sp.sem_inc(passed, 1)
                if due(q * 256):
                    sp.wait_ge(y_ld, q * 256)
                    sp.sem_inc(passed, 1)
                for c4 in range(4):
                    sp.dma_start(y_scr.rearrange("(k c) m n -> c m k n", k=2)[c4],
                                 y_sb[c4 * 32:c4 * 32 + 2 * STEPS, :, :]).then_inc(y_wr, 16)
                sp.wait_ge(gate_wr, (q + 1) * 16)
                sp.sem_inc(passed, 1)
                if due(q * HB):
                    sp.wait_ge(ffn_u_ps, q * HB)
                    sp.sem_inc(passed, 1)
                sp.dma_start(gate_fx[:, :].rearrange("p (a n) -> p a n", a=2), gate_scr[q]).then_inc(gate_ld, 16)
                sp.wait_ge(y_wr, (q + 1) * 64)
                sp.sem_inc(passed, 1)
                for c in range(CHUNKS):
                    for d2 in range(2):
                        p0 = (c % 4) * 32 + d2
                        sp.dma_start(
                            yT[p0:p0 + 31:2, c // 4, :].rearrange("p (t b) -> p t b", b=B),
                            y_scr[c].rearrange("(t two) (l b) -> two l t b", two=2, b=B)[d2]).then_inc(y_ld, 16)
            if pre and not image:
                sp.wait_ge(tok_wr, g * 16)
                sp.sem_inc(passed, 1)
                sp.wait_ge(xa_done, g * 2)
                sp.sem_inc(passed, 1)
                t0 = (g - IMG_GROUPS) * ROW
                if last_pre:
                    for par in range(2):
                        for b in range(B):
                            n = (LAST + 1 - par) // 2
                            sp.dma_start(tok[(b % 16) * STEPS:(b % 16) * STEPS + n, par * 2 + b // 16, :],
                                         txt[b, t0 + par:t0 + par + 2 * n - 1:2, :]).then_inc(txt_in, 16)
                else:
                    src = halves(txt[:, bass.ds(t0, ROW), :])
                    for par in range(2):
                        for hf in range(2):
                            sp.dma_start(tok[:, par * 2 + hf, :], src[par][hf * 16:hf * 16 + 16]).then_inc(txt_in, 16)
            if scan and steps > EARLY:
                sp.wait_ge(scan_wr, (s + 1) * 64)
                sp.sem_inc(passed, 1)
                if due(s * SLOTS):
                    sp.wait_ge(driven, s * SLOTS)
                    sp.sem_inc(passed, 1)
                load_diag(sp, EARLY, STEPS, diag_late)
            if down:
                for pair in range(2):
                    sp.wait_ge(out_done, d * 2 + pair + 1)
                    sp.sem_inc(passed, 1)
                    for hf in range(2):
                        k = pair * 2 + hf
                        if last_down:
                            n = (LAST + 1 - pair) // 2
                            t0 = d * ROW + pair
                            for b in range(16):
                                sp.dma_start(out[hf * 16 + b, t0:t0 + 2 * n - 1:2, :],
                                             res[b * STEPS:b * STEPS + n, k, :]).then_inc(stored, 16)
                        else:
                            dst = halves(out[:, bass.ds(d * ROW, ROW), :])
                            sp.dma_start(dst[pair][hf * 16:hf * 16 + 16], res[:, k, :]).then_inc(stored, 16)
            if post:
                if due(q * 64):
                    sp.wait_ge(stored, q * 64)
                    sp.sem_inc(passed, 1)
                sp.wait_ge(tok_wr, (q + 1) * 16)
                sp.sem_inc(passed, 1)
                sp.dma_start(res[:, :, :], tok_scr[q]).then_inc(res_ld, 16)
            if pre:
                if image:
                    sp.wait_ge(tok_done, (g + 1) * 2)
                    sp.sem_inc(passed, 1)
                elif last_pre:
                    sp.wait_ge(txt_in, (g - IMG_GROUPS) * 64 + 2 * B * 16)
                    sp.sem_inc(passed, 1)
                else:
                    sp.wait_ge(txt_in, (g - IMG_GROUPS + 1) * 64)
                    sp.sem_inc(passed, 1)
                sp.dma_start(tok_scr[g], tok[:, :, :]).then_inc(tok_wr, 16)
                sp.wait_ge(x_hi_done, g + 1)
                sp.sem_inc(passed, 1)
                sp.wait_ge(x_lo_done, g + 1)
                sp.sem_inc(passed, 1)
                if due(g * 256):
                    sp.wait_ge(diag_early, g * 256)
                    sp.sem_inc(passed, 1)
                    sp.wait_ge(diag_late, g * 256)
                    sp.sem_inc(passed, 1)
                for bpart in range(2):
                    for xpart, part in enumerate((x_hi, x_lo)):
                        sp.dma_start(scan_scr.rearrange("(k p) r t -> r p k t", k=DB)[bpart * 2 + xpart],
                                     part[:, :, :]).then_inc(scan_wr, 16)
                sp.wait_ge(scan_wr, (g + 1) * 64)
                sp.sem_inc(passed, 1)
                if scan:
                    sp.wait_ge(driven, s * SLOTS + EARLY * CHUNKS)
                    sp.sem_inc(passed, 1)
                load_diag(sp, 0, EARLY, diag_early)
                sp.wait_ge(gate_done, (g + 1) * 3)
                sp.sem_inc(passed, 1)
                sp.dma_start(gate_scr[g], gate_o[:, :, :, :].rearrange("p a k t -> p a (k t)")).then_inc(gate_wr, 16)

        def load_diag(sp, t0, t1, done):
            for l in range(DL):
                sp.dma_start(x_diag[l * 8:l * 8 + 8, :, l, t0 * B:t1 * B],
                             scan_scr.rearrange("(c l two) r t -> l (two r) c t", c=CHUNKS, two=2)[l][:, :, t0 * B:t1 * B])\
                    .then_inc(done, 16)

        def vector_body(dve, i, image, ahead, pre, scan, post, down, steps):
            r, g, s, q, d = i + 1, i, i - 1, i - 2, i - 3

            def grow(slot):
                t, c = divmod(slot, CHUNKS)
                if due(s * SLOTS + bank_user(slot) + 1):
                    dve.wait_ge(squashed, s * SLOTS + bank_user(slot) + 1)
                dve.tensor_tensor(U[bank_of(slot)][:, :].rearrange("p (l b) -> p l b", b=B),
                                  h[:, c, :].rearrange("p (l b) -> p l b", b=B),
                                  a_col[:, c * DL:c * DL + DL].unsqueeze(2).to_broadcast([128, DL, B]),
                                  ALU.mult).then_inc(grown, 1)

            def raw_patch(w):
                dve.wait_ge(raw_in, (r + 1) * 16)
                dve.bn_stats(raw_st[:, w, :], raw[:, :, w, :]).then_inc(raw_stats, 1)

            def raw_means():
                dve.wait_ge(raw_stats, (r + 1) * ROW)
                dve.sem_inc(passed, 1)
                for w in range(ROW):
                    dve.bn_aggr(raw_mv[:, w, :], raw_st[:, w, :]).then_inc(raw_aggr, 1)

            def raw_deviation():
                dve.wait_ge(avg_ps, r * 2 + 1)
                dve.tensor_copy(raw_s[:, 0, :], P[1][0:RAWP, 0:ROW]).then_inc(raw_small, 1)
                dve.wait_ge(raw_small, r * 6 + 1)
                dve.tensor_tensor(raw_s[:, 1, :], raw_mv[:, :, 0], raw_s[:, 0, :], ALU.subtract).then_inc(raw_small, 1)
                dve.wait_ge(raw_small, r * 6 + 2)
                dve.tensor_tensor(raw_s[:, 2, :], raw_s[:, 1, :], raw_s[:, 1, :], ALU.mult).then_inc(raw_small, 1)
                dve.wait_ge(raw_small, r * 6 + 3)
                dve.tensor_tensor(raw_s[:, 3, :], raw_mv[:, :, 1], raw_s[:, 2, :], ALU.add).then_inc(raw_small, 1)

            def raw_variance():
                dve.wait_ge(avg_ps, r * 2 + 2)
                dve.tensor_scalar(raw_s[:, 4, :], P[1][0:RAWP, 0:ROW], EPS, None, ALU.add).then_inc(raw_small, 1)

            def raw_shift():
                dve.wait_ge(raw_rstd, r + 1)
                dve.scalar_tensor_tensor(raw_s[:, 6, :], raw_s[:, 0, :], -1.0, raw_s[:, 5, :], ALU.mult, ALU.mult)\
                    .then_inc(raw_small, 1)

            def tok_stats(pair):
                n = g * 16 + pair * 8
                dve.wait_ge(tok_ps, g * 2 + pair + 1)
                if pair == 0:
                    if due(g * 16):
                        dve.wait_ge(tok_wr, g * 16)
                for k in range(2):
                    dve.tensor_tensor(tok[:, pair * 2 + k, :], P[2 - pair][0:PT, k * D:k * D + D], rows[:, 0, :], ALU.add)\
                        .then_inc(tok_small, 1)
                for k in range(2):
                    dve.wait_ge(tok_small, n + 1 + k)
                    dve.bn_stats(tok_st[:, pair * 2 + k, :], tok[:, pair * 2 + k, :]).then_inc(tok_small, 1)
                dve.wait_ge(tok_small, n + 4)
                dve.sem_inc(passed, 1)
                for k in range(2):
                    dve.bn_aggr(tok_mv[:, pair * 2 + k, :], tok_st[:, pair * 2 + k, :]).then_inc(tok_small, 1)
                dve.wait_ge(tok_small, n + 6)
                dve.tensor_scalar(tok_s[:, 0, pair * 2:pair * 2 + 2], tok_mv[:, pair * 2:pair * 2 + 2, 1], EPS, None,
                                  ALU.add).then_inc(tok_small, 1)

            def tok_shift(pair):
                dve.wait_ge(tok_rstd, g * 2 + pair + 1)
                dve.scalar_tensor_tensor(tok_s[:, 2, pair * 2:pair * 2 + 2], tok_mv[:, pair * 2:pair * 2 + 2, 0], -1.0,
                                         tok_s[:, 1, pair * 2:pair * 2 + 2], ALU.mult, ALU.mult).then_inc(tok_small, 1)

            def ln_stats():
                if image:
                    dve.wait_ge(tok_done, g * 2 + 1)
                else:
                    dve.wait_ge(txt_in, txt_count)
                for k in range(2):
                    dve.bn_stats(ln_st[:, k, :], tok[:, k, :]).then_inc(ln_small, 1)
                dve.wait_ge(ln_small, g * 6 + 2)
                dve.sem_inc(passed, 1)
                for k in range(2):
                    dve.bn_aggr(ln_mv[:, k, :], ln_st[:, k, :]).then_inc(ln_small, 1)
                dve.wait_ge(ln_small, g * 6 + 4)
                dve.tensor_scalar(ln_s[:, 0, :], ln_mv[:, :, 1], 1.0 + RMS_EPS, EPS * RMS_EPS, ALU.mult, ALU.add)\
                    .then_inc(ln_small, 1)

            def ln_shift():
                dve.wait_ge(ln_rstd, g + 1)
                dve.scalar_tensor_tensor(ln_s[:, 2, :], ln_mv[:, :, 0], -1.0, ln_s[:, 1, :], ALU.mult, ALU.mult)\
                    .then_inc(ln_small, 1)

            def x_low_part():
                dve.wait_ge(x_hi_done, g + 1)
                if due(g * 64):
                    dve.wait_ge(scan_wr, g * 64)
                dve.scalar_tensor_tensor(x_lo[:, :, :], xf[:, :, :], X_SCALE, x_hi[:, :, :], ALU.mult, ALU.subtract)\
                    .then_inc(x_lo_done, 1)

            def skip_term():
                dve.wait_ge(xf_done, (g + 1) * 2)
                if due(g * 16):
                    dve.wait_ge(gate_wr, g * 16)
                for k in range(DB):
                    dve.tensor_scalar(gate_o[:, 0, k, :], xf[:, k, :], cols[:, 4 + k:5 + k], None, ALU.mult)\
                        .then_inc(gate_done, 1)

            def silu():
                dve.wait_ge(gth_done, g + 1)
                dve.scalar_tensor_tensor(gate_o[:, 1, :, :], gth[:, :, :], 1.0, gf[:, :, :], ALU.add, ALU.mult)\
                    .then_inc(gate_done, 1)

            def attn_bias():
                dve.wait_ge(attn_ps, q + 1)
                if due(q):
                    dve.wait_ge(res_done, q)
                dve.tensor_tensor(attn[:, :, :], P[0][0:PT, :].rearrange("p (k d) -> p k d", k=2),
                                  rows[:, 3, :].unsqueeze(1).to_broadcast([PT, 2, D]), ALU.add).then_inc(attn_done, 1)

            def res_stats():
                dve.wait_ge(res_done, q + 1)
                for k in range(4):
                    dve.bn_stats(res_st[:, k, :], res[:, k, :]).then_inc(res_small, 1)

            def res_variance():
                dve.wait_ge(res_small, q * 10 + 4)
                dve.sem_inc(passed, 1)
                for k in range(4):
                    dve.bn_aggr(res_mv[:, k, :], res_st[:, k, :]).then_inc(res_small, 1)
                dve.wait_ge(res_small, q * 10 + 8)
                dve.tensor_scalar(res_s[:, 0, :], res_mv[:, :, 1], EPS, None, ALU.add).then_inc(res_small, 1)

            def res_shift():
                dve.wait_ge(res_rstd, q + 1)
                dve.scalar_tensor_tensor(res_s[:, 2, :], res_mv[:, :, 0], -1.0, res_s[:, 1, :], ALU.mult, ALU.mult)\
                    .then_inc(res_small, 1)

            def ffn_silu(k):
                dve.wait_ge(fth_done, q * HB + k + 1)
                if due(q * HB + k):
                    dve.wait_ge(act_done, q * HB + k)
                dve.scalar_tensor_tensor(fsg[:, :], fth[:, :], 1.0, P[0][:, 0:4 * PT], ALU.add, ALU.mult)\
                    .then_inc(fsg_done, 1)

            def ffn_product(k):
                dve.wait_ge(ffn_u_ps, q * HB + k + 1)
                dve.wait_ge(fsg_done, q * HB + k + 1)
                dve.scalar_tensor_tensor(act[:, k, :], fsg[:, :], ACT_SCALE * 0.5 * DEQUANT * DEQUANT, P[1][:, 0:4 * PT],
                                         ALU.mult, ALU.mult).then_inc(act_done, 1)

            def fx_low_part(j):
                dve.wait_ge(fxT_done, q * 4 + 2 * j + 2)
                dve.tensor_tensor(fx_lo[:, j, :], fxT[:, j, :], fx_hi[:, j, :], ALU.subtract).then_inc(fx_lo_done, 1)

            def finish(pair):
                dve.wait_ge(down_ps, d * 2 + pair + 1)
                dve.scalar_tensor_tensor(res[:, pair * 2:pair * 2 + 2, :],
                                         P[pair][0:PT, :].rearrange("p (k d) -> p k d", k=2), DEQUANT / ACT_SCALE,
                                         res[:, pair * 2:pair * 2 + 2, :], ALU.mult, ALU.add).then_inc(out_done, 1)

            txt_count = ((g - IMG_GROUPS) * 64 + 2 * B * 16 if isinstance(g, int) and g == GROUPS - 1
                         else (g - IMG_GROUPS + 1) * 64)
            for slot in range(SLOTS):
                if scan and slot < steps * CHUNKS:
                    grow(slot)
                if down and slot in (6, 10):
                    finish((6, 10).index(slot))
                if ahead:
                    if 6 <= slot < 6 + ROW:
                        raw_patch(slot - 6)
                    if slot == 20:
                        raw_means()
                    if slot == 22:
                        raw_deviation()
                    if slot == 24:
                        raw_variance()
                    if slot == 28:
                        raw_shift()
                if post:
                    if slot == 19:
                        attn_bias()
                    if slot == 24:
                        res_stats()
                    if slot == 25:
                        res_variance()
                    if slot == 27:
                        res_shift()
                    if slot in (31, 32):
                        fx_low_part(slot - 31)
                if pre and image:
                    if slot in (26, 33):
                        tok_stats((26, 33).index(slot))
                    if slot in (29, 36):
                        tok_shift((29, 36).index(slot))
                if pre:
                    if slot == 34:
                        ln_stats()
                    if slot == 37:
                        ln_shift()
                    if slot == 44:
                        x_low_part()
                    if slot == 45:
                        skip_term()
                    if slot == 50:
                        silu()
                if post:
                    if slot in FFN_SILU:
                        ffn_silu(FFN_SILU.index(slot))
                    if slot in FFN_PRODUCT:
                        ffn_product(FFN_PRODUCT.index(slot))

        def scalar_body(sc, i, image, ahead, pre, scan, post, down, steps):
            r, g, s, q, d = i + 1, i, i - 1, i - 2, i - 3

            def squash(slot):
                t, c = divmod(slot, CHUNKS)
                sc.wait_ge(driven, s * SLOTS + slot + 1)
                sc.activation(h[:, c, :], U[bank_of(slot)][:, :], ACT.Tanh, scale=1.0 / U_SCALE).then_inc(squashed, 1)

            def y_copy(k):
                sc.wait_ge(y_ps, q + 1)
                if due(q * 64):
                    sc.wait_ge(y_wr, q * 64)
                sc.activation(y_sb[:, k, :], Y[k][:, :], ACT.Copy).then_inc(y_out, 1)

            def normalise(t):
                w = 2 * t
                sc.wait_ge(raw_small, (r + 1) * 6)
                sc.activation(rawn[:, w, :].rearrange("p (y x) -> p y x", x=PATCH), raw[:, :, w, :], ACT.Identity, scale=raw_s[:, 5, w:w + 1],
                              bias=raw_s[:, 6, w:w + 1]).then_inc(norm_even, 1)

            def xT_copy(n):
                hf, par, t0, nt = turn_part(n)
                sc.wait_ge(turned_ps, g * 8 + n + 1)
                sc.activation(
                    xT[:, hf * CH:hf * CH + CH, par, :].rearrange("p c (b t) -> p t c b", t=STEPS)[:, t0:t0 + nt],
                    P[turn_bank(n)][:, 0:nt * RAWP].rearrange("p (t c b) -> p t c b", c=CH, b=B),
                    ACT.Copy).then_inc(xT_done, 1)

            def tok_normalise(pair):
                sc.wait_ge(tok_small, g * 16 + pair * 8 + 8)
                for k in range(pair * 2, pair * 2 + 2):
                    sc.activation(tok[:, k, :], tok[:, k, :], ACT.Identity, scale=tok_s[:, 1, k:k + 1],
                                  bias=tok_s[:, 2, k:k + 1]).then_inc(tok_norm, 1)

            def ln_apply():
                sc.wait_ge(ln_small, (g + 1) * 6)
                for k in range(2):
                    sc.activation(xa[:, k, :], tok[:, k, :], ACT.Identity, scale=ln_s[:, 1, k:k + 1],
                                  bias=ln_s[:, 2, k:k + 1]).then_inc(xa_done, 1)

            def xaT_copy():
                sc.wait_ge(xa_ps, g + 1)
                sc.activation(xaT[:, :, :], P[2][:, 0:2 * TOK].rearrange("p (j t) -> p j t", j=DB),
                              ACT.Copy).then_inc(xaT_done, 1)

            def bank_in_step_order(k):
                return P[2][:, k * TOK:k * TOK + TOK].rearrange("p (b t) -> p t b", t=STEPS)

            def x_copy():
                sc.wait_ge(proj_ps, g * 2 + 1)
                if due(g):
                    sc.wait_ge(x_lo_done, g)
                if due(g * 3):
                    sc.wait_ge(gate_done, g * 3)
                for k in range(DB):
                    sc.activation(xf[:, k, :].rearrange("p (t b) -> p t b", b=B), bank_in_step_order(k),
                                  ACT.Identity, bias=cols[:, k:k + 1]).then_inc(xf_done, 1)
                sc.wait_ge(xf_done, (g + 1) * 2)
                if due(g * 64):
                    sc.wait_ge(scan_wr, g * 64)
                sc.activation(x_hi[:, :, :], xf[:, :, :], ACT.Copy, scale=X_SCALE).then_inc(x_hi_done, 1)

            def gate_copy():
                sc.wait_ge(proj_ps, g * 2 + 2)
                for k in range(DB):
                    sc.activation(gf[:, k, :].rearrange("p (t b) -> p t b", b=B), bank_in_step_order(k),
                                  ACT.Identity, bias=cols[:, 2 + k:3 + k]).then_inc(gf_done, 1)
                sc.wait_ge(gf_done, (g + 1) * 2)
                sc.activation(gth[:, :, :], gf[:, :, :], ACT.Tanh, scale=0.5).then_inc(gth_done, 1)

            def fx_apply(k):
                sc.wait_ge(res_small, (q + 1) * 10)
                sc.activation(fx[:, k, :], res[:, k, :], ACT.Identity, scale=res_s[:, 1, k:k + 1],
                              bias=res_s[:, 2, k:k + 1]).then_inc(fx_done, 1)

            def fxT_copy(j):
                sc.wait_ge(fx_ps, q * 2 + j + 1)
                sc.activation(fxT[:, j, :], P[2 * j][:, 0:4 * PT], ACT.Copy).then_inc(fxT_done, 1)
                sc.activation(fx_hi[:, j, :], P[2 * j][:, 0:4 * PT], ACT.Copy).then_inc(fxT_done, 1)

            def ffn_tanh(k):
                sc.wait_ge(ffn_g_ps, q * HB + k + 1)
                if due(q * HB + k):
                    sc.wait_ge(fsg_done, q * HB + k)
                sc.activation(fth[:, :], P[0][:, 0:4 * PT], ACT.Tanh, scale=0.5 * DEQUANT).then_inc(fth_done, 1)

            def act_high_part(k):
                sc.wait_ge(act_done, q * HB + k + 1)
                sc.activation(act_hi[:, k, :], act[:, k, :], ACT.Copy).then_inc(act_hi_done, 1)

            for slot in range(SLOTS):
                if scan and slot < steps * CHUNKS:
                    squash(slot)
                if post:
                    if slot < 2:
                        y_copy(slot)
                    if slot in (26, 27):
                        fx_apply(2 * (slot - 26))
                        fx_apply(2 * (slot - 26) + 1)
                    if slot in (29, 30):
                        fxT_copy(slot - 29)
                    if slot in FFN_TANH:
                        ffn_tanh(FFN_TANH.index(slot))
                    if slot in FFN_HIGH:
                        act_high_part(FFN_HIGH.index(slot))
                if pre and image:
                    if 9 <= slot < 17:
                        xT_copy(slot - 9)
                    if slot in (28, 38):
                        tok_normalise((28, 38).index(slot))
                if ahead and slot in NORMALISE:
                    normalise(NORMALISE.index(slot))
                if pre:
                    if slot == 36:
                        ln_apply()
                    if slot == 39:
                        xaT_copy()
                    if slot == 42:
                        x_copy()
                    if slot == 48:
                        gate_copy()

        def gpsimd_body(gp, i, image, ahead, pre, scan, post, down, steps):
            r, g, s, q, d = i + 1, i, i - 1, i - 2, i - 3

            def rsqrt(dst, src, parts, n):
                return gp.tensor_tensor(dst, src, half_th[0:parts, :].to_broadcast([parts, n]), ALU.pow)

            if post:
                gp.wait_ge(y_ld, (q + 1) * 256)
                gp.wait_ge(gate_ld, (q + 1) * 16)
                gp.tensor_tensor(yT[:, :, :], yT[:, :, :], gate_i[:, 0, :, :], ALU.add).then_inc(z_sum, 1)
                gp.wait_ge(z_sum, q + 1)
                if due(q):
                    gp.wait_ge(attn_ps, q)
                gp.tensor_tensor(zT[:, :, :].rearrange("p k (b t) -> p k t b", t=STEPS),
                                 yT[:, :, :].rearrange("p k (t b) -> p k t b", b=B),
                                 gate_i[:, 1, :, :].rearrange("p k (t b) -> p k t b", b=B), ALU.mult).then_inc(z_done, 1)
            if post:
                gp.wait_ge(res_ld, (q + 1) * 16)
                gp.wait_ge(attn_done, q + 1)
                both = res[:, :, :].rearrange("p (a k) d -> p a (k d)", a=2)
                gp.tensor_tensor(both, both, attn[:, :, :].rearrange("p k d -> p (k d)").unsqueeze(1)
                                 .to_broadcast([PT, 2, 2 * D]), ALU.add).then_inc(res_done, 1)
                gp.wait_ge(res_small, q * 10 + 9)
                rsqrt(res_s[:, 1, :], res_s[:, 0, :], PT, 4).then_inc(res_rstd, 1)
            if ahead:
                gp.wait_ge(raw_small, r * 6 + 5)
                rsqrt(raw_s[:, 5, :], raw_s[:, 4, :], RAWP, ROW).then_inc(raw_rstd, 1)

            def normalise(t):
                w = 2 * t + 1
                if t == 0:
                    gp.wait_ge(raw_small, r * 6 + 6)
                    gp.sem_inc(passed, 1)
                gp.tensor_scalar(rawn[:, w, :].rearrange("p (y x) -> p y x", x=PATCH), raw[:, :, w, :],
                                 raw_s[:, 5, w:w + 1], raw_s[:, 6, w:w + 1], ALU.mult, ALU.add).then_inc(norm_odd, 1)

            def act_low_part(k):
                gp.wait_ge(act_hi_done, q * HB + k + 1)
                gp.tensor_tensor(act_lo[:, k, :], act[:, k, :], act_hi[:, k, :], ALU.subtract).then_inc(act_lo_done, 1)

            def token_tiles(pair):
                two = tok[:, pair * 2:pair * 2 + 2, :]
                gp.wait_ge(tok_norm, g * 4 + pair * 2 + 2)
                gp.tensor_tensor(two, two, rows[:, 1, :].unsqueeze(1).to_broadcast([PT, 2, D]), ALU.mult)\
                    .then_inc(tok_g, 1)
                gp.wait_ge(tok_g, g * 2 + pair + 1)
                gp.tensor_tensor(two, two, rows[:, 2, :].unsqueeze(1).to_broadcast([PT, 2, D]), ALU.add)\
                    .then_inc(tok_done, 1)

            def token_rstd(pair):
                gp.wait_ge(tok_small, g * 16 + pair * 8 + 7)
                rsqrt(tok_s[:, 1, pair * 2:pair * 2 + 2], tok_s[:, 0, pair * 2:pair * 2 + 2], PT, 2).then_inc(tok_rstd, 1)

            if pre and image:
                token_rstd(0)
                token_tiles(0)
            if ahead:
                for t in range(3):
                    normalise(t)
            if pre:
                gp.wait_ge(ln_small, g * 6 + 5)
                rsqrt(ln_s[:, 1, :], ln_s[:, 0, :], PT, 2).then_inc(ln_rstd, 1)
            if pre and image:
                token_rstd(1)
                token_tiles(1)
            for k in range(HB):
                if post:
                    act_low_part(k)
                if ahead and k < STEPS - 3:
                    normalise(k + 3)

        def turn_part(n):
            hf, par, late = n // 4, (n // 2) % 2, n % 2
            return hf, par, 4 * late, 3 if late else 4

        def turn_bank(n):
            return (2, 1, 0)[n % 3]

        def whole_part(w):
            return w.bitcast(BF16)[:, 1::2]

        def tensor_body(pe, i, image, ahead, pre, scan, post, down, steps, general):
            r, g, s, q, d = i + 1, i, i - 1, i - 2, i - 3
            slots = steps * CHUNKS

            def drive(slot):
                t, c = divmod(slot, CHUNKS)
                if slot == 0:
                    pe.wait_ge(diag_early, (s + 1) * 256)
                if slot == EARLY * CHUNKS:
                    pe.wait_ge(diag_late, (s + 1) * 256)
                pe.wait_ge(grown, s * SLOTS + slot + 1)
                pe.matmul(U[bank_of(slot)][:, :], b_st[:, c, :], x_diag[:, c, :, t * B:t * B + B],
                          start=False, stop=True, skip_group_check=True).then_inc(driven, 1)

            def read(slot):
                t, c = divmod(slot, CHUNKS)
                pe.wait_ge(squashed, s * SLOTS + slot + 1)
                if t == 0 and c % 4 == 0:
                    if due((s - 1) * 2 + c // 4 + 1):
                        pe.wait_ge(y_out, (s - 1) * 2 + c // 4 + 1)
                q4 = (c % 4) * 32
                mm = pe.matmul(Y[c // 4][q4:q4 + 32, :], read_st[:, t, :], h[:, c, :],
                               start=(t == 0), stop=(t == steps - 1), skip_group_check=True)
                if slot == slots - 1:
                    mm.then_inc(y_ps, 1)

            def average(which):
                if which == 0:
                    pe.wait_ge(raw_aggr, (r + 1) * ROW)
                    src = raw_mv[:, :, 0]
                else:
                    pe.wait_ge(raw_small, r * 6 + 4)
                    src = raw_s[:, 3, :]
                pe.matmul(P[1][0:RAWP, 0:ROW], cst[0:RAWP, C_AVG:C_AVG + RAWP], src, start=True, stop=True)\
                    .then_inc(avg_ps, 1)

            def turn(n):
                hf, par, t0, nt = turn_part(n)
                if par == 0:
                    pe.wait_ge(norm_even, g * STEPS + t0 + nt)
                else:
                    pe.wait_ge(norm_odd, g * STEPS + t0 + nt)
                if n == 0 and due(g * 2):
                    pe.wait_ge(gf_done, g * 2)
                if n == 1:
                    if down:
                        pe.wait_ge(out_done, d * 2 + 2)
                    elif due(g * 16 - 6):
                        pe.wait_ge(tok_small, g * 16 - 6)
                if n >= 3:
                    pe.wait_ge(xT_done, g * 8 + n - 2)
                for k in range(nt):
                    w = 2 * (t0 + k) + par
                    mm = pe.transpose(P[turn_bank(n)][:, k * RAWP:k * RAWP + RAWP], rawn[:, w, hf * 128:hf * 128 + 128],
                                      cst[0:RAWP, C_ID:C_ID + RAWP])
                mm.then_inc(turned_ps, 1)

            def embed(k, f0):
                if f0 == 0 and k == 0:
                    pe.wait_ge(xT_done, (g + 1) * 8)
                if f0 == 0 and k == 2 and ahead:
                    pe.wait_ge(raw_small, r * 6 + 5)
                for f in range(f0, f0 + 2):
                    mm = pe.matmul(P[2 - k // 2][0:PT, (k % 2) * D:(k % 2) * D + D],
                                   xT[:, f, k // 2, (k % 2) * PT:(k % 2) * PT + PT], tok_w[:, f, :],
                                   start=(f == 0), stop=(f == KF - 1))
                if f0 == KF - 2 and k % 2:
                    mm.then_inc(tok_ps, 1)

            def turn_xa():
                pe.wait_ge(xa_done, (g + 1) * 2)
                if post:
                    pe.wait_ge(fxT_done, (q + 1) * 4)
                elif image:
                    pe.wait_ge(tok_small, g * 16 + 2)
                for j in range(DB):
                    for k in range(2):
                        mm = pe.transpose(P[2][:, (j * 2 + k) * PT:(j * 2 + k + 1) * PT], xa[:, k, j * 128:j * 128 + 128],
                                          cst[0:PT, C_ID:C_ID + PT])
                mm.then_inc(xa_ps, 1)

            def project(part, k):
                if part == 0:
                    pe.wait_ge(xaT_done, g + 1)
                else:
                    pe.wait_ge(xf_done, (g + 1) * 2)
                e0 = (part * DB + k) * 128
                for j in range(DB):
                    mm = pe.matmul(P[2][:, k * TOK:k * TOK + TOK], in_w[:, j, e0:e0 + 128], xaT[:, j, :],
                                   start=(j == 0), stop=(j == DB - 1))
                if k == DB - 1:
                    mm.then_inc(proj_ps, 1)

            def attend(k):
                pe.wait_ge(z_done, q + 1)
                if pre and image:
                    pe.wait_ge(xT_done, g * 8 + 6)
                elif down:
                    pe.wait_ge(out_done, d * 2 + 1)
                for j in range(DB):
                    mm = pe.matmul(P[0][0:PT, k * D:k * D + D], zT[:, j, k * PT:k * PT + PT], out_w[:, j, :],
                                   start=(j == 0), stop=(j == DB - 1))
                if k == 1:
                    mm.then_inc(attn_ps, 1)

            def turn_fx(j):
                pe.wait_ge(fx_done, (q + 1) * 4)
                if j == 0:
                    pe.wait_ge(attn_done, q + 1)
                elif pre and image:
                    pe.wait_ge(tok_small, g * 16 + 2)
                elif pre or i == GROUPS:
                    pe.wait_ge(gf_done, g * 2)
                for k in range(4):
                    mm = pe.transpose(P[2 * j][:, k * PT:k * PT + PT], fx[:, k, j * 128:j * 128 + 128],
                                      cst[0:PT, C_ID:C_ID + PT])
                mm.then_inc(fx_ps, 1)

            def ffn(k, which):
                if k == 0 and which == 0:
                    pe.wait_ge(fxT_done, (q + 1) * 4)
                    pe.wait_ge(fx_lo_done, (q + 1) * 2)
                if k == 0 and which == 1:
                    if pre and image:
                        pe.wait_ge(tok_small, g * 16 + 10)
                    elif down:
                        pe.wait_ge(out_done, d * 2 + 2)
                if k > 0 and which == 0:
                    pe.wait_ge(fsg_done, q * HB + k)
                if k > 0 and which == 1:
                    pe.wait_ge(act_done, q * HB + k)
                w = (gate_w, up_w)[which]
                bank = P[which][:, 0:4 * PT]
                for j in range(DB):
                    if general:
                        mm = pe.matmul(bank, w[:, j, k * 128:k * 128 + 128], fxT[:, j, :],
                                       start=(j == 0), stop=(j == DB - 1))
                    else:
                        half = whole_part(w[:, j, k * 128:k * 128 + 128])
                        pe.matmul(bank, half, fx_hi[:, j, :], start=(j == 0), stop=False)
                        mm = pe.matmul(bank, half, fx_lo[:, j, :], start=False, stop=(j == DB - 1))
                mm.then_inc((ffn_g_ps, ffn_u_ps)[which], 1)

            def shrink(k, f0):
                if k == 0 and f0 == 0:
                    pe.wait_ge(act_lo_done, (d + 1) * HB)
                bank = P[k // 2][0:PT, (k % 2) * D:(k % 2) * D + D]
                for f in range(f0, f0 + 3):
                    if general:
                        mm = pe.matmul(bank, act[:, f, k * PT:k * PT + PT], down_w[:, f, :],
                                       start=(f == 0), stop=(f == HB - 1))
                    else:
                        half = whole_part(down_w[:, f, :])
                        pe.matmul(bank, act_hi[:, f, k * PT:k * PT + PT], half, start=(f == 0), stop=False)
                        mm = pe.matmul(bank, act_lo[:, f, k * PT:k * PT + PT], half, start=False, stop=(f == HB - 1))
                if f0 and k % 2:
                    mm.then_inc(down_ps, 1)

            for slot in range(SLOTS):
                if scan and slot < slots:
                    drive(slot)
                    if slot >= LAG:
                        read(slot - LAG)
                if down and slot < 8:
                    shrink(slot // 2, 3 * (slot % 2))
                if pre and image:
                    if 8 <= slot < 16:
                        turn(slot - 8)
                    if slot in EMBED:
                        n = EMBED.index(slot)
                        embed(n // 3, 2 * (n % 3))
                if ahead and slot in (20, 22):
                    average((20, 22).index(slot))
                if post:
                    if slot in (16, 17):
                        attend(slot - 16)
                    if slot in (28, 29):
                        turn_fx(slot - 28)
                    if slot in FFN_GATE:
                        ffn(FFN_GATE.index(slot), 0)
                    if slot in FFN_UP:
                        ffn(FFN_UP.index(slot), 1)
                if pre:
                    if slot == 38:
                        turn_xa()
                    if slot in (40, 41):
                        project(0, slot - 40)
                    if slot in (46, 47):
                        project(1, slot - 46)
                if scan and slot == slots - 1:
                    for late in range(slots - LAG, slots):
                        read(late)

        IMAGE = dict(image=True, ahead=True, pre=True, scan=True, post=True, down=True, steps=STEPS)
        TEXT = dict(IMAGE, image=False, ahead=False)
        AHEAD = dict(IMAGE, pre=False, scan=False, post=False, down=False)
        HEAD = [dict(IMAGE, scan=False, post=False, down=False), dict(IMAGE, post=False, down=False),
                dict(IMAGE, down=False)]
        LAST_IMAGE = dict(IMAGE, ahead=False)
        TAIL = [dict(TEXT, pre=False, steps=LAST_STEPS), dict(TEXT, pre=False, scan=False),
                dict(TEXT, pre=False, scan=False, post=False)]

        def bodies(eng, body, **how):
            for i, parts in enumerate(HEAD):
                body(eng, i, **parts, **how)
            with eng.Fori(len(HEAD), IMG_GROUPS - 1) as i:
                body(eng, i, **IMAGE, **how)
            body(eng, IMG_GROUPS - 1, **LAST_IMAGE, **how)
            with eng.Fori(IMG_GROUPS, GROUPS - 1) as i:
                body(eng, i, **TEXT, **how)
            body(eng, GROUPS - 1, **TEXT, **how)
            for n, parts in enumerate(TAIL):
                body(eng, GROUPS + n, **parts, **how)

        def sync_bodies(sp):
            for i, parts in enumerate(HEAD):
                sync_body(sp, i, **parts)
            with sp.Fori(len(HEAD), IMG_GROUPS - 1) as i:
                sync_body(sp, i, **IMAGE)
            sync_body(sp, IMG_GROUPS - 1, **LAST_IMAGE)
            with sp.Fori(IMG_GROUPS, GROUPS - 1) as i:
                sync_body(sp, i, **TEXT)
            sync_body(sp, GROUPS - 1, **TEXT, last_pre=True)
            for n, parts in enumerate(TAIL):
                sync_body(sp, GROUPS + n, **parts, last_down=n == len(TAIL) - 1)
            sp.wait_ge(stored, (GROUPS - 1) * 64 + 64 * 16)

        with nc.Block() as block:
            @block.sync
            def _(sp):
                setup_sync(sp)

            @block.vector
            def _(dve):
                setup_vector(dve)

            @block.scalar
            def _(sc):
                setup_scalar(sc)

            @block.gpsimd
            def _(gp):
                setup_gpsimd(gp)

            @block.tensor
            def _(pe):
                setup_tensor(pe)

        with nc.Block() as block:
            @block.sync
            def _(sp):
                sync_bodies(sp)

            @block.vector
            def _(dve):
                bodies(dve, vector_body)

            @block.scalar
            def _(sc):
                bodies(sc, scalar_body)

            @block.gpsimd
            def _(gp):
                bodies(gp, gpsimd_body)

            @block.tensor
            def _(pe):
                flag = pe.value_load(large_flag[:, :], min_val=0, max_val=1)
                with pe.If(flag > 0):
                    bodies(pe, tensor_body, general=True)
                with pe.Else():
                    bodies(pe, tensor_body, general=False)


def raw_rows(x, g):
    v = x.rearrange("b c (g y) w -> g c b (y w)", y=PATCH)
    return v[g]


_INS = ['x', 'txt', 'L0_tok_W', 'L0_tok_bias', 'L0_tok_ln1_g', 'L0_tok_ln1_b', 'L0_tok_ln2_g', 'L0_tok_ln2_b',
        'L0_attn_w_in', 'L0_attn_b_in', 'L0_attn_A', 'L0_attn_Bm', 'L0_attn_Cm', 'L0_attn_Dv', 'L0_attn_w_out',
        'L0_attn_b_out', 'L0_attn_g_norm', 'L0_ffn_w_gate', 'L0_ffn_w_up', 'L0_ffn_w_down']


def kernel(**inputs):
    import concourse.bacc as _bacc
    from concourse.bass_utils import run_bass_kernel_spmd as _run

    nc = _bacc.Bacc("TRN2", target_bir_lowering=False, num_devices=1)
    arrays, args = {}, []
    for name in _INS:
        a = np.ascontiguousarray(inputs[name])
        arrays[f"in_{name}"] = a
        args.append(nc.dram_tensor(f"in_{name}", a.shape, mybir.dt.from_np(a.dtype), kind="ExternalInput").ap())
    table = constant_table()
    arrays["constants"] = table
    args.append(nc.dram_tensor("constants", table.shape, FP32, kind="ExternalInput").ap())
    args.append(nc.dram_tensor("out", (B, L, D), FP32, kind="ExternalOutput").ap())
    build(nc, *args)
    r = _run(nc, [arrays], core_ids=[0])
    return r.results[0]["out"]
```

```python
import numpy as np
import concourse.bass as bass
from concourse import mybir
from contextlib import ExitStack

FP32 = mybir.dt.float32
FP16 = mybir.dt.float16
INT32 = mybir.dt.int32
BF16 = mybir.dt.bfloat16
ACT = mybir.ActivationFunctionType
ALU = mybir.AluOpType

B = 32
CH, IMG, PATCH = 3, 224, 16
ROW = IMG // PATCH
NTXT = 77
L = ROW * ROW + NTXT
D, S, HID = 256, 64, 768
DB = D // 128
HB = HID // 128
STEPS = ROW // 2
TOK = B * STEPS
PT = TOK // 2
IMG_GROUPS = ROW
GROUPS = -(-L // ROW)
LAST = L - (GROUPS - 1) * ROW
LAST_STEPS = (LAST + 1) // 2
EARLY = 4
CHUNKS = 8
DL = 16
CW = DL * B
SLOTS = STEPS * CHUNKS
LAG = 3
NU = 4
KF = CH * PATCH * PATCH // 128
RAWP = CH * B
X_SCALE, B_SCALE = 16.0, 64.0
U_SCALE = X_SCALE * B_SCALE
EPS = 1e-5
RMS_EPS = 1e-6
DEQUANT = 1.0 / 127.0
EXACT = 256.0
ACT_SCALE = 2.0 ** -6

C_ID, C_AVG, C_HI, C_LO, C_D0, C_D1, C_READ = 0, 128, 224, 225, 226, 227, 228
C_COLS = C_READ + STEPS * 2 * 32


def span(first, end):
    return tuple(range(first, end))


PLANS = {
    "image": dict(
        shrink=(3, 3, 4, 5, 6, 6, 8, 8), turn=(9, 10, 12, 12, 13, 14, 15, 16), attend=(16, 16), average=(23, 26),
        embed=(19, 20, 21, 22, 22, 23, 24, 27, 27, 28, 28, 32), turn_fx=(30, 33),
        ffn_gate=(35, 38, 42, 45, 48, 50), ffn_up=(37, 40, 43, 46, 49, 51), turn_xa=(39,),
        project=(41, 41, 43, 49), finish=(8, 11), raw_patch=(9, 9, 10, 11, 15, 15, 16, 17, 18, 19, 20, 21, 22, 23),
        raw_means=(23,), raw_deviation=(27,), raw_variance=(29,), attn_bias=(20,), res_stats=(24,),
        res_variance=(27,), res_shift=(29,), fx_low_part=(35, 36), tok_stats=(29, 35), tok_shift=(32, 42),
        ln_stats=(37,), ln_shift=(39,), raw_shift=(38,), x_low_part=(43,), silu=(52,),
        ffn_silu=(38, 42, 45, 48, 51, 53), ffn_product=(40, 42, 46, 49, 51, 53), y_copy=(0,),
        xT_copy=(10, 10, 11, 12, 13, 14, 15, 16), fx_apply=(25, 25, 27, 27), fxT_copy=(31, 33),
        tok_normalise=(31, 40), ln_apply=(38,), xaT_copy=(39,), x_copy=(41,), gate_copy=(49,),
        ffn_tanh=(36, 39, 43, 46, 49, 51), act_high_part=(41, 43, 47, 48, 53, 53),
        normalise=(43, 44, 46, 47, 50, 53, 54)),
    "text": dict(
        shrink=(1, 2, 3, 4, 5, 6, 7, 8), attend=(16, 16), turn_fx=(31, 31), ffn_gate=(35, 38, 41, 43, 47, 50),
        ffn_up=(36, 39, 42, 45, 48, 51), turn_xa=(15,), project=(17, 19, 34, 34), finish=(6, 12), attn_bias=(20,),
        res_stats=(23,), res_variance=(27,), res_shift=(28,), fx_low_part=(34, 37), ln_stats=(11,), ln_shift=(12,),
        x_low_part=(32,), silu=(38,), ffn_silu=(38, 41, 44, 48, 50, 53), ffn_product=(39, 42, 45, 49, 51, 54),
        y_copy=(0,), fx_apply=(28, 28, 29, 29), fxT_copy=(31, 31), ln_apply=(11,), xaT_copy=(16,), x_copy=(23,),
        gate_copy=(34,), ffn_tanh=(35, 38, 41, 44, 47, 50), act_high_part=(38, 41, 46, 49, 50, 54)),
    "last": dict(
        shrink=(1, 2, 3, 3, 5, 6, 8, 9), attend=(17, 17), turn_fx=(30, 30), ffn_gate=(33, 37, 40, 43, 46, 50),
        ffn_up=(35, 37, 41, 44, 47, 50), finish=(8, 13), attn_bias=(20,), res_stats=(26,), res_variance=(27,),
        res_shift=(28,), fx_low_part=(35, 35), ffn_silu=(38, 40, 44, 48, 51, 54),
        ffn_product=(39, 42, 45, 48, 51, 54), y_copy=(1,), fx_apply=(27, 27, 28, 28), fxT_copy=(30, 30),
        ffn_tanh=(35, 41, 41, 45, 48, 51), act_high_part=(41, 44, 47, 50, 52, 54)),
    "first": dict(
        turn=(0, 1, 2, 3, 4, 5, 6, 7), average=(14, 18), embed=(9, 10, 11, 12, 13, 14, 15, 16, 17, 18, 19, 20),
        turn_xa=(24,), project=(24, 24, 34, 35),
        raw_patch=(10, 10, 10, 10, 10, 10, 10, 10, 10, 10, 10, 10, 10, 10), raw_means=(10,), raw_deviation=(17,),
        raw_variance=(19,), tok_stats=(15, 22), tok_shift=(16, 23), ln_stats=(18,), ln_shift=(18,),
        raw_shift=(24,), x_low_part=(25,), silu=(35,), xT_copy=(1, 2, 3, 4, 5, 6, 8, 8), tok_normalise=(16, 24),
        ln_apply=(19,), xaT_copy=(22,), x_copy=(24,), gate_copy=(34,), normalise=(26, 26, 26, 26, 30, 30, 30),
        ffn_turn=(21, 21, 21, 26, 27, 28, 29, 30, 31, 32, 33), count_large=(43,), flag_large=(41,),
        ffn_even=(21, 22, 27, 29, 31, 33), ffn_odd=(22, 27, 29, 31, 33)),
    "second": dict(
        turn=(5, 5, 6, 7, 8, 9, 10, 11), average=(25, 27), embed=(12, 13, 14, 15, 17, 17, 18, 19, 20, 21, 22, 23),
        turn_xa=(32,), project=(34, 34, 40, 44), raw_patch=(8, 9, 10, 11, 12, 13, 13, 14, 15, 16, 17, 18, 19, 20),
        raw_means=(23,), raw_deviation=(29,), raw_variance=(30,), tok_stats=(21, 27), tok_shift=(23, 31),
        ln_stats=(29,), ln_shift=(32,), raw_shift=(34,), x_low_part=(40,), silu=(46,),
        xT_copy=(5, 6, 7, 8, 9, 10, 11, 12), tok_normalise=(21, 30), ln_apply=(31,), xaT_copy=(32,), x_copy=(35,),
        gate_copy=(42,), normalise=(36, 40, 42, 43, 47, 49, 51)),
}

POOL_ORDER = {
    "image": (
        ("gating", 0), ("residual", 0), ("res_rsqrt", 0), ("token_rsqrt", 0), ("raw_rsqrt", 0), ("token_tiles", 0),
        ("token_rsqrt", 1), ("ln_rsqrt", 0), ("token_tiles", 1), ("act_low_part", 0), ("act_low_part", 1),
        ("normalise", 0), ("act_low_part", 2), ("skip_term", 0), ("normalise", 1), ("normalise", 2),
        ("normalise", 3), ("normalise", 4), ("act_low_part", 3), ("act_low_part", 4), ("normalise", 5),
        ("normalise", 6), ("act_low_part", 5)),
    "text": (
        ("ln_rsqrt", 0), ("gating", 0), ("residual", 0), ("res_rsqrt", 0), ("skip_term", 0), ("act_low_part", 0),
        ("act_low_part", 1), ("act_low_part", 2), ("act_low_part", 3), ("act_low_part", 4), ("act_low_part", 5)),
    "last": (
        ("gating", 0), ("residual", 0), ("res_rsqrt", 0), ("skip_term", 0), ("act_low_part", 0),
        ("act_low_part", 1), ("act_low_part", 2), ("act_low_part", 3), ("act_low_part", 4), ("act_low_part", 5)),
    "first": (
        ("token_rsqrt", 0), ("token_tiles", 0), ("ln_rsqrt", 0), ("token_rsqrt", 1), ("raw_rsqrt", 0),
        ("token_tiles", 1), ("normalise", 0), ("normalise", 1), ("normalise", 2), ("normalise", 3),
        ("normalise", 4), ("normalise", 5), ("normalise", 6), ("skip_term", 0)),
    "second": (
        ("token_rsqrt", 0), ("token_tiles", 0), ("ln_rsqrt", 0), ("token_rsqrt", 1), ("raw_rsqrt", 0),
        ("token_tiles", 1), ("normalise", 0), ("normalise", 1), ("normalise", 2), ("normalise", 3),
        ("normalise", 4), ("normalise", 5), ("skip_term", 0), ("normalise", 6)),
}


def kind_of(i, image, pre):
    if isinstance(i, int) and i == 0:
        return "first"
    if isinstance(i, int) and i == 1:
        return "second"
    return "image" if image else "text" if pre else "last"


def parts_at(plan, name, slot):
    return [n for n, at in enumerate(plan.get(name, ())) if at == slot]


def constant_table():
    t = np.zeros((128, C_COLS), np.float32)
    p = np.arange(128)
    t[:, C_ID:C_ID + 128] = np.eye(128)
    for a in range(RAWP):
        for c in range(CH):
            t[a, C_AVG + c * B + a % B] = 1.0 / CH
    t[:, C_HI] = (p // 2) % 2 == 0
    t[:, C_LO] = (p // 2) % 2 == 1
    t[:, C_D0] = (p // 4) % 2 == 0
    t[:, C_D1] = (p // 4) % 2 == 1
    for tau in range(STEPS):
        for k in range(2):
            t[p, C_READ + (tau * 2 + k) * 32 + 4 * tau + 2 * (p // S) + k] = 1.0
    return t


def build(nc, x, txt, W, tok_bias, ln1_g, ln1_b, ln2_g, ln2_b, w_in, b_in, A, Bm, Cm, Dv, w_out, b_out,
          g_norm, w_gate, w_up, w_down, consts, out):
    scan_scr = nc.dram_tensor("scan_scr", [D, 4, TOK], FP16).ap()
    gate_scr = nc.dram_tensor("gate_scr", [GROUPS, 128, 2, DB * TOK], FP32).ap()
    tok_scr = nc.dram_tensor("tok_scr", [GROUPS, PT, 4, D], FP32).ap()
    y_scr = nc.dram_tensor("y_scr", [4, DL, STEPS, 2, DB * B], FP32).ap()

    ctx = ExitStack()
    with ctx:
        def sb(name, shape, dt=FP32):
            return ctx.enter_context(nc.sbuf_tensor(name, shape, dt))

        def sem(name):
            return ctx.enter_context(nc.semaphore(name))

        cst = sb("cst", [128, C_COLS])
        ident = cst[:, C_ID:C_ID + 128]
        tok_w = sb("tok_w", [128, KF, D])
        in_w = sb("in_w", [128, DB, 2 * D])
        out_w = sb("out_w", [128, DB, D])
        gate_w = sb("gate_w", [128, DB, HID])
        up_w = sb("up_w", [128, DB, HID])
        down_w = sb("down_w", [128, HB, D])
        large = sb("large", [128, 8])
        large_flag = sb("large_flag", [1, 1], INT32)
        rows = sb("rows", [PT, 4, D])
        cols = sb("cols", [128, 4 * DB])
        a_col = sb("a_col", [128, CHUNKS * DL])
        b_st = sb("b_st", [128, CHUNKS, 2 * S], FP16)
        read_st = sb("read_st", [128, STEPS, 2, 32])
        half_th = sb("half_th", [128, 1])

        h = sb("h", [128, CHUNKS, CW])
        x_diag = sb("x_diag", [128, CHUNKS, DL, TOK], FP16)
        y_fx = sb("y_fx", [128, 2 * CW])
        y_sb = y_fx[:, 0:CW]

        raw = sb("raw", [RAWP, PATCH, ROW, PATCH])
        rawn = sb("rawn", [RAWP, ROW, PATCH * PATCH])
        raw_st = sb("raw_st", [RAWP, ROW, 6])
        raw_mv = sb("raw_mv", [RAWP, ROW, 2])
        raw_s = sb("raw_s", [RAWP, 7, ROW])
        xT_act = sb("xT_act", [128, KF * 2 * TOK])
        xT = xT_act[:, :].rearrange("p (f a t) -> p f a t", f=KF, a=2)
        act_hi, act_lo = (xT_act[:, n * HB * 2 * PT:(n + 1) * HB * 2 * PT].bitcast(FP16)
                          .rearrange("p (k t) -> p k t", k=HB) for n in range(2))
        tok = sb("tok", [PT, 4, D])
        tok_st = sb("tok_st", [PT, 4, 6])
        tok_mv = sb("tok_mv", [PT, 4, 2])
        tok_s = sb("tok_s", [PT, 3, 4])
        ln_st = sb("ln_st", [PT, 2, 6])
        ln_mv = sb("ln_mv", [PT, 2, 2])
        ln_s = sb("ln_s", [PT, 3, 2])
        xa = sb("xa", [PT, 2, D])
        xaT = sb("xaT", [128, DB, TOK])
        xf = sb("xf", [128, DB, TOK])
        x_hi = sb("x_hi", [128, DB, TOK], FP16)
        x_lo = sb("x_lo", [128, DB, TOK], FP16)
        gf = sb("gf", [128, DB, TOK])
        gth = sb("gth", [128, DB, TOK])
        gate_o = sb("gate_o", [128, 2, DB, TOK])

        yT = sb("yT", [128, STEPS, DB, B])
        gate_fx = sb("gate_fx", [128, 2 * DB * TOK])
        gate_i = gate_fx[:, :].rearrange("p (a k t) -> p a k t", a=2, k=DB)
        fx_hi, fx_lo = (gate_fx[:, n * DB * TOK:(n + 1) * DB * TOK].bitcast(FP16)
                        .rearrange("p (j t) -> p j t", j=DB) for n in range(2))
        zT = sb("zT", [128, DB, TOK])
        attn = sb("attn", [PT, 2, D])
        res = sb("res", [PT, 4, D])
        res_st = sb("res_st", [PT, 4, 6])
        res_mv = sb("res_mv", [PT, 4, 2])
        res_s = sb("res_s", [PT, 3, 4])
        fx = y_fx[0:PT, :].rearrange("p (k d) -> p k d", k=4)
        fxT = sb("fxT", [128, DB, 4 * PT])
        fth = sb("fth", [128, 4 * PT])
        fsg = sb("fsg", [128, 4 * PT])
        act = sb("act", [128, HB, 4 * PT])

        U = [ctx.enter_context(nc.psum_tensor(f"U{n}", [128, CW], FP32)) for n in range(NU)]
        Y = ctx.enter_context(nc.psum_tensor("Y", [128, CW], FP32))
        P = [ctx.enter_context(nc.psum_tensor(f"P{n}", [128, 512], FP32)) for n in range(3)]

        stage = x_diag[:, :, :, :].rearrange("p c l t -> p (c l t)").bitcast(FP32)
        STAGED = 4608
        WORDS = CHUNKS * DL * TOK // 2

        def staged(at, n):
            return stage[:, at:at + n]

        w_in_r = staged(0, 4 * D).rearrange("p (k d) -> p k d", k=4)
        w_out_r = staged(1024, 2 * D).rearrange("p (k d) -> p k d", k=2)
        a_r = staged(1536, 2 * S)
        c_r = staged(1664, 2 * S)
        b_r = staged(1792, CHUNKS * S).rearrange("p (c s) -> p c s", c=CHUNKS)
        b_d = staged(2304, CHUNKS * S).rearrange("p (c s) -> p c s", c=CHUNKS)
        b_t = staged(2816, CHUNKS * S).rearrange("p (c s) -> p c s", c=CHUNKS)
        b_h = staged(3328, CHUNKS * S // 2).bitcast(FP16).rearrange("p (c s) -> p c s", c=CHUNKS)
        g1 = staged(3584, KF)
        b1 = staged(3592, KF)
        ones = staged(3600, 128)
        b1_rep = staged(3728, KF * PT).rearrange("p (k t) -> p k t", k=KF)
        c_dup = staged(4400, 2 * S)
        c_sum = staged(4528, 1)
        act_w = act[:, :, :].rearrange("p k t -> p (k t)")
        ffn_r = [(act_w[:, 0:6 * D], w_gate, 0, 6), (act_w[:, 6 * D:10 * D], w_up, 0, 4), (gate_fx[:, 0:2 * D], w_up, 4, 2),
                 (y_fx[:, 0:HID], w_down, 0, 1), (fxT[:, :, :].rearrange("p j t -> p (j t)")[:, 0:HID], w_down, 1, 1)]

        def ffn_block(w, k, j):
            for where, m, k0, n in ffn_r:
                if m is w and k0 <= k < k0 + n:
                    at = (k - k0) * w.shape[1] + j * 128
                    return where[:, at:at + 128]

        s_cst = sem("s_cst")
        s_ld = sem("s_ld")
        s_int = sem("s_int")
        s_half = sem("s_half")
        s_rep = sem("s_rep")
        s_flt = sem("s_flt")
        s_max = sem("s_max")
        s_flag = sem("s_flag")
        s_ffn_tr = sem("s_ffn_tr")
        s_ffn_even = sem("s_ffn_even")
        s_ffn_odd = sem("s_ffn_odd")
        s_free = sem("s_free")
        s_row = sem("s_row")
        s_sum = sem("s_sum")
        s_own = sem("s_own")
        s_bias = sem("s_bias")
        s_csum = sem("s_csum")
        s_large = sem("s_large")
        s_tr = sem("s_tr")
        s_ev = sem("s_ev")
        s_zero = sem("s_zero")
        s_bits = sem("s_bits")
        raw_in = sem("raw_in")

        turns = []
        for j in range(DB):
            turns.append(([w_in_r[:, k, j * 128:j * 128 + 128] for k in range(4)], in_w[:, j, :], cols[:, 6 + j:7 + j]))
            turns.append(([w_out_r[:, k, j * 128:j * 128 + 128] for k in range(2)], out_w[:, j, :], 0.5))
        turns.append(([a_r], a_col[:, :], U_SCALE))
        ffn_turns = []
        for w, dst in ((w_gate, gate_w), (w_up, up_w)):
            for j in range(DB):
                for k0, k1 in ((0, 4), (4, HB)):
                    ffn_turns.append(([ffn_block(w, k, j) for k in range(k0, k1)], dst[:, j, k0 * 128:k1 * 128]))
        for j in range(0, HB, 2):
            ffn_turns.append(([ffn_block(w_down, k, jj) for jj in (j, j + 1) for k in range(DB)],
                              down_w[:, j:j + 2, :].rearrange("p j d -> p (j d)")))

        def setup_sync(sp):
            def load(dst, src, **slow):
                sp.dma_start(dst, src, **slow).then_inc(s_ld, 16)

            sp.dma_start(raw[:, :, :, :], raw_rows(x, 0)).then_inc(raw_in, 16)
            sp.dma_start(cst[:, :], consts).then_inc(s_cst, 16)
            load(tok_w[:, :, :], W.rearrange("(h k c) e -> k h c e", h=2, c=CH))
            load(g1, ln1_g.rearrange("(h k c) -> k h c", h=2, c=CH))
            load(b1, ln1_b.rearrange("(h k c) -> k h c", h=2, c=CH))
            load(w_in_r, w_in.rearrange("(k p) d -> p k d", p=128))
            load(w_out_r, w_out.rearrange("(k p) d -> p k d", p=128))
            load(a_r, A.rearrange("(p two) s -> p (two s)", two=2))
            load(c_r, Cm.rearrange("(p two) s -> p (two s)", two=2))
            for q in range(4):
                load(b_r[q:128:4, :, :], Bm.rearrange("(c r) s -> r c s", c=CHUNKS))
            for n, v in enumerate((tok_bias, ln2_g, ln2_b, b_out)):
                load(rows[:, n, :], v.rearrange("(a d) -> a d", a=1).to_broadcast([PT, D]))
            load(cols[:, 0:4], b_in.rearrange("(k p) -> p k", p=128), allow_slow_non_contiguous=True)
            load(cols[:, 4:6], Dv.rearrange("(k p) -> p k", p=128), allow_slow_non_contiguous=True)
            load(cols[:, 6:8], g_norm.rearrange("(k p) -> p k", p=128), allow_slow_non_contiguous=True)
            for where, w, k0, n in ffn_r:
                sp.dma_start(where.bitcast(INT32).rearrange("p (k d) -> p k d", k=n),
                             w.rearrange("(k p) d -> p k d", p=128)[:, k0:k0 + n, :]).then_inc(s_int, 16)

        LOADS = 7 + 4 + 4 + 3

        def setup_vector(dve):
            count = [0]

            def own(ins):
                count[0] += 1
                ins.then_inc(s_own, 1)

            dve.memset(half_th[:, :], -0.5).then_inc(s_half, 1)
            vector_body(dve, -1, **AHEAD)
            dve.wait_ge(s_cst, 16)
            dve.wait_ge(s_ld, 16 * LOADS)
            own(dve.memset(ones, 1.0))
            own(dve.tensor_scalar(b_h, b_r, B_SCALE, None, ALU.mult))
            own(dve.tensor_tensor(c_dup[:, 0:S], c_r[:, 0:S], c_r[:, S:2 * S], ALU.add))
            own(dve.tensor_tensor(c_dup[:, S:2 * S], c_r[:, 0:S], c_r[:, S:2 * S], ALU.add))
            dve.wait_ge(s_own, count[0])
            for f in range(KF):
                last = dve.tensor_scalar(b1_rep[:, f, :], ones[:, 0:PT], b1[:, f:f + 1], None, ALU.mult)
            last.then_inc(s_rep, 1)
            own(dve.scalar_tensor_tensor(b_d, b_r, B_SCALE, b_h, ALU.mult, ALU.subtract))
            own(dve.tensor_scalar(b_t, b_h, cst[:, C_HI:C_HI + 1], None, ALU.mult))
            dve.wait_ge(s_own, count[0])
            own(dve.scalar_tensor_tensor(b_d, b_d, cst[:, C_LO:C_LO + 1], b_t, ALU.mult, ALU.add))
            dve.wait_ge(s_own, count[0])
            for d2, c in ((0, C_D0), (1, C_D1)):
                own(dve.tensor_scalar(b_st[:, :, d2 * S:d2 * S + S], b_d, cst[:, c:c + 1], None, ALU.mult))
            dve.wait_ge(s_bias, 1)
            dve.tensor_tensor(rows[:, 0, :], P[2][0:PT, 0:D], rows[:, 0, :], ALU.add).then_inc(s_row, 1)
            for f in range(KF):
                own(dve.tensor_scalar(tok_w[:, f, :], tok_w[:, f, :], g1[:, f:f + 1], None, ALU.mult))
            dve.wait_ge(s_csum, 1)
            dve.tensor_copy(c_sum, P[2][:, 0:1]).then_inc(s_sum, 1)
            dve.wait_ge(s_sum, 1)
            own(dve.tensor_scalar(read_st[:, :, :, :], cst[:, C_READ:C_COLS].rearrange("p (t k m) -> p t k m", k=2, m=32),
                                  c_sum, None, ALU.mult))
            dve.wait_ge(s_own, count[0])
            dve.wait_ge(s_ev, len(turns))
            dve.sem_inc(s_free, 1)
            dve.memset(stage[:, 0:STAGED // 2].bitcast(INT32), 0)

        def setup_gpsimd(gp):
            gp.memset(h[:, :, :].rearrange("p c n -> p (c n)").bitcast(INT32), 0).then_inc(s_zero, 1)
            gp.memset(stage[:, STAGED:WORDS].bitcast(INT32), 0)
            gp.wait_ge(s_half, 1)
            gpsimd_body(gp, -1, **AHEAD)
            gp.wait_ge(s_free, 1)
            gp.memset(stage[:, STAGED // 2:STAGED].bitcast(INT32), 0)

        def setup_tensor(pe):
            pe.wait_ge(s_cst, 16)
            pe.wait_ge(s_zero, 1)
            for n in range(NU - 1):
                pe.matmul(U[n][:, :], ident, h[:, 0, :], start=True, stop=True).then_inc(s_bits, 1)
            tensor_body(pe, -1, general=False, **AHEAD)
            pe.wait_ge(s_rep, 1)
            for f in range(KF):
                mm = pe.matmul(P[2][0:PT, 0:D], b1_rep[:, f, :], tok_w[:, f, :], start=(f == 0), stop=(f == KF - 1))
            mm.then_inc(s_bias, 1)
            pe.wait_ge(s_row, 1)
            pe.matmul(P[2][:, 0:1], c_dup, ones[:, 0:1], start=True, stop=True).then_inc(s_csum, 1)
            for n, (blocks, _, _) in enumerate(turns):
                if n == 0:
                    pe.wait_ge(raw_small, 5)
                if n >= 2:
                    pe.wait_ge(s_ev, n - 1)
                for k, src in enumerate(blocks):
                    mm = pe.transpose(P[n % 2][:, k * 128:k * 128 + 128], src, ident)
                mm.then_inc(s_tr, 1)

        def ffn_setup_vector(dve):
            for n, (where, _, _, _) in enumerate(ffn_r):
                dve.wait_ge(s_int, 16 * len(ffn_r))
                dve.tensor_copy(where, where.bitcast(INT32)).then_inc(s_flt, 1)
            for n, (where, _, _, _) in enumerate(ffn_r):
                dve.wait_ge(s_flt, n + 1)
                dve.tensor_reduce(large[:, n:n + 1], where, mybir.AxisListType.X, ALU.max,
                                  apply_absolute_value=True).then_inc(s_max, 1)
            dve.memset(large[:, 7:8], 1.0).then_inc(s_max, 1)
            dve.wait_ge(s_max, len(ffn_r))
            dve.tensor_reduce(large[:, 5:6], large[:, 0:len(ffn_r)], mybir.AxisListType.X, ALU.max).then_inc(s_max, 1)
            dve.wait_ge(s_max, len(ffn_r) + 2)
            dve.tensor_scalar(large[:, 6:7], large[:, 5:6], EXACT, None, ALU.is_gt).then_inc(s_max, 1)

        def ffn_turn(pe, n):
            blocks, _ = ffn_turns[n]
            if n == 0:
                pe.wait_ge(s_flt, len(ffn_r))
            if n >= 2 and n % 2 == 0:
                pe.wait_ge(s_ffn_even, n // 2)
            if n >= 2 and n % 2 == 1:
                pe.wait_ge(s_ffn_odd, n // 2)
            for k, src in enumerate(blocks):
                mm = pe.transpose((Y, U[NU - 1])[n % 2][:, k * 128:k * 128 + 128], src, ident)
            mm.then_inc(s_ffn_tr, 1)

        def ffn_even(sc, n):
            blocks, dst = ffn_turns[2 * n]
            sc.wait_ge(s_ffn_tr, 2 * n + 1)
            sc.activation(dst, Y[:, 0:128 * len(blocks)], ACT.Copy).then_inc(s_ffn_even, 1)

        def ffn_odd(dve, n):
            blocks, dst = ffn_turns[2 * n + 1]
            dve.wait_ge(s_ffn_tr, 2 * n + 2)
            dve.tensor_copy(dst, U[NU - 1][:, 0:128 * len(blocks)]).then_inc(s_ffn_odd, 1)

        def count_large(pe):
            pe.wait_ge(s_max, len(ffn_r) + 3)
            pe.wait_ge(s_ffn_even, (len(ffn_turns) + 1) // 2)
            pe.matmul(Y[0:1, 0:1], large[:, 6:7], large[:, 7:8], start=True, stop=True).then_inc(s_large, 1)
            pe.wait_ge(s_ffn_odd, len(ffn_turns) // 2)
            pe.matmul(U[NU - 1][:, :], ident, h[:, 0, :], start=True, stop=True).then_inc(s_bits, 1)

        def flag_large(dve):
            dve.wait_ge(s_large, 1)
            dve.tensor_scalar(large_flag[:, :], Y[0:1, 0:1], 0.5, None, ALU.is_gt).then_inc(s_flag, 1)

        def setup_scalar(sc):
            scalar_body(sc, -1, **AHEAD)
            for n, (blocks, dst, scale) in enumerate(turns):
                sc.wait_ge(s_tr, n + 1)
                sc.activation(dst, P[n % 2][:, 0:128 * len(blocks)], ACT.Copy, scale=scale).then_inc(s_ev, 1)

        raw_stats = sem("raw_stats")
        raw_aggr = sem("raw_aggr")
        avg_ps = sem("avg_ps")
        raw_small = sem("raw_small")
        raw_rstd = sem("raw_rstd")
        norm_even = sem("norm_even")
        norm_odd = sem("norm_odd")
        turned_ps = sem("turned_ps")
        xT_done = sem("xT_done")
        tok_ps = sem("tok_ps")
        tok_small = sem("tok_small")
        tok_rstd = sem("tok_rstd")
        tok_norm = sem("tok_norm")
        tok_g = sem("tok_g")
        tok_done = sem("tok_done")
        txt_in = sem("txt_in")
        ln_small = sem("ln_small")
        ln_rstd = sem("ln_rstd")
        xa_done = sem("xa_done")
        xa_ps = sem("xa_ps")
        xaT_done = sem("xaT_done")
        proj_ps = sem("proj_ps")
        xf_done = sem("xf_done")
        x_hi_done = sem("x_hi_done")
        x_lo_done = sem("x_lo_done")
        gf_done = sem("gf_done")
        gth_done = sem("gth_done")
        gate_done = sem("gate_done")
        scan_wr = sem("scan_wr")
        gate_wr = sem("gate_wr")
        tok_wr = sem("tok_wr")
        diag_early = sem("diag_early")
        diag_late = sem("diag_late")
        grown = sem("grown")
        driven = sem("driven")
        squashed = sem("squashed")
        y_ps = sem("y_ps")
        y_out = sem("y_out")
        y_wr = sem("y_wr")
        y_ld = sem("y_ld")
        gate_ld = sem("gate_ld")
        res_ld = sem("res_ld")
        z_sum = sem("z_sum")
        z_done = sem("z_done")
        attn_ps = sem("attn_ps")
        attn_done = sem("attn_done")
        res_done = sem("res_done")
        res_small = sem("res_small")
        res_rstd = sem("res_rstd")
        fx_done = sem("fx_done")
        fx_ps = sem("fx_ps")
        fxT_done = sem("fxT_done")
        fx_lo_done = sem("fx_lo_done")
        ffn_g_ps = sem("ffn_g_ps")
        ffn_u_ps = sem("ffn_u_ps")
        fth_done = sem("fth_done")
        fsg_done = sem("fsg_done")
        act_done = sem("act_done")
        act_hi_done = sem("act_hi_done")
        act_lo_done = sem("act_lo_done")
        down_ps = sem("down_ps")
        out_done = sem("out_done")
        stored = sem("stored")
        passed = sem("passed")

        def due(count):
            return not (isinstance(count, int) and count <= 0)

        def bank_of(slot):
            return slot % NU

        def bank_user(slot):
            if slot >= NU:
                return slot - NU
            return max(n for n in range(SLOTS) if bank_of(n) == bank_of(slot)) - SLOTS

        def halves(t):
            return t.rearrange("b (t two) d -> two b t d", two=2)

        def sync_body(sp, i, image, ahead, pre, scan, post, down, steps, last_pre=False, last_down=False):
            r, g, s, q, d = i + 1, i, i - 1, i - 2, i - 3
            if ahead:
                sp.wait_ge(norm_even, r * STEPS)
                sp.sem_inc(passed, 1)
                sp.wait_ge(norm_odd, r * STEPS)
                sp.sem_inc(passed, 1)
                sp.dma_start(raw[:, :, :, :], raw_rows(x, r)).then_inc(raw_in, 16)
            if post:
                sp.wait_ge(y_out, q + 1)
                sp.sem_inc(passed, 1)
                if due(q * 32):
                    sp.wait_ge(y_ld, q * 32)
                    sp.sem_inc(passed, 1)
                for c4 in range(4):
                    sp.dma_start(y_scr[c4].rearrange("l t two (k b) -> (t two k) l b", b=B),
                                 y_sb[c4 * 32:c4 * 32 + 4 * STEPS, :].rearrange("p (l b) -> p l b", b=B)).then_inc(y_wr, 16)
                sp.wait_ge(gate_wr, (q + 1) * 16)
                sp.sem_inc(passed, 1)
                if due(q * HB):
                    sp.wait_ge(ffn_u_ps, q * HB)
                    sp.sem_inc(passed, 1)
                sp.dma_start(gate_fx[:, :].rearrange("p (a n) -> p a n", a=2), gate_scr[q]).then_inc(gate_ld, 16)
            if pre and not image:
                sp.wait_ge(tok_wr, g * 16)
                sp.sem_inc(passed, 1)
                sp.wait_ge(xa_done, g * 2)
                sp.sem_inc(passed, 1)
                t0 = (g - IMG_GROUPS) * ROW
                if last_pre:
                    for n in range(LAST):
                        for hf in range(2):
                            sp.dma_start(tok[n // 2:n // 2 + 15 * STEPS + 1:STEPS, (n % 2) * 2 + hf, :],
                                         txt[hf * 16:hf * 16 + 16, t0 + n, :]).then_inc(txt_in, 16)
                else:
                    src = halves(txt[:, bass.ds(t0, ROW), :])
                    for par in range(2):
                        for hf in range(2):
                            sp.dma_start(tok[:, par * 2 + hf, :], src[par][hf * 16:hf * 16 + 16]).then_inc(txt_in, 16)
            if post:
                sp.wait_ge(y_wr, (q + 1) * 64)
                sp.sem_inc(passed, 1)
                for d2 in range(2):
                    sp.dma_start(yT[d2:127 + d2:2, :, :, :].rearrange("p t k b -> p t (k b)"),
                                 y_scr[:, :, :, d2, :].rearrange("c l t n -> (c l) t n")).then_inc(y_ld, 16)
            if down:
                for pair in range(2):
                    sp.wait_ge(out_done, d * 2 + pair + 1)
                    sp.sem_inc(passed, 1)
                    for hf in range(2):
                        k = pair * 2 + hf
                        if last_down:
                            for n in range(pair, LAST, 2):
                                sp.dma_start(out[hf * 16:hf * 16 + 16, d * ROW + n, :],
                                             res[n // 2:n // 2 + 15 * STEPS + 1:STEPS, k, :]).then_inc(stored, 16)
                        else:
                            dst = halves(out[:, bass.ds(d * ROW, ROW), :])
                            sp.dma_start(dst[pair][hf * 16:hf * 16 + 16], res[:, k, :]).then_inc(stored, 16)
            if post:
                if due(q * 64):
                    sp.wait_ge(stored, q * 64)
                    sp.sem_inc(passed, 1)
                sp.wait_ge(tok_wr, (q + 1) * 16)
                sp.sem_inc(passed, 1)
                sp.dma_start(res[:, :, :], tok_scr[q]).then_inc(res_ld, 16)
            if scan and steps > EARLY:
                sp.wait_ge(scan_wr, (s + 1) * 64)
                sp.sem_inc(passed, 1)
                if due(s * SLOTS):
                    sp.wait_ge(driven, s * SLOTS)
                    sp.sem_inc(passed, 1)
                load_diag(sp, EARLY, STEPS, diag_late)
            if pre:
                if image:
                    sp.wait_ge(tok_done, (g + 1) * 2)
                    sp.sem_inc(passed, 1)
                elif last_pre:
                    sp.wait_ge(txt_in, (g - IMG_GROUPS) * 64 + LAST * 2 * 16)
                    sp.sem_inc(passed, 1)
                else:
                    sp.wait_ge(txt_in, (g - IMG_GROUPS + 1) * 64)
                    sp.sem_inc(passed, 1)
                sp.dma_start(tok_scr[g], tok[:, :, :]).then_inc(tok_wr, 16)
                if due(g * 256):
                    sp.wait_ge(diag_early, g * 256)
                    sp.sem_inc(passed, 1)
                    sp.wait_ge(diag_late, g * 256)
                    sp.sem_inc(passed, 1)
                for xpart, (part, done) in enumerate(((x_hi, x_hi_done), (x_lo, x_lo_done))):
                    sp.wait_ge(done, g + 1)
                    sp.sem_inc(passed, 1)
                    for bpart in range(2):
                        sp.dma_start(scan_scr.rearrange("(k p) r t -> r p k t", k=DB)[bpart * 2 + xpart],
                                     part[:, :, :]).then_inc(scan_wr, 16)
                sp.wait_ge(scan_wr, (g + 1) * 64)
                sp.sem_inc(passed, 1)
                if scan:
                    sp.wait_ge(driven, s * SLOTS + EARLY * CHUNKS)
                    sp.sem_inc(passed, 1)
                load_diag(sp, 0, EARLY, diag_early)
                sp.wait_ge(gate_done, (g + 1) * 3)
                sp.sem_inc(passed, 1)
                sp.dma_start(gate_scr[g], gate_o[:, :, :, :].rearrange("p a k t -> p a (k t)")).then_inc(gate_wr, 16)

        def load_diag(sp, t0, t1, done):
            for l in range(DL):
                sp.dma_start(x_diag[l * 8:l * 8 + 8, :, l, t0 * B:t1 * B],
                             scan_scr.rearrange("(c l two) r t -> l (two r) c t", c=CHUNKS, two=2)[l][:, :, t0 * B:t1 * B])\
                    .then_inc(done, 16)

        def vector_body(dve, i, image, ahead, pre, scan, post, down, steps):
            r, g, s, q, d = i + 1, i, i - 1, i - 2, i - 3
            plan = PLANS[kind_of(i, image, pre)]

            def grow(slot):
                t, c = divmod(slot, CHUNKS)
                if due(s * SLOTS + bank_user(slot) + 1):
                    dve.wait_ge(squashed, s * SLOTS + bank_user(slot) + 1)
                dve.tensor_tensor(U[bank_of(slot)][:, :].rearrange("p (l b) -> p l b", b=B),
                                  h[:, c, :].rearrange("p (l b) -> p l b", b=B),
                                  a_col[:, c * DL:c * DL + DL].unsqueeze(2).to_broadcast([128, DL, B]),
                                  ALU.mult).then_inc(grown, 1)

            def raw_patch(w):
                dve.wait_ge(raw_in, (r + 1) * 16)
                dve.bn_stats(raw_st[:, w, :], raw[:, :, w, :]).then_inc(raw_stats, 1)

            def raw_means():
                dve.wait_ge(raw_stats, (r + 1) * ROW)
                dve.sem_inc(passed, 1)
                for w in range(ROW):
                    dve.bn_aggr(raw_mv[:, w, :], raw_st[:, w, :]).then_inc(raw_aggr, 1)

            def raw_deviation():
                dve.wait_ge(avg_ps, r * 2 + 1)
                dve.tensor_copy(raw_s[:, 0, :], P[0][0:RAWP, 0:ROW]).then_inc(raw_small, 1)
                dve.wait_ge(raw_small, r * 6 + 1)
                dve.tensor_tensor(raw_s[:, 1, :], raw_mv[:, :, 0], raw_s[:, 0, :], ALU.subtract).then_inc(raw_small, 1)
                dve.wait_ge(raw_small, r * 6 + 2)
                dve.tensor_tensor(raw_s[:, 2, :], raw_s[:, 1, :], raw_s[:, 1, :], ALU.mult).then_inc(raw_small, 1)
                dve.wait_ge(raw_small, r * 6 + 3)
                dve.tensor_tensor(raw_s[:, 3, :], raw_mv[:, :, 1], raw_s[:, 2, :], ALU.add).then_inc(raw_small, 1)

            def raw_variance():
                dve.wait_ge(avg_ps, r * 2 + 2)
                dve.tensor_scalar(raw_s[:, 4, :], P[0][0:RAWP, 0:ROW], EPS, None, ALU.add).then_inc(raw_small, 1)

            def raw_shift():
                dve.wait_ge(raw_rstd, r + 1)
                dve.scalar_tensor_tensor(raw_s[:, 6, :], raw_s[:, 0, :], -1.0, raw_s[:, 5, :], ALU.mult, ALU.mult)\
                    .then_inc(raw_small, 1)

            def tok_stats(pair):
                n = g * 16 + pair * 8
                dve.wait_ge(tok_ps, g * 2 + pair + 1)
                if pair == 0:
                    if due(g * 16):
                        dve.wait_ge(tok_wr, g * 16)
                for k in range(2):
                    dve.tensor_tensor(tok[:, pair * 2 + k, :], P[2 - pair][0:PT, k * D:k * D + D], rows[:, 0, :], ALU.add)\
                        .then_inc(tok_small, 1)
                for k in range(2):
                    dve.wait_ge(tok_small, n + 1 + k)
                    dve.bn_stats(tok_st[:, pair * 2 + k, :], tok[:, pair * 2 + k, :]).then_inc(tok_small, 1)
                dve.wait_ge(tok_small, n + 4)
                dve.sem_inc(passed, 1)
                for k in range(2):
                    dve.bn_aggr(tok_mv[:, pair * 2 + k, :], tok_st[:, pair * 2 + k, :]).then_inc(tok_small, 1)
                dve.wait_ge(tok_small, n + 6)
                dve.tensor_scalar(tok_s[:, 0, pair * 2:pair * 2 + 2], tok_mv[:, pair * 2:pair * 2 + 2, 1], EPS, None,
                                  ALU.add).then_inc(tok_small, 1)

            def tok_shift(pair):
                dve.wait_ge(tok_rstd, g * 2 + pair + 1)
                dve.scalar_tensor_tensor(tok_s[:, 2, pair * 2:pair * 2 + 2], tok_mv[:, pair * 2:pair * 2 + 2, 0], -1.0,
                                         tok_s[:, 1, pair * 2:pair * 2 + 2], ALU.mult, ALU.mult).then_inc(tok_small, 1)

            def ln_stats():
                if image:
                    dve.wait_ge(tok_done, g * 2 + 1)
                else:
                    dve.wait_ge(txt_in, txt_count)
                for k in range(2):
                    dve.bn_stats(ln_st[:, k, :], tok[:, k, :]).then_inc(ln_small, 1)
                dve.wait_ge(ln_small, g * 6 + 2)
                dve.sem_inc(passed, 1)
                for k in range(2):
                    dve.bn_aggr(ln_mv[:, k, :], ln_st[:, k, :]).then_inc(ln_small, 1)
                dve.wait_ge(ln_small, g * 6 + 4)
                dve.tensor_scalar(ln_s[:, 0, :], ln_mv[:, :, 1], 1.0 + RMS_EPS, EPS * RMS_EPS, ALU.mult, ALU.add)\
                    .then_inc(ln_small, 1)

            def ln_shift():
                dve.wait_ge(ln_rstd, g + 1)
                dve.scalar_tensor_tensor(ln_s[:, 2, :], ln_mv[:, :, 0], -1.0, ln_s[:, 1, :], ALU.mult, ALU.mult)\
                    .then_inc(ln_small, 1)

            def x_low_part():
                dve.wait_ge(x_hi_done, g + 1)
                if due(g * 64):
                    dve.wait_ge(scan_wr, g * 64)
                dve.scalar_tensor_tensor(x_lo[:, :, :], xf[:, :, :], X_SCALE, x_hi[:, :, :], ALU.mult, ALU.subtract)\
                    .then_inc(x_lo_done, 1)

            def silu():
                dve.wait_ge(gth_done, g + 1)
                if due(g * 16):
                    dve.wait_ge(gate_wr, g * 16)
                dve.scalar_tensor_tensor(gate_o[:, 1, :, :], gth[:, :, :], 1.0, gf[:, :, :], ALU.add, ALU.mult)\
                    .then_inc(gate_done, 1)

            def attn_bias():
                dve.wait_ge(attn_ps, q + 1)
                if due(q):
                    dve.wait_ge(res_done, q)
                dve.tensor_tensor(attn[:, :, :], P[0][0:PT, :].rearrange("p (k d) -> p k d", k=2),
                                  rows[:, 3, :].unsqueeze(1).to_broadcast([PT, 2, D]), ALU.add).then_inc(attn_done, 1)

            def res_stats():
                dve.wait_ge(res_done, q + 1)
                for k in range(4):
                    dve.bn_stats(res_st[:, k, :], res[:, k, :]).then_inc(res_small, 1)

            def res_variance():
                dve.wait_ge(res_small, q * 10 + 4)
                dve.sem_inc(passed, 1)
                for k in range(4):
                    dve.bn_aggr(res_mv[:, k, :], res_st[:, k, :]).then_inc(res_small, 1)
                dve.wait_ge(res_small, q * 10 + 8)
                dve.tensor_scalar(res_s[:, 0, :], res_mv[:, :, 1], EPS, None, ALU.add).then_inc(res_small, 1)

            def res_shift():
                dve.wait_ge(res_rstd, q + 1)
                dve.scalar_tensor_tensor(res_s[:, 2, :], res_mv[:, :, 0], -1.0, res_s[:, 1, :], ALU.mult, ALU.mult)\
                    .then_inc(res_small, 1)

            def ffn_silu(k):
                dve.wait_ge(fth_done, q * HB + k + 1)
                if due(q * HB + k):
                    dve.wait_ge(act_done, q * HB + k)
                dve.scalar_tensor_tensor(fsg[:, :], fth[:, :], 1.0, P[0][:, 0:4 * PT], ALU.add, ALU.mult)\
                    .then_inc(fsg_done, 1)

            def ffn_product(k):
                dve.wait_ge(ffn_u_ps, q * HB + k + 1)
                dve.wait_ge(fsg_done, q * HB + k + 1)
                dve.scalar_tensor_tensor(act[:, k, :], fsg[:, :], ACT_SCALE * 0.5 * DEQUANT * DEQUANT, P[1][:, 0:4 * PT],
                                         ALU.mult, ALU.mult).then_inc(act_done, 1)

            def fx_low_part(j):
                dve.wait_ge(fxT_done, q * 4 + 2 * j + 2)
                dve.tensor_tensor(fx_lo[:, j, :], fxT[:, j, :], fx_hi[:, j, :], ALU.subtract).then_inc(fx_lo_done, 1)

            def finish(pair):
                dve.wait_ge(down_ps, d * 2 + pair + 1)
                dve.scalar_tensor_tensor(res[:, pair * 2:pair * 2 + 2, :],
                                         P[pair][0:PT, :].rearrange("p (k d) -> p k d", k=2), DEQUANT / ACT_SCALE,
                                         res[:, pair * 2:pair * 2 + 2, :], ALU.mult, ALU.add).then_inc(out_done, 1)

            txt_count = ((g - IMG_GROUPS) * 64 + LAST * 2 * 16 if isinstance(g, int) and g == GROUPS - 1
                         else (g - IMG_GROUPS + 1) * 64)
            for slot in range(SLOTS):
                if scan and slot < steps * CHUNKS:
                    grow(slot)
                for k in parts_at(plan, "ffn_odd", slot):
                    ffn_odd(dve, k)
                for k in parts_at(plan, "flag_large", slot):
                    flag_large(dve)
                if down:
                    for k in parts_at(plan, "finish", slot):
                        finish(k)
                if ahead:
                    for k in parts_at(plan, "raw_patch", slot):
                        raw_patch(k)
                    for k in parts_at(plan, "raw_means", slot):
                        raw_means()
                    for k in parts_at(plan, "raw_deviation", slot):
                        raw_deviation()
                    for k in parts_at(plan, "raw_variance", slot):
                        raw_variance()
                    for k in parts_at(plan, "raw_shift", slot):
                        raw_shift()
                if post:
                    for k in parts_at(plan, "attn_bias", slot):
                        attn_bias()
                    for k in parts_at(plan, "res_stats", slot):
                        res_stats()
                    for k in parts_at(plan, "res_variance", slot):
                        res_variance()
                    for k in parts_at(plan, "res_shift", slot):
                        res_shift()
                    for k in parts_at(plan, "fx_low_part", slot):
                        fx_low_part(k)
                if pre and image:
                    for k in parts_at(plan, "tok_stats", slot):
                        tok_stats(k)
                    for k in parts_at(plan, "tok_shift", slot):
                        tok_shift(k)
                if pre:
                    for k in parts_at(plan, "ln_stats", slot):
                        ln_stats()
                    for k in parts_at(plan, "ln_shift", slot):
                        ln_shift()
                    for k in parts_at(plan, "x_low_part", slot):
                        x_low_part()
                    for k in parts_at(plan, "silu", slot):
                        silu()
                if post:
                    for k in parts_at(plan, "ffn_silu", slot):
                        ffn_silu(k)
                    for k in parts_at(plan, "ffn_product", slot):
                        ffn_product(k)

        def scalar_body(sc, i, image, ahead, pre, scan, post, down, steps):
            r, g, s, q, d = i + 1, i, i - 1, i - 2, i - 3
            plan = PLANS[kind_of(i, image, pre)]

            def squash(slot):
                t, c = divmod(slot, CHUNKS)
                sc.wait_ge(driven, s * SLOTS + slot + 1)
                sc.activation(h[:, c, :], U[bank_of(slot)][:, :], ACT.Tanh, scale=1.0 / U_SCALE).then_inc(squashed, 1)

            def y_copy():
                sc.wait_ge(y_ps, q + 1)
                if due(q * 64):
                    sc.wait_ge(y_wr, q * 64)
                sc.activation(y_sb, Y[:, :], ACT.Copy).then_inc(y_out, 1)

            def normalise(t):
                w = 2 * t
                sc.wait_ge(raw_small, (r + 1) * 6)
                sc.activation(rawn[:, w, :].rearrange("p (y x) -> p y x", x=PATCH), raw[:, :, w, :], ACT.Identity, scale=raw_s[:, 5, w:w + 1],
                              bias=raw_s[:, 6, w:w + 1]).then_inc(norm_even, 1)

            def xT_copy(n):
                hf, par, t0, nt = turn_part(n)
                sc.wait_ge(turned_ps, g * 8 + n + 1)
                sc.activation(
                    xT[:, hf * CH:hf * CH + CH, par, :].rearrange("p c (b t) -> p t c b", t=STEPS)[:, t0:t0 + nt],
                    P[turn_bank(n)][:, 0:nt * RAWP].rearrange("p (t c b) -> p t c b", c=CH, b=B),
                    ACT.Copy).then_inc(xT_done, 1)

            def tok_normalise(pair):
                sc.wait_ge(tok_small, g * 16 + pair * 8 + 8)
                for k in range(pair * 2, pair * 2 + 2):
                    sc.activation(tok[:, k, :], tok[:, k, :], ACT.Identity, scale=tok_s[:, 1, k:k + 1],
                                  bias=tok_s[:, 2, k:k + 1]).then_inc(tok_norm, 1)

            def ln_apply():
                sc.wait_ge(ln_small, (g + 1) * 6)
                for k in range(2):
                    sc.activation(xa[:, k, :], tok[:, k, :], ACT.Identity, scale=ln_s[:, 1, k:k + 1],
                                  bias=ln_s[:, 2, k:k + 1]).then_inc(xa_done, 1)

            def xaT_copy():
                sc.wait_ge(xa_ps, g + 1)
                sc.activation(xaT[:, :, :], P[2][:, 0:2 * TOK].rearrange("p (j t) -> p j t", j=DB),
                              ACT.Copy).then_inc(xaT_done, 1)

            def bank_in_step_order(k):
                return P[2][:, k * TOK:k * TOK + TOK].rearrange("p (b t) -> p t b", t=STEPS)

            def x_copy():
                sc.wait_ge(proj_ps, g * 2 + 1)
                if due(g):
                    sc.wait_ge(x_lo_done, g)
                if due(g * 3):
                    sc.wait_ge(gate_done, g * 3)
                for k in range(DB):
                    sc.activation(xf[:, k, :].rearrange("p (t b) -> p t b", b=B), bank_in_step_order(k),
                                  ACT.Identity, bias=cols[:, k:k + 1]).then_inc(xf_done, 1)
                sc.wait_ge(xf_done, (g + 1) * 2)
                if due(g * 64):
                    sc.wait_ge(scan_wr, g * 64)
                sc.activation(x_hi[:, :, :], xf[:, :, :], ACT.Copy, scale=X_SCALE).then_inc(x_hi_done, 1)

            def gate_copy():
                sc.wait_ge(proj_ps, g * 2 + 2)
                for k in range(DB):
                    sc.activation(gf[:, k, :].rearrange("p (t b) -> p t b", b=B), bank_in_step_order(k),
                                  ACT.Identity, bias=cols[:, 2 + k:3 + k]).then_inc(gf_done, 1)
                sc.wait_ge(gf_done, (g + 1) * 2)
                sc.activation(gth[:, :, :], gf[:, :, :], ACT.Tanh, scale=0.5).then_inc(gth_done, 1)

            def fx_apply(k):
                sc.wait_ge(res_small, (q + 1) * 10)
                sc.activation(fx[:, k, :], res[:, k, :], ACT.Identity, scale=res_s[:, 1, k:k + 1],
                              bias=res_s[:, 2, k:k + 1]).then_inc(fx_done, 1)

            def fxT_copy(j):
                sc.wait_ge(fx_ps, q * 2 + j + 1)
                sc.activation(fxT[:, j, :], P[2 * j][:, 0:4 * PT], ACT.Copy).then_inc(fxT_done, 1)
                sc.activation(fx_hi[:, j, :], P[2 * j][:, 0:4 * PT], ACT.Copy).then_inc(fxT_done, 1)

            def ffn_tanh(k):
                sc.wait_ge(ffn_g_ps, q * HB + k + 1)
                if due(q * HB + k):
                    sc.wait_ge(fsg_done, q * HB + k)
                sc.activation(fth[:, :], P[0][:, 0:4 * PT], ACT.Tanh, scale=0.5 * DEQUANT).then_inc(fth_done, 1)

            def act_high_part(k):
                sc.wait_ge(act_done, q * HB + k + 1)
                sc.activation(act_hi[:, k, :], act[:, k, :], ACT.Copy).then_inc(act_hi_done, 1)

            for slot in range(SLOTS):
                if scan and slot < steps * CHUNKS:
                    squash(slot)
                for k in parts_at(plan, "ffn_even", slot):
                    ffn_even(sc, k)
                if post:
                    for k in parts_at(plan, "y_copy", slot):
                        y_copy()
                    for k in parts_at(plan, "fx_apply", slot):
                        fx_apply(k)
                    for k in parts_at(plan, "fxT_copy", slot):
                        fxT_copy(k)
                    for k in parts_at(plan, "ffn_tanh", slot):
                        ffn_tanh(k)
                    for k in parts_at(plan, "act_high_part", slot):
                        act_high_part(k)
                if pre and image:
                    for k in parts_at(plan, "xT_copy", slot):
                        xT_copy(k)
                    for k in parts_at(plan, "tok_normalise", slot):
                        tok_normalise(k)
                if ahead:
                    for k in parts_at(plan, "normalise", slot):
                        normalise(k)
                if pre:
                    for k in parts_at(plan, "ln_apply", slot):
                        ln_apply()
                    for k in parts_at(plan, "xaT_copy", slot):
                        xaT_copy()
                    for k in parts_at(plan, "x_copy", slot):
                        x_copy()
                    for k in parts_at(plan, "gate_copy", slot):
                        gate_copy()

        def gpsimd_body(gp, i, image, ahead, pre, scan, post, down, steps):
            r, g, s, q, d = i + 1, i, i - 1, i - 2, i - 3

            def rsqrt(dst, src, parts, n):
                return gp.tensor_tensor(dst, src, half_th[0:parts, :].to_broadcast([parts, n]), ALU.pow)

            def ln_rsqrt():
                gp.wait_ge(ln_small, g * 6 + 5)
                rsqrt(ln_s[:, 1, :], ln_s[:, 0, :], PT, 2).then_inc(ln_rstd, 1)

            def gating():
                gp.wait_ge(y_ld, (q + 1) * 32)
                gp.wait_ge(gate_ld, (q + 1) * 16)
                y = yT[:, :, :, :].rearrange("p t k b -> p k t b")
                gp.tensor_tensor(y, y, gate_i[:, 0, :, :].rearrange("p k (t b) -> p k t b", b=B), ALU.add).then_inc(z_sum, 1)
                gp.wait_ge(z_sum, q + 1)
                if due(q):
                    gp.wait_ge(attn_ps, q)
                gp.tensor_tensor(zT[:, :, :].rearrange("p k (b t) -> p k t b", t=STEPS),
                                 y, gate_i[:, 1, :, :].rearrange("p k (t b) -> p k t b", b=B), ALU.mult).then_inc(z_done, 1)

            def residual():
                gp.wait_ge(res_ld, (q + 1) * 16)
                gp.wait_ge(attn_done, q + 1)
                both = res[:, :, :].rearrange("p (a k) d -> p a (k d)", a=2)
                gp.tensor_tensor(both, both, attn[:, :, :].rearrange("p k d -> p (k d)").unsqueeze(1)
                                 .to_broadcast([PT, 2, 2 * D]), ALU.add).then_inc(res_done, 1)

            def res_rsqrt():
                gp.wait_ge(res_small, q * 10 + 9)
                rsqrt(res_s[:, 1, :], res_s[:, 0, :], PT, 4).then_inc(res_rstd, 1)

            def raw_rsqrt():
                gp.wait_ge(raw_small, r * 6 + 5)
                rsqrt(raw_s[:, 5, :], raw_s[:, 4, :], RAWP, ROW).then_inc(raw_rstd, 1)

            def normalise(t):
                w = 2 * t + 1
                if t == 0:
                    gp.wait_ge(raw_small, r * 6 + 6)
                    gp.sem_inc(passed, 1)
                gp.tensor_scalar(rawn[:, w, :].rearrange("p (y x) -> p y x", x=PATCH), raw[:, :, w, :],
                                 raw_s[:, 5, w:w + 1], raw_s[:, 6, w:w + 1], ALU.mult, ALU.add).then_inc(norm_odd, 1)

            def token_rsqrt(pair):
                gp.wait_ge(tok_small, g * 16 + pair * 8 + 7)
                rsqrt(tok_s[:, 1, pair * 2:pair * 2 + 2], tok_s[:, 0, pair * 2:pair * 2 + 2], PT, 2).then_inc(tok_rstd, 1)

            def token_tiles(pair):
                two = tok[:, pair * 2:pair * 2 + 2, :]
                gp.wait_ge(tok_norm, g * 4 + pair * 2 + 2)
                gp.tensor_tensor(two, two, rows[:, 1, :].unsqueeze(1).to_broadcast([PT, 2, D]), ALU.mult)\
                    .then_inc(tok_g, 1)
                gp.wait_ge(tok_g, g * 2 + pair + 1)
                gp.tensor_tensor(two, two, rows[:, 2, :].unsqueeze(1).to_broadcast([PT, 2, D]), ALU.add)\
                    .then_inc(tok_done, 1)

            def act_low_part(k):
                gp.wait_ge(act_hi_done, q * HB + k + 1)
                gp.tensor_tensor(act_lo[:, k, :], act[:, k, :], act_hi[:, k, :], ALU.subtract).then_inc(act_lo_done, 1)

            def skip_term():
                gp.wait_ge(xf_done, (g + 1) * 2)
                if due(g * 16):
                    gp.wait_ge(gate_wr, g * 16)
                gp.sem_inc(passed, 1)
                for k in range(DB):
                    gp.tensor_scalar(gate_o[:, 0, k, :], xf[:, k, :], cols[:, 4 + k:5 + k], None, ALU.mult)\
                        .then_inc(gate_done, 1)

            for name, k in POOL_ORDER[kind_of(i, image, pre)]:
                if post and name == "gating":
                    gating()
                if post and name == "residual":
                    residual()
                if post and name == "res_rsqrt":
                    res_rsqrt()
                if pre and image and name == "token_rsqrt":
                    token_rsqrt(k)
                if pre and image and name == "token_tiles":
                    token_tiles(k)
                if ahead and name == "raw_rsqrt":
                    raw_rsqrt()
                if pre and name == "ln_rsqrt":
                    ln_rsqrt()
                if pre and name == "skip_term":
                    skip_term()
                if post and name == "act_low_part":
                    act_low_part(k)
                if ahead and name == "normalise":
                    normalise(k)

        def turn_part(n):
            hf, par, late = n // 4, (n // 2) % 2, n % 2
            return hf, par, 4 * late, 3 if late else 4

        def turn_bank(n):
            return (2, 1, 0)[n % 3]

        def whole_part(w):
            return w.bitcast(BF16)[:, 1::2]

        def tensor_body(pe, i, image, ahead, pre, scan, post, down, steps, general):
            r, g, s, q, d = i + 1, i, i - 1, i - 2, i - 3
            plan = PLANS[kind_of(i, image, pre)]
            slots = steps * CHUNKS

            def drive(slot):
                t, c = divmod(slot, CHUNKS)
                if slot == 0:
                    pe.wait_ge(diag_early, (s + 1) * 256)
                if slot == EARLY * CHUNKS:
                    pe.wait_ge(diag_late, (s + 1) * 256)
                pe.wait_ge(grown, s * SLOTS + slot + 1)
                pe.matmul(U[bank_of(slot)][:, :], b_st[:, c, :], x_diag[:, c, :, t * B:t * B + B],
                          start=False, stop=True, skip_group_check=True).then_inc(driven, 1)

            def read(slot, s, steps):
                t, c = divmod(slot, CHUNKS)
                pe.wait_ge(squashed, s * SLOTS + slot + 1)
                if slot == 0 and due(s):
                    pe.wait_ge(y_out, s)
                q4 = (c % 4) * 32
                mm = pe.matmul(Y[q4:q4 + 32, :], read_st[:, t, c // 4, :], h[:, c, :],
                               start=(t == 0 and c < 4), stop=(t == steps - 1), skip_group_check=True)
                if slot == steps * CHUNKS - 1:
                    mm.then_inc(y_ps, 1)

            def average(which):
                if which == 0:
                    pe.wait_ge(raw_aggr, (r + 1) * ROW)
                    if post:
                        pe.wait_ge(attn_done, q + 1)
                    src = raw_mv[:, :, 0]
                else:
                    pe.wait_ge(raw_small, r * 6 + 4)
                    src = raw_s[:, 3, :]
                pe.matmul(P[0][0:RAWP, 0:ROW], cst[0:RAWP, C_AVG:C_AVG + RAWP], src, start=True, stop=True)\
                    .then_inc(avg_ps, 1)

            def turn(n):
                hf, par, t0, nt = turn_part(n)
                if par == 0:
                    pe.wait_ge(norm_even, g * STEPS + t0 + nt)
                else:
                    pe.wait_ge(norm_odd, g * STEPS + t0 + nt)
                if n == 0 and due(g * 2):
                    pe.wait_ge(gf_done, g * 2)
                if n == 1:
                    if down:
                        pe.wait_ge(out_done, d * 2 + 2)
                    elif due(g * 16 - 6):
                        pe.wait_ge(tok_small, g * 16 - 6)
                if n >= 3:
                    pe.wait_ge(xT_done, g * 8 + n - 2)
                for k in range(nt):
                    w = 2 * (t0 + k) + par
                    mm = pe.transpose(P[turn_bank(n)][:, k * RAWP:k * RAWP + RAWP], rawn[:, w, hf * 128:hf * 128 + 128],
                                      cst[0:RAWP, C_ID:C_ID + RAWP])
                mm.then_inc(turned_ps, 1)

            def embed(k, f0):
                if f0 == 0 and k == 0:
                    pe.wait_ge(xT_done, (g + 1) * 8)
                for f in range(f0, f0 + 2):
                    mm = pe.matmul(P[2 - k // 2][0:PT, (k % 2) * D:(k % 2) * D + D],
                                   xT[:, f, k // 2, (k % 2) * PT:(k % 2) * PT + PT], tok_w[:, f, :],
                                   start=(f == 0), stop=(f == KF - 1))
                if f0 == KF - 2 and k % 2:
                    mm.then_inc(tok_ps, 1)

            def turn_xa():
                pe.wait_ge(xa_done, (g + 1) * 2)
                if not image:
                    pe.wait_ge(gf_done, g * 2)
                elif post:
                    pe.wait_ge(fxT_done, (q + 1) * 4)
                else:
                    pe.wait_ge(tok_small, g * 16 + 2)
                for j in range(DB):
                    for k in range(2):
                        mm = pe.transpose(P[2][:, (j * 2 + k) * PT:(j * 2 + k + 1) * PT], xa[:, k, j * 128:j * 128 + 128],
                                          cst[0:PT, C_ID:C_ID + PT])
                mm.then_inc(xa_ps, 1)

            def project(part, k):
                if part == 0:
                    pe.wait_ge(xaT_done, g + 1)
                elif image:
                    pe.wait_ge(xf_done, (g + 1) * 2)
                else:
                    pe.wait_ge(fxT_done, (q + 1) * 4)
                e0 = (part * DB + k) * 128
                for j in range(DB):
                    mm = pe.matmul(P[2][:, k * TOK:k * TOK + TOK], in_w[:, j, e0:e0 + 128], xaT[:, j, :],
                                   start=(j == 0), stop=(j == DB - 1))
                if k == DB - 1:
                    mm.then_inc(proj_ps, 1)

            def attend(k):
                pe.wait_ge(z_done, q + 1)
                if pre and image:
                    pe.wait_ge(xT_done, g * 8 + 6)
                elif down:
                    pe.wait_ge(out_done, d * 2 + 1)
                for j in range(DB):
                    mm = pe.matmul(P[0][0:PT, k * D:k * D + D], zT[:, j, k * PT:k * PT + PT], out_w[:, j, :],
                                   start=(j == 0), stop=(j == DB - 1))
                if k == 1:
                    mm.then_inc(attn_ps, 1)

            def turn_fx(j):
                pe.wait_ge(fx_done, (q + 1) * 4)
                if j == 0:
                    pe.wait_ge(attn_done, q + 1)
                    if ahead:
                        pe.wait_ge(raw_small, r * 6 + 5)
                elif pre and image:
                    pe.wait_ge(tok_small, g * 16 + 2)
                elif pre:
                    pe.wait_ge(xf_done, (g + 1) * 2)
                elif i == GROUPS:
                    pe.wait_ge(gf_done, g * 2)
                for k in range(4):
                    mm = pe.transpose(P[2 * j][:, k * PT:k * PT + PT], fx[:, k, j * 128:j * 128 + 128],
                                      cst[0:PT, C_ID:C_ID + PT])
                mm.then_inc(fx_ps, 1)

            def ffn(k, which):
                if k == 0 and which == 0:
                    pe.wait_ge(fxT_done, (q + 1) * 4)
                    pe.wait_ge(fx_lo_done, (q + 1) * 2)
                if k == 0 and which == 1:
                    if pre and image:
                        pe.wait_ge(tok_small, g * 16 + 10)
                    elif down:
                        pe.wait_ge(out_done, d * 2 + 2)
                if k > 0 and which == 0:
                    pe.wait_ge(fsg_done, q * HB + k)
                if k > 0 and which == 1:
                    pe.wait_ge(act_done, q * HB + k)
                w = (gate_w, up_w)[which]
                bank = P[which][:, 0:4 * PT]
                for j in range(DB):
                    if general:
                        mm = pe.matmul(bank, w[:, j, k * 128:k * 128 + 128], fxT[:, j, :],
                                       start=(j == 0), stop=(j == DB - 1))
                    else:
                        half = whole_part(w[:, j, k * 128:k * 128 + 128])
                        pe.matmul(bank, half, fx_hi[:, j, :], start=(j == 0), stop=False)
                        mm = pe.matmul(bank, half, fx_lo[:, j, :], start=False, stop=(j == DB - 1))
                mm.then_inc((ffn_g_ps, ffn_u_ps)[which], 1)

            def shrink(k, f0):
                if k == 0 and f0 == 0:
                    pe.wait_ge(act_lo_done, (d + 1) * HB)
                bank = P[k // 2][0:PT, (k % 2) * D:(k % 2) * D + D]
                for f in range(f0, f0 + 3):
                    if general:
                        mm = pe.matmul(bank, act[:, f, k * PT:k * PT + PT], down_w[:, f, :],
                                       start=(f == 0), stop=(f == HB - 1))
                    else:
                        half = whole_part(down_w[:, f, :])
                        pe.matmul(bank, act_hi[:, f, k * PT:k * PT + PT], half, start=(f == 0), stop=False)
                        mm = pe.matmul(bank, act_lo[:, f, k * PT:k * PT + PT], half, start=False, stop=(f == HB - 1))
                if f0 and k % 2:
                    mm.then_inc(down_ps, 1)

            for slot in range(SLOTS):
                if scan and slot < slots:
                    drive(slot)
                    if slot >= LAG:
                        read(slot - LAG, s, steps)
                    elif slot < 2 and due(s):
                        for late in (span(SLOTS - LAG, SLOTS - 1), (SLOTS - 1,))[slot]:
                            read(late, s - 1, STEPS)
                for k in parts_at(plan, "ffn_turn", slot):
                    ffn_turn(pe, k)
                for k in parts_at(plan, "count_large", slot):
                    count_large(pe)
                if down:
                    for k in parts_at(plan, "shrink", slot):
                        shrink(k // 2, 3 * (k % 2))
                if pre and image:
                    for k in parts_at(plan, "turn", slot):
                        turn(k)
                    for k in parts_at(plan, "embed", slot):
                        embed(k // 3, 2 * (k % 3))
                if post:
                    for k in parts_at(plan, "attend", slot):
                        attend(k)
                if ahead:
                    for k in parts_at(plan, "average", slot):
                        average(k)
                if post:
                    for k in parts_at(plan, "turn_fx", slot):
                        turn_fx(k)
                    for k in parts_at(plan, "ffn_gate", slot):
                        ffn(k, 0)
                    for k in parts_at(plan, "ffn_up", slot):
                        ffn(k, 1)
                if pre:
                    for k in parts_at(plan, "turn_xa", slot):
                        turn_xa()
                    for k in parts_at(plan, "project", slot):
                        project(k // DB, k % DB)
                if scan and steps < STEPS and slot == slots - 1:
                    for late in range(slots - LAG, slots):
                        read(late, s, steps)

        IMAGE = dict(image=True, ahead=True, pre=True, scan=True, post=True, down=True, steps=STEPS)
        TEXT = dict(IMAGE, image=False, ahead=False)
        AHEAD = dict(IMAGE, pre=False, scan=False, post=False, down=False)
        HEAD = [dict(IMAGE, scan=False, post=False, down=False), dict(IMAGE, post=False, down=False),
                dict(IMAGE, down=False)]
        LAST_IMAGE = dict(IMAGE, ahead=False)
        TAIL = [dict(TEXT, pre=False, steps=LAST_STEPS), dict(TEXT, pre=False, scan=False),
                dict(TEXT, pre=False, scan=False, post=False)]

        def bodies(eng, body, **how):
            for i, parts in enumerate(HEAD[1:], 1):
                body(eng, i, **parts, **how)
            with eng.Fori(len(HEAD), IMG_GROUPS - 1) as i:
                body(eng, i, **IMAGE, **how)
            body(eng, IMG_GROUPS - 1, **LAST_IMAGE, **how)
            with eng.Fori(IMG_GROUPS, GROUPS - 1) as i:
                body(eng, i, **TEXT, **how)
            body(eng, GROUPS - 1, **TEXT, **how)
            for n, parts in enumerate(TAIL):
                body(eng, GROUPS + n, **parts, **how)

        def sync_bodies(sp):
            for i, parts in enumerate(HEAD):
                sync_body(sp, i, **parts)
            with sp.Fori(len(HEAD), IMG_GROUPS - 1) as i:
                sync_body(sp, i, **IMAGE)
            sync_body(sp, IMG_GROUPS - 1, **LAST_IMAGE)
            with sp.Fori(IMG_GROUPS, GROUPS - 1) as i:
                sync_body(sp, i, **TEXT)
            sync_body(sp, GROUPS - 1, **TEXT, last_pre=True)
            for n, parts in enumerate(TAIL):
                sync_body(sp, GROUPS + n, **parts, last_down=n == len(TAIL) - 1)
            sp.wait_ge(stored, (GROUPS - 1) * 64 + LAST * 2 * 16)

        with nc.Block() as block:
            @block.sync
            def _(sp):
                setup_sync(sp)

            @block.vector
            def _(dve):
                setup_vector(dve)

            @block.scalar
            def _(sc):
                setup_scalar(sc)

            @block.gpsimd
            def _(gp):
                setup_gpsimd(gp)

            @block.tensor
            def _(pe):
                setup_tensor(pe)

        with nc.Block() as block:
            @block.sync
            def _(sp):
                sync_bodies(sp)

            @block.vector
            def _(dve):
                ffn_setup_vector(dve)
                vector_body(dve, 0, **HEAD[0])
                dve.wait_ge(s_bits, NU)
                bodies(dve, vector_body)

            @block.scalar
            def _(sc):
                scalar_body(sc, 0, **HEAD[0])
                bodies(sc, scalar_body)

            @block.gpsimd
            def _(gp):
                gpsimd_body(gp, 0, **HEAD[0])
                bodies(gp, gpsimd_body)

            @block.tensor
            def _(pe):
                tensor_body(pe, 0, general=False, **HEAD[0])
                pe.wait_ge(s_flag, 1)
                flag = pe.value_load(large_flag[:, :], min_val=0, max_val=1)
                with pe.If(flag > 0):
                    bodies(pe, tensor_body, general=True)
                with pe.Else():
                    bodies(pe, tensor_body, general=False)


def raw_rows(x, g):
    v = x.rearrange("b c (g y) w -> g c b (y w)", y=PATCH)
    return v[g]


_INS = ['x', 'txt', 'L0_tok_W', 'L0_tok_bias', 'L0_tok_ln1_g', 'L0_tok_ln1_b', 'L0_tok_ln2_g', 'L0_tok_ln2_b',
        'L0_attn_w_in', 'L0_attn_b_in', 'L0_attn_A', 'L0_attn_Bm', 'L0_attn_Cm', 'L0_attn_Dv', 'L0_attn_w_out',
        'L0_attn_b_out', 'L0_attn_g_norm', 'L0_ffn_w_gate', 'L0_ffn_w_up', 'L0_ffn_w_down']


def kernel(**inputs):
    import concourse.bacc as _bacc
    from concourse.bass_utils import run_bass_kernel_spmd as _run

    nc = _bacc.Bacc("TRN2", target_bir_lowering=False, num_devices=1)
    arrays, args = {}, []
    for name in _INS:
        a = np.ascontiguousarray(inputs[name])
        arrays[f"in_{name}"] = a
        args.append(nc.dram_tensor(f"in_{name}", a.shape, mybir.dt.from_np(a.dtype), kind="ExternalInput").ap())
    table = constant_table()
    arrays["constants"] = table
    args.append(nc.dram_tensor("constants", table.shape, FP32, kind="ExternalInput").ap())
    args.append(nc.dram_tensor("out", (B, L, D), FP32, kind="ExternalOutput").ap())
    build(nc, *args)
    r = _run(nc, [arrays], core_ids=[0])
    return r.results[0]["out"]
```
